# Optimizing a Trainium2 kernel written in Bass

```python
import numpy as np
import jax
import jax.numpy as jnp

def _softmax(x, axis=-1):
    return jax.nn.softmax(x, axis=axis)

def _gelu(x):
    return jax.nn.gelu(x, approximate=True)

def _silu(x):
    return jax.nn.silu(x)

def _sigmoid(x):
    return jax.nn.sigmoid(x)

def _layernorm(x, axis=-1, eps=1e-05):
    m = jnp.mean(x, axis=axis, keepdims=True)
    v = jnp.var(x, axis=axis, keepdims=True)
    return (x - m) / jnp.sqrt(v + eps)

def _scatter_add(tgt, idx, src, axis=0):
    return tgt.at[idx].add(src)

def _segment_sum(src, seg, n):
    return jax.ops.segment_sum(src, seg, n)
kernel_name = 'mk_xattn_seq_d4_seqx_r8_398f2a'

def setup_inputs(seed: int=0):
    np.random.seed(seed)
    _w = jnp.asarray

    def _rec_inputs():
        import jax
        import jax.numpy as jnp
        _rk = jax.random.key(seed)
        x = -0.0002928 + 1 * jax.random.normal(jax.random.fold_in(_rk, 1), (16, 128, 256), jnp.float32)
        _lenS = 128 - jax.random.randint(jax.random.fold_in(_rk, 7), (16,), 0, max(1, 128 // 4) + 1, jnp.int32)
        _lenS2 = 128 - jax.random.randint(jax.random.fold_in(_rk, 8), (16,), 0, max(1, 128 // 4) + 1, jnp.int32)
        _ctx_2048P = jax.random.normal(jax.random.fold_in(_rk, 11), (16, 16, 256), jnp.float32)
        _ctx_2048c = jax.random.dirichlet(jax.random.fold_in(_rk, 511), 0.3 * jnp.ones((16,), jnp.float32), (16, 128))
        _ctx_2048t = jnp.einsum('bsk,bkd->bsd', _ctx_2048c, _ctx_2048P)
        _ctx_2048t = _ctx_2048t * jax.lax.rsqrt(jnp.mean(jnp.square(_ctx_2048t)) + 1e-12) * 0.953939
        ctx_2048 = -1.39393e-06 + 0.999914 * (_ctx_2048t + 0.3 * jax.random.normal(jax.random.fold_in(_rk, 611), (16, 128, 256), jnp.float32))
        _validS = jnp.arange(128)[None, :] < _lenS[:, None]
        _validS2 = jnp.arange(128)[None, :] < _lenS2[:, None]
        _causal = jnp.tril(jnp.ones((128, 128), dtype=bool))
        mask_1x1xSxS2_fc1 = jnp.where(jnp.broadcast_to(_validS2[0:1, None, None, :], (1, 1, 128, 128)), 1.0, 0.0).astype(jnp.float32)
        mask_Bx1xSxS2_ff1 = jnp.where(jnp.ones((16, 1, 128, 128), dtype=bool), 1.0, 0.0).astype(jnp.float32)
        return (x, ctx_2048, mask_1x1xSxS2_fc1, mask_Bx1xSxS2_ff1)
    x, ctx_2048, mask_1x1xSxS2_fc1, mask_Bx1xSxS2_ff1 = _rec_inputs()

    def _L0_xattn_setup():
        import jax, jax.numpy as jnp
        import numpy as np
        H = 256
        NH = 16
        HD = H // NH
        EPS = 1e-05

        def gelu(x):
            return 0.5 * x * (1.0 + jnp.tanh(0.7978845608028654 * x * (1.0 + 0.044715 * x * x)))

        def layernorm(x, scale, bias):
            m = jnp.mean(x, axis=-1, keepdims=True)
            v = jnp.mean(jnp.square(x - m), axis=-1, keepdims=True)
            return (x - m) * jax.lax.rsqrt(v + EPS) * scale + bias

        def split_heads(x):
            b, s, _ = x.shape
            return x.reshape(b, s, NH, HD).transpose(0, 2, 1, 3)

        def merge_heads(x):
            b, nh, s, hd = x.shape
            return x.transpose(0, 2, 1, 3).reshape(b, s, nh * hd)

        def attention(q, k, v, mask):
            scores = jnp.einsum('bhqd,bhkd->bhqk', q, k) / jnp.sqrt(jnp.float32(HD))
            scores = scores * mask - 10000.0 * (1.0 - mask)
            probs = jax.nn.softmax(scores, axis=-1)
            return jnp.einsum('bhqk,bhkd->bhqd', probs, v)
        key = jax.random.key(seed)
        ks = jax.random.split(key, 16)
        b, s, t = (2, 128, 128)
        w = lambda k, i, o: jax.random.normal(k, (i, o), jnp.float32) * 0.02
        inp = {'hidden_states': jax.random.normal(ks[0], (b, s, H), jnp.float32), 'encoder_states': jax.random.normal(ks[1], (b, t, H), jnp.float32), 'ltor_mask': jnp.tril(jnp.ones((1, 1, s, s), jnp.float32)), 'cross_mask': jnp.ones((b, 1, s, t), jnp.float32), 'ln1_s': jnp.ones((H,), jnp.float32), 'ln1_b': jnp.zeros((H,), jnp.float32), 'w_qkv': w(ks[2], H, 3 * H), 'b_qkv': jnp.zeros((3 * H,), jnp.float32), 'w_ao': w(ks[3], H, H), 'b_ao': jnp.zeros((H,), jnp.float32), 'ln2_s': jnp.ones((H,), jnp.float32), 'ln2_b': jnp.zeros((H,), jnp.float32), 'w_q': w(ks[4], H, H), 'b_q': jnp.zeros((H,), jnp.float32), 'w_kv': w(ks[5], H, 2 * H), 'b_kv': jnp.zeros((2 * H,), jnp.float32), 'w_co': w(ks[6], H, H), 'b_co': jnp.zeros((H,), jnp.float32), 'ln3_s': jnp.ones((H,), jnp.float32), 'ln3_b': jnp.zeros((H,), jnp.float32), 'w1': w(ks[7], H, 4 * H), 'b1': jnp.zeros((4 * H,), jnp.float32), 'w2': w(ks[8], 4 * H, H), 'b2': jnp.zeros((H,), jnp.float32)}
        return inp
    _L0_xattn_all = _L0_xattn_setup()
    _L0_xattn_in = {k: v for k, v in _L0_xattn_all.items() if k in ('ln1_s', 'ln1_b', 'w_qkv', 'b_qkv', 'w_ao', 'b_ao', 'ln2_s', 'ln2_b', 'w_q', 'b_q', 'w_kv', 'b_kv', 'w_co', 'b_co', 'ln3_s', 'ln3_b', 'w1', 'b1', 'w2', 'b2')}
    del _L0_xattn_all

    def _L1_xattn_setup():
        import jax, jax.numpy as jnp
        import numpy as np
        B, Q, S1, S2 = (4, 32, 256, 256)
        D, H, K, F = (256, 16, 128, 1024)
        LN_EPS = 1e-05

        def _layer_norm(x, scale, offset):
            mu = jnp.mean(x, axis=-1, keepdims=True)
            var = jnp.var(x, axis=-1, keepdims=True)
            return (x - mu) * jax.lax.rsqrt(var + LN_EPS) * scale + offset

        def _cross_attention(q_in, kv_in, wq, bq, wk, bk, wv, bv, wo, bo, bias_k, bias_v):
            b, q_len, _ = q_in.shape
            t = kv_in.shape[1]
            qh = (q_in @ wq + bq).reshape(b, q_len, H, K)
            kh = (kv_in @ wk + bk).reshape(b, t, H, K)
            vh = (kv_in @ wv + bv).reshape(b, t, H, K)
            kh = jnp.concatenate([kh, jnp.broadcast_to(bias_k, (b, 1, H, K))], axis=1)
            vh = jnp.concatenate([vh, jnp.broadcast_to(bias_v, (b, 1, H, K))], axis=1)
            scale = jnp.sqrt(jnp.asarray(K, q_in.dtype))
            logits = jnp.einsum('bqhk,bthk->bhqt', qh, kh) / scale
            weights = jax.nn.softmax(logits, axis=-1)
            ctx = jnp.einsum('bhqt,bthk->bqhk', weights, vh).reshape(b, q_len, H * K)
            return ctx @ wo + bo

        def _forward(x, xf_1, xf_2, ln1_scale, ln1_offset, wq1, bq1, wk1, bk1, wv1, bv1, wo1, bo1, bias_k1, bias_v1, ln2_scale, ln2_offset, wq2, bq2, wk2, bk2, wv2, bv2, wo2, bo2, bias_k2, bias_v2, ln_mlp_scale, ln_mlp_offset, w_fc1, b_fc1, w_fc2, b_fc2):
            res = x
            h = _layer_norm(x, ln1_scale, ln1_offset)
            x = res + _cross_attention(h, xf_1, wq1, bq1, wk1, bk1, wv1, bv1, wo1, bo1, bias_k1, bias_v1)
            res = x
            h = _layer_norm(x, ln2_scale, ln2_offset)
            x = res + _cross_attention(h, xf_2, wq2, bq2, wk2, bk2, wv2, bv2, wo2, bo2, bias_k2, bias_v2)
            h = _layer_norm(x, ln_mlp_scale, ln_mlp_offset)
            h = jax.nn.gelu(h @ w_fc1 + b_fc1, approximate=False) @ w_fc2 + b_fc2
            return x + h
        key = jax.random.key(seed)
        ks = iter(jax.random.split(key, 64))

        def rn(shape, s=0.02):
            return jax.random.normal(next(ks), shape, jnp.float32) * s
        inp = {'x': rn((B, Q, D), 1.0), 'xf_1': rn((B, S1, D), 1.0), 'xf_2': rn((B, S2, D), 1.0)}
        for i in (1, 2):
            inp[f'ln{i}_scale'] = jnp.ones((D,), jnp.float32)
            inp[f'ln{i}_offset'] = jnp.zeros((D,), jnp.float32)
            inp[f'wq{i}'] = rn((D, H * K))
            inp[f'bq{i}'] = jnp.zeros((H * K,), jnp.float32)
            inp[f'wk{i}'] = rn((D, H * K))
            inp[f'bk{i}'] = jnp.zeros((H * K,), jnp.float32)
            inp[f'wv{i}'] = rn((D, H * K))
            inp[f'bv{i}'] = jnp.zeros((H * K,), jnp.float32)
            inp[f'wo{i}'] = rn((H * K, D))
            inp[f'bo{i}'] = jnp.zeros((D,), jnp.float32)
            inp[f'bias_k{i}'] = rn((1, 1, H, K))
            inp[f'bias_v{i}'] = rn((1, 1, H, K))
        inp['ln_mlp_scale'] = jnp.ones((D,), jnp.float32)
        inp['ln_mlp_offset'] = jnp.zeros((D,), jnp.float32)
        inp['w_fc1'] = rn((D, F))
        inp['b_fc1'] = jnp.zeros((F,), jnp.float32)
        inp['w_fc2'] = rn((F, D))
        inp['b_fc2'] = jnp.zeros((D,), jnp.float32)
        return inp
    _L1_xattn_all = _L1_xattn_setup()
    _L1_xattn_in = {k: v for k, v in _L1_xattn_all.items() if k in ('ln1_scale', 'ln1_offset', 'wq1', 'bq1', 'wk1', 'bk1', 'wv1', 'bv1', 'wo1', 'bo1', 'bias_k1', 'bias_v1', 'ln2_scale', 'ln2_offset', 'wq2', 'bq2', 'wk2', 'bk2', 'wv2', 'bv2', 'wo2', 'bo2', 'bias_k2', 'bias_v2', 'ln_mlp_scale', 'ln_mlp_offset', 'w_fc1', 'b_fc1', 'w_fc2', 'b_fc2')}
    del _L1_xattn_all

    def _L2_xattn_setup():
        import jax, jax.numpy as jnp
        import numpy as np
        H = 256
        B, L, S = (4, 512, 10)
        key = jax.random.key(seed)
        k1, k2, k3, k4, k5, k6 = jax.random.split(key, 6)
        scale = 1.0 / np.sqrt(H)
        return {'h_english': jax.random.normal(k1, (B, L, H), dtype=jnp.float32), 'h_lojban': jax.random.normal(k2, (B, S, H), dtype=jnp.float32), 'w_q': jax.random.normal(k3, (H, H), dtype=jnp.float32) * scale, 'w_k': jax.random.normal(k4, (H, H), dtype=jnp.float32) * scale, 'w_v': jax.random.normal(k5, (H, H), dtype=jnp.float32) * scale, 'w_o': jax.random.normal(k6, (H, H), dtype=jnp.float32) * scale, 'alpha': jnp.float32(0.1)}
    _L2_xattn_all = _L2_xattn_setup()
    _L2_xattn_in = {k: v for k, v in _L2_xattn_all.items() if k in ('w_q', 'w_k', 'w_v', 'w_o', 'alpha')}
    del _L2_xattn_all

    def _L3_xattn_setup():
        import jax, jax.numpy as jnp
        import numpy as np
        E, H, L, B = (256, 32, 128, 4)
        S = E // H
        DM, DD = (32, 64)

        def _ln(x, w, b, eps=1e-05):
            m = x.mean(-1, keepdims=True)
            v = ((x - m) ** 2).mean(-1, keepdims=True)
            return (x - m) / jnp.sqrt(v + eps) * w + b

        def _block(x, state, ln1_w, ln1_b, ln2_w, ln2_b, maa_x, maa_w1, maa_w2, maa_stack, time_decay, td_w1, td_w2, u, Wr, Wk, Wv, Wg, Wo, gn_w, gn_b, ffn_maa_k, ffn_maa_r, Wfk, Wfr, Wfv):
            b, l, e = x.shape
            h = u.shape[0]
            s_ = e // h
            xa = _ln(x, ln1_w, ln1_b)
            sx = jnp.concatenate([state[:, 1:2] - xa[:, :1], xa[:, :-1] - xa[:, 1:]], axis=1)
            xxx = jnp.tanh((xa + sx * maa_x) @ maa_w1).reshape(b, l, 5, DM)
            xxx = jnp.einsum('blfd,fde->blfe', xxx, maa_w2)
            xm = xa[:, :, None] + sx[:, :, None] * (maa_stack + xxx)
            xk, xw, xv, xr, xg = (xm[:, :, j] for j in range(5))
            w = jnp.exp(-jnp.exp(time_decay + jnp.tanh(xw @ td_w1) @ td_w2)).reshape(b, l, h, s_)
            r = (xr @ Wr.T).reshape(b, l, h, s_)
            k = (xk @ Wk.T).reshape(b, l, h, s_)
            v = (xv @ Wv.T).reshape(b, l, h, s_)
            g = jax.nn.silu(xg @ Wg.T)
            s0 = state[:, 2:2 + s_].reshape(b, h, s_, s_)

            def step(s, rkvw):
                r_t, k_t, v_t, w_t = rkvw
                a = k_t[..., :, None] * v_t[..., None, :]
                out = jnp.einsum('bhi,bhij->bhj', r_t, u * a + s)
                s = a + w_t[..., :, None] * s
                return (s, out)
            rkvw = tuple((jnp.moveaxis(t, 1, 0) for t in (r, k, v, w)))
            _, out = jax.lax.scan(step, s0, rkvw)
            out = jnp.moveaxis(out, 0, 1).reshape(b, l, e)
            og = out.reshape(b, l, h, s_)
            m = og.mean(-1, keepdims=True)
            va = ((og - m) ** 2).mean(-1, keepdims=True)
            og = ((og - m) / jnp.sqrt(va + 1e-05)).reshape(b, l, e) * gn_w + gn_b
            x1 = x + og * g @ Wo.T
            xc = _ln(x1, ln2_w, ln2_b)
            sx2 = jnp.concatenate([state[:, 0:1] - xc[:, :1], xc[:, :-1] - xc[:, 1:]], axis=1)
            xk2 = xc + sx2 * ffn_maa_k
            xr2 = xc + sx2 * ffn_maa_r
            rr = jax.nn.sigmoid(xr2 @ Wfr.T)
            kk = jnp.square(jax.nn.relu(xk2 @ Wfk.T))
            return x1 + rr * (kk @ Wfv.T)
        key = jax.random.key(seed)
        ks = jax.random.split(key, 24)
        sc = 0.02
        d = {'x': jax.random.normal(ks[0], (B, L, E), jnp.float32), 'state': jax.random.normal(ks[1], (B, 2 + S, E), jnp.float32) * 0.1, 'ln1_w': jnp.ones((E,), jnp.float32), 'ln1_b': jnp.zeros((E,), jnp.float32), 'ln2_w': jnp.ones((E,), jnp.float32), 'ln2_b': jnp.zeros((E,), jnp.float32), 'maa_x': jax.random.normal(ks[2], (E,), jnp.float32) * 0.1, 'maa_w1': jax.random.normal(ks[3], (E, 5 * DM), jnp.float32) * sc, 'maa_w2': jax.random.normal(ks[4], (5, DM, E), jnp.float32) * sc, 'maa_stack': jax.random.normal(ks[5], (1, 5, E), jnp.float32) * 0.1, 'time_decay': jax.random.normal(ks[6], (E,), jnp.float32) * 0.5, 'td_w1': jax.random.normal(ks[7], (E, DD), jnp.float32) * sc, 'td_w2': jax.random.normal(ks[8], (DD, E), jnp.float32) * sc, 'u': jax.random.normal(ks[9], (H, S, 1), jnp.float32) * 0.1, 'Wr': jax.random.normal(ks[10], (E, E), jnp.float32) * sc, 'Wk': jax.random.normal(ks[11], (E, E), jnp.float32) * sc, 'Wv': jax.random.normal(ks[12], (E, E), jnp.float32) * sc, 'Wg': jax.random.normal(ks[13], (E, E), jnp.float32) * sc, 'Wo': jax.random.normal(ks[14], (E, E), jnp.float32) * sc, 'gn_w': jnp.ones((E,), jnp.float32), 'gn_b': jnp.zeros((E,), jnp.float32), 'ffn_maa_k': jax.random.normal(ks[15], (E,), jnp.float32) * 0.1, 'ffn_maa_r': jax.random.normal(ks[16], (E,), jnp.float32) * 0.1, 'Wfk': jax.random.normal(ks[17], (E, E), jnp.float32) * sc, 'Wfr': jax.random.normal(ks[18], (E, E), jnp.float32) * sc, 'Wfv': jax.random.normal(ks[19], (E, E), jnp.float32) * sc}
        return d
    _L3_xattn_all = _L3_xattn_setup()
    _L3_xattn_in = {k: v for k, v in _L3_xattn_all.items() if k in ('ln1_w', 'ln1_b', 'ln2_w', 'ln2_b', 'maa_x', 'maa_w1', 'maa_w2', 'maa_stack', 'time_decay', 'td_w1', 'td_w2', 'u', 'Wr', 'Wk', 'Wv', 'Wg', 'Wo', 'gn_w', 'gn_b', 'ffn_maa_k', 'ffn_maa_r', 'Wfk', 'Wfr', 'Wfv')}
    del _L3_xattn_all
    return {'x': x, 'ctx_2048': ctx_2048, 'mask_1x1xSxS2_fc1': mask_1x1xSxS2_fc1, 'mask_Bx1xSxS2_ff1': mask_Bx1xSxS2_ff1, 'L0_xattn_ln1_s': _L0_xattn_in['ln1_s'], 'L0_xattn_ln1_b': _L0_xattn_in['ln1_b'], 'L0_xattn_w_qkv': _L0_xattn_in['w_qkv'], 'L0_xattn_b_qkv': _L0_xattn_in['b_qkv'], 'L0_xattn_w_ao': _L0_xattn_in['w_ao'], 'L0_xattn_b_ao': _L0_xattn_in['b_ao'], 'L0_xattn_ln2_s': _L0_xattn_in['ln2_s'], 'L0_xattn_ln2_b': _L0_xattn_in['ln2_b'], 'L0_xattn_w_q': _L0_xattn_in['w_q'], 'L0_xattn_b_q': _L0_xattn_in['b_q'], 'L0_xattn_w_kv': _L0_xattn_in['w_kv'], 'L0_xattn_b_kv': _L0_xattn_in['b_kv'], 'L0_xattn_w_co': _L0_xattn_in['w_co'], 'L0_xattn_b_co': _L0_xattn_in['b_co'], 'L0_xattn_ln3_s': _L0_xattn_in['ln3_s'], 'L0_xattn_ln3_b': _L0_xattn_in['ln3_b'], 'L0_xattn_w1': _L0_xattn_in['w1'], 'L0_xattn_b1': _L0_xattn_in['b1'], 'L0_xattn_w2': _L0_xattn_in['w2'], 'L0_xattn_b2': _L0_xattn_in['b2'], 'L1_xattn_ln1_scale': _L1_xattn_in['ln1_scale'], 'L1_xattn_ln1_offset': _L1_xattn_in['ln1_offset'], 'L1_xattn_wq1': _L1_xattn_in['wq1'], 'L1_xattn_bq1': _L1_xattn_in['bq1'], 'L1_xattn_wk1': _L1_xattn_in['wk1'], 'L1_xattn_bk1': _L1_xattn_in['bk1'], 'L1_xattn_wv1': _L1_xattn_in['wv1'], 'L1_xattn_bv1': _L1_xattn_in['bv1'], 'L1_xattn_wo1': _L1_xattn_in['wo1'], 'L1_xattn_bo1': _L1_xattn_in['bo1'], 'L1_xattn_bias_k1': _L1_xattn_in['bias_k1'], 'L1_xattn_bias_v1': _L1_xattn_in['bias_v1'], 'L1_xattn_ln2_scale': _L1_xattn_in['ln2_scale'], 'L1_xattn_ln2_offset': _L1_xattn_in['ln2_offset'], 'L1_xattn_wq2': _L1_xattn_in['wq2'], 'L1_xattn_bq2': _L1_xattn_in['bq2'], 'L1_xattn_wk2': _L1_xattn_in['wk2'], 'L1_xattn_bk2': _L1_xattn_in['bk2'], 'L1_xattn_wv2': _L1_xattn_in['wv2'], 'L1_xattn_bv2': _L1_xattn_in['bv2'], 'L1_xattn_wo2': _L1_xattn_in['wo2'], 'L1_xattn_bo2': _L1_xattn_in['bo2'], 'L1_xattn_bias_k2': _L1_xattn_in['bias_k2'], 'L1_xattn_bias_v2': _L1_xattn_in['bias_v2'], 'L1_xattn_ln_mlp_scale': _L1_xattn_in['ln_mlp_scale'], 'L1_xattn_ln_mlp_offset': _L1_xattn_in['ln_mlp_offset'], 'L1_xattn_w_fc1': _L1_xattn_in['w_fc1'], 'L1_xattn_b_fc1': _L1_xattn_in['b_fc1'], 'L1_xattn_w_fc2': _L1_xattn_in['w_fc2'], 'L1_xattn_b_fc2': _L1_xattn_in['b_fc2'], 'L2_xattn_w_q': _L2_xattn_in['w_q'], 'L2_xattn_w_k': _L2_xattn_in['w_k'], 'L2_xattn_w_v': _L2_xattn_in['w_v'], 'L2_xattn_w_o': _L2_xattn_in['w_o'], 'L2_xattn_alpha': _L2_xattn_in['alpha'], 'L3_xattn_ln1_w': _L3_xattn_in['ln1_w'], 'L3_xattn_ln1_b': _L3_xattn_in['ln1_b'], 'L3_xattn_ln2_w': _L3_xattn_in['ln2_w'], 'L3_xattn_ln2_b': _L3_xattn_in['ln2_b'], 'L3_xattn_maa_x': _L3_xattn_in['maa_x'], 'L3_xattn_maa_w1': _L3_xattn_in['maa_w1'], 'L3_xattn_maa_w2': _L3_xattn_in['maa_w2'], 'L3_xattn_maa_stack': _L3_xattn_in['maa_stack'], 'L3_xattn_time_decay': _L3_xattn_in['time_decay'], 'L3_xattn_td_w1': _L3_xattn_in['td_w1'], 'L3_xattn_td_w2': _L3_xattn_in['td_w2'], 'L3_xattn_u': _L3_xattn_in['u'], 'L3_xattn_Wr': _L3_xattn_in['Wr'], 'L3_xattn_Wk': _L3_xattn_in['Wk'], 'L3_xattn_Wv': _L3_xattn_in['Wv'], 'L3_xattn_Wg': _L3_xattn_in['Wg'], 'L3_xattn_Wo': _L3_xattn_in['Wo'], 'L3_xattn_gn_w': _L3_xattn_in['gn_w'], 'L3_xattn_gn_b': _L3_xattn_in['gn_b'], 'L3_xattn_ffn_maa_k': _L3_xattn_in['ffn_maa_k'], 'L3_xattn_ffn_maa_r': _L3_xattn_in['ffn_maa_r'], 'L3_xattn_Wfk': _L3_xattn_in['Wfk'], 'L3_xattn_Wfr': _L3_xattn_in['Wfr'], 'L3_xattn_Wfv': _L3_xattn_in['Wfv']}

def reference(x, ctx_2048, mask_1x1xSxS2_fc1, mask_Bx1xSxS2_ff1, L0_xattn_ln1_s, L0_xattn_ln1_b, L0_xattn_w_qkv, L0_xattn_b_qkv, L0_xattn_w_ao, L0_xattn_b_ao, L0_xattn_ln2_s, L0_xattn_ln2_b, L0_xattn_w_q, L0_xattn_b_q, L0_xattn_w_kv, L0_xattn_b_kv, L0_xattn_w_co, L0_xattn_b_co, L0_xattn_ln3_s, L0_xattn_ln3_b, L0_xattn_w1, L0_xattn_b1, L0_xattn_w2, L0_xattn_b2, L1_xattn_ln1_scale, L1_xattn_ln1_offset, L1_xattn_wq1, L1_xattn_bq1, L1_xattn_wk1, L1_xattn_bk1, L1_xattn_wv1, L1_xattn_bv1, L1_xattn_wo1, L1_xattn_bo1, L1_xattn_bias_k1, L1_xattn_bias_v1, L1_xattn_ln2_scale, L1_xattn_ln2_offset, L1_xattn_wq2, L1_xattn_bq2, L1_xattn_wk2, L1_xattn_bk2, L1_xattn_wv2, L1_xattn_bv2, L1_xattn_wo2, L1_xattn_bo2, L1_xattn_bias_k2, L1_xattn_bias_v2, L1_xattn_ln_mlp_scale, L1_xattn_ln_mlp_offset, L1_xattn_w_fc1, L1_xattn_b_fc1, L1_xattn_w_fc2, L1_xattn_b_fc2, L2_xattn_w_q, L2_xattn_w_k, L2_xattn_w_v, L2_xattn_w_o, L2_xattn_alpha, L3_xattn_ln1_w, L3_xattn_ln1_b, L3_xattn_ln2_w, L3_xattn_ln2_b, L3_xattn_maa_x, L3_xattn_maa_w1, L3_xattn_maa_w2, L3_xattn_maa_stack, L3_xattn_time_decay, L3_xattn_td_w1, L3_xattn_td_w2, L3_xattn_u, L3_xattn_Wr, L3_xattn_Wk, L3_xattn_Wv, L3_xattn_Wg, L3_xattn_Wo, L3_xattn_gn_w, L3_xattn_gn_b, L3_xattn_ffn_maa_k, L3_xattn_ffn_maa_r, L3_xattn_Wfk, L3_xattn_Wfr, L3_xattn_Wfv):
    import jax
    import jax.numpy as jnp

    def _L0_xattn_ref(hidden_states, encoder_states, ltor_mask, cross_mask, ln1_s, ln1_b, w_qkv, b_qkv, w_ao, b_ao, ln2_s, ln2_b, w_q, b_q, w_kv, b_kv, w_co, b_co, ln3_s, ln3_b, w1, b1, w2, b2):
        import jax, jax.numpy as jnp
        import numpy as np
        H = 256
        NH = 16
        HD = H // NH
        EPS = 1e-05

        def gelu(x):
            return 0.5 * x * (1.0 + jnp.tanh(0.7978845608028654 * x * (1.0 + 0.044715 * x * x)))

        def layernorm(x, scale, bias):
            m = jnp.mean(x, axis=-1, keepdims=True)
            v = jnp.mean(jnp.square(x - m), axis=-1, keepdims=True)
            return (x - m) * jax.lax.rsqrt(v + EPS) * scale + bias

        def split_heads(x):
            b, s, _ = x.shape
            return x.reshape(b, s, NH, HD).transpose(0, 2, 1, 3)

        def merge_heads(x):
            b, nh, s, hd = x.shape
            return x.transpose(0, 2, 1, 3).reshape(b, s, nh * hd)

        def attention(q, k, v, mask):
            scores = jnp.einsum('bhqd,bhkd->bhqk', q, k) / jnp.sqrt(jnp.float32(HD))
            scores = scores * mask - 10000.0 * (1.0 - mask)
            probs = jax.nn.softmax(scores, axis=-1)
            return jnp.einsum('bhqk,bhkd->bhqd', probs, v)
        ln_out = layernorm(hidden_states, ln1_s, ln1_b)
        qkv = ln_out @ w_qkv + b_qkv
        q, k, v = jnp.split(qkv, 3, axis=-1)
        ctx = merge_heads(attention(split_heads(q), split_heads(k), split_heads(v), ltor_mask))
        attn_out = ctx @ w_ao + b_ao
        x = hidden_states + attn_out
        ln_out = layernorm(x, ln2_s, ln2_b)
        q = ln_out @ w_q + b_q
        kv = encoder_states @ w_kv + b_kv
        k, v = jnp.split(kv, 2, axis=-1)
        ctx = merge_heads(attention(split_heads(q), split_heads(k), split_heads(v), cross_mask))
        cross_out = ctx @ w_co + b_co
        x = x + cross_out
        ln_out = layernorm(x, ln3_s, ln3_b)
        mlp_out = gelu(ln_out @ w1 + b1) @ w2 + b2
        return x + mlp_out

    def _L1_xattn_ref(x, xf_1, xf_2, ln1_scale, ln1_offset, wq1, bq1, wk1, bk1, wv1, bv1, wo1, bo1, bias_k1, bias_v1, ln2_scale, ln2_offset, wq2, bq2, wk2, bk2, wv2, bv2, wo2, bo2, bias_k2, bias_v2, ln_mlp_scale, ln_mlp_offset, w_fc1, b_fc1, w_fc2, b_fc2):
        import jax, jax.numpy as jnp
        import numpy as np
        B, Q, S1, S2 = (4, 32, 256, 256)
        D, H, K, F = (256, 16, 128, 1024)
        LN_EPS = 1e-05

        def _layer_norm(x, scale, offset):
            mu = jnp.mean(x, axis=-1, keepdims=True)
            var = jnp.var(x, axis=-1, keepdims=True)
            return (x - mu) * jax.lax.rsqrt(var + LN_EPS) * scale + offset

        def _cross_attention(q_in, kv_in, wq, bq, wk, bk, wv, bv, wo, bo, bias_k, bias_v):
            b, q_len, _ = q_in.shape
            t = kv_in.shape[1]
            qh = (q_in @ wq + bq).reshape(b, q_len, H, K)
            kh = (kv_in @ wk + bk).reshape(b, t, H, K)
            vh = (kv_in @ wv + bv).reshape(b, t, H, K)
            kh = jnp.concatenate([kh, jnp.broadcast_to(bias_k, (b, 1, H, K))], axis=1)
            vh = jnp.concatenate([vh, jnp.broadcast_to(bias_v, (b, 1, H, K))], axis=1)
            scale = jnp.sqrt(jnp.asarray(K, q_in.dtype))
            logits = jnp.einsum('bqhk,bthk->bhqt', qh, kh) / scale
            weights = jax.nn.softmax(logits, axis=-1)
            ctx = jnp.einsum('bhqt,bthk->bqhk', weights, vh).reshape(b, q_len, H * K)
            return ctx @ wo + bo

        def _forward(x, xf_1, xf_2, ln1_scale, ln1_offset, wq1, bq1, wk1, bk1, wv1, bv1, wo1, bo1, bias_k1, bias_v1, ln2_scale, ln2_offset, wq2, bq2, wk2, bk2, wv2, bv2, wo2, bo2, bias_k2, bias_v2, ln_mlp_scale, ln_mlp_offset, w_fc1, b_fc1, w_fc2, b_fc2):
            res = x
            h = _layer_norm(x, ln1_scale, ln1_offset)
            x = res + _cross_attention(h, xf_1, wq1, bq1, wk1, bk1, wv1, bv1, wo1, bo1, bias_k1, bias_v1)
            res = x
            h = _layer_norm(x, ln2_scale, ln2_offset)
            x = res + _cross_attention(h, xf_2, wq2, bq2, wk2, bk2, wv2, bv2, wo2, bo2, bias_k2, bias_v2)
            h = _layer_norm(x, ln_mlp_scale, ln_mlp_offset)
            h = jax.nn.gelu(h @ w_fc1 + b_fc1, approximate=False) @ w_fc2 + b_fc2
            return x + h
        return _forward(x, xf_1, xf_2, ln1_scale, ln1_offset, wq1, bq1, wk1, bk1, wv1, bv1, wo1, bo1, bias_k1, bias_v1, ln2_scale, ln2_offset, wq2, bq2, wk2, bk2, wv2, bv2, wo2, bo2, bias_k2, bias_v2, ln_mlp_scale, ln_mlp_offset, w_fc1, b_fc1, w_fc2, b_fc2)

    def _L2_xattn_ref(h_english, h_lojban, w_q, w_k, w_v, w_o, alpha):
        import jax, jax.numpy as jnp
        import numpy as np
        H = 256
        B, L, S = (4, 512, 10)
        h = h_english.shape[-1]
        q = jnp.einsum('blh,oh->blo', h_english, w_q)
        k = jnp.einsum('bsh,oh->bso', h_lojban, w_k)
        v = jnp.einsum('bsh,oh->bso', h_lojban, w_v)
        scores = jnp.einsum('blh,bsh->bls', q, k) / jnp.sqrt(jnp.float32(h))
        probs = jax.nn.softmax(scores, axis=-1)
        context = jnp.einsum('bls,bsh->blh', probs, v)
        delta = jnp.einsum('blh,oh->blo', context, w_o)
        return h_english + alpha * delta

    def _L3_xattn_ref(x, state, ln1_w, ln1_b, ln2_w, ln2_b, maa_x, maa_w1, maa_w2, maa_stack, time_decay, td_w1, td_w2, u, Wr, Wk, Wv, Wg, Wo, gn_w, gn_b, ffn_maa_k, ffn_maa_r, Wfk, Wfr, Wfv):
        import jax, jax.numpy as jnp
        import numpy as np
        E, H, L, B = (256, 32, 128, 4)
        S = E // H
        DM, DD = (32, 64)

        def _ln(x, w, b, eps=1e-05):
            m = x.mean(-1, keepdims=True)
            v = ((x - m) ** 2).mean(-1, keepdims=True)
            return (x - m) / jnp.sqrt(v + eps) * w + b

        def _block(x, state, ln1_w, ln1_b, ln2_w, ln2_b, maa_x, maa_w1, maa_w2, maa_stack, time_decay, td_w1, td_w2, u, Wr, Wk, Wv, Wg, Wo, gn_w, gn_b, ffn_maa_k, ffn_maa_r, Wfk, Wfr, Wfv):
            b, l, e = x.shape
            h = u.shape[0]
            s_ = e // h
            xa = _ln(x, ln1_w, ln1_b)
            sx = jnp.concatenate([state[:, 1:2] - xa[:, :1], xa[:, :-1] - xa[:, 1:]], axis=1)
            xxx = jnp.tanh((xa + sx * maa_x) @ maa_w1).reshape(b, l, 5, DM)
            xxx = jnp.einsum('blfd,fde->blfe', xxx, maa_w2)
            xm = xa[:, :, None] + sx[:, :, None] * (maa_stack + xxx)
            xk, xw, xv, xr, xg = (xm[:, :, j] for j in range(5))
            w = jnp.exp(-jnp.exp(time_decay + jnp.tanh(xw @ td_w1) @ td_w2)).reshape(b, l, h, s_)
            r = (xr @ Wr.T).reshape(b, l, h, s_)
            k = (xk @ Wk.T).reshape(b, l, h, s_)
            v = (xv @ Wv.T).reshape(b, l, h, s_)
            g = jax.nn.silu(xg @ Wg.T)
            s0 = state[:, 2:2 + s_].reshape(b, h, s_, s_)

            def step(s, rkvw):
                r_t, k_t, v_t, w_t = rkvw
                a = k_t[..., :, None] * v_t[..., None, :]
                out = jnp.einsum('bhi,bhij->bhj', r_t, u * a + s)
                s = a + w_t[..., :, None] * s
                return (s, out)
            rkvw = tuple((jnp.moveaxis(t, 1, 0) for t in (r, k, v, w)))
            _, out = jax.lax.scan(step, s0, rkvw)
            out = jnp.moveaxis(out, 0, 1).reshape(b, l, e)
            og = out.reshape(b, l, h, s_)
            m = og.mean(-1, keepdims=True)
            va = ((og - m) ** 2).mean(-1, keepdims=True)
            og = ((og - m) / jnp.sqrt(va + 1e-05)).reshape(b, l, e) * gn_w + gn_b
            x1 = x + og * g @ Wo.T
            xc = _ln(x1, ln2_w, ln2_b)
            sx2 = jnp.concatenate([state[:, 0:1] - xc[:, :1], xc[:, :-1] - xc[:, 1:]], axis=1)
            xk2 = xc + sx2 * ffn_maa_k
            xr2 = xc + sx2 * ffn_maa_r
            rr = jax.nn.sigmoid(xr2 @ Wfr.T)
            kk = jnp.square(jax.nn.relu(xk2 @ Wfk.T))
            return x1 + rr * (kk @ Wfv.T)
        return _block(x, state, ln1_w, ln1_b, ln2_w, ln2_b, maa_x, maa_w1, maa_w2, maa_stack, time_decay, td_w1, td_w2, u, Wr, Wk, Wv, Wg, Wo, gn_w, gn_b, ffn_maa_k, ffn_maa_r, Wfk, Wfr, Wfv)
    x = _L0_xattn_ref(x, ctx_2048, mask_1x1xSxS2_fc1, mask_Bx1xSxS2_ff1, L0_xattn_ln1_s, L0_xattn_ln1_b, L0_xattn_w_qkv, L0_xattn_b_qkv, L0_xattn_w_ao, L0_xattn_b_ao, L0_xattn_ln2_s, L0_xattn_ln2_b, L0_xattn_w_q, L0_xattn_b_q, L0_xattn_w_kv, L0_xattn_b_kv, L0_xattn_w_co, L0_xattn_b_co, L0_xattn_ln3_s, L0_xattn_ln3_b, L0_xattn_w1, L0_xattn_b1, L0_xattn_w2, L0_xattn_b2)
    x = _L1_xattn_ref(x, ctx_2048, ctx_2048, L1_xattn_ln1_scale, L1_xattn_ln1_offset, L1_xattn_wq1, L1_xattn_bq1, L1_xattn_wk1, L1_xattn_bk1, L1_xattn_wv1, L1_xattn_bv1, L1_xattn_wo1, L1_xattn_bo1, L1_xattn_bias_k1, L1_xattn_bias_v1, L1_xattn_ln2_scale, L1_xattn_ln2_offset, L1_xattn_wq2, L1_xattn_bq2, L1_xattn_wk2, L1_xattn_bk2, L1_xattn_wv2, L1_xattn_bv2, L1_xattn_wo2, L1_xattn_bo2, L1_xattn_bias_k2, L1_xattn_bias_v2, L1_xattn_ln_mlp_scale, L1_xattn_ln_mlp_offset, L1_xattn_w_fc1, L1_xattn_b_fc1, L1_xattn_w_fc2, L1_xattn_b_fc2)
    x = _L2_xattn_ref(x, ctx_2048, L2_xattn_w_q, L2_xattn_w_k, L2_xattn_w_v, L2_xattn_w_o, L2_xattn_alpha)
    x = _L3_xattn_ref(x, ctx_2048, L3_xattn_ln1_w, L3_xattn_ln1_b, L3_xattn_ln2_w, L3_xattn_ln2_b, L3_xattn_maa_x, L3_xattn_maa_w1, L3_xattn_maa_w2, L3_xattn_maa_stack, L3_xattn_time_decay, L3_xattn_td_w1, L3_xattn_td_w2, L3_xattn_u, L3_xattn_Wr, L3_xattn_Wk, L3_xattn_Wv, L3_xattn_Wg, L3_xattn_Wo, L3_xattn_gn_w, L3_xattn_gn_b, L3_xattn_ffn_maa_k, L3_xattn_ffn_maa_r, L3_xattn_Wfk, L3_xattn_Wfr, L3_xattn_Wfv)
    return x

_drawn_inputs = setup_inputs


def setup_inputs(seed=0):
    import zlib

    import numpy as np

    out = dict(_drawn_inputs(seed))
    spreads = {'L0_xattn_ln1_s': (1.0, 0.6),
     'L0_xattn_ln1_b': (0.0, 0.789),
     'L0_xattn_b_qkv': (0.0, 0.281),
     'L0_xattn_b_ao': (0.0, 0.1),
     'L0_xattn_ln2_s': (1.0, 0.6),
     'L0_xattn_ln2_b': (0.0, 2.0),
     'L0_xattn_b_q': (0.0, 2.0),
     'L0_xattn_b_kv': (0.0, 0.292),
     'L0_xattn_b_co': (0.0, 0.1),
     'L0_xattn_ln3_s': (1.0, 0.6),
     'L0_xattn_ln3_b': (0.0, 0.682),
     'L0_xattn_b1': (0.0, 0.1),
     'L0_xattn_b2': (0.0, 0.1),
     'L1_xattn_ln1_scale': (1.0, 0.6),
     'L1_xattn_ln1_offset': (0.0, 0.8),
     'L1_xattn_bq1': (0.0, 0.8),
     'L1_xattn_bk1': (0.0, 2.0),
     'L1_xattn_bv1': (0.0, 0.1),
     'L1_xattn_bo1': (0.0, 0.1),
     'L1_xattn_ln2_scale': (1.0, 0.6),
     'L1_xattn_ln2_offset': (0.0, 0.8),
     'L1_xattn_bq2': (0.0, 0.8),
     'L1_xattn_bk2': (0.0, 2.0),
     'L1_xattn_bv2': (0.0, 0.1),
     'L1_xattn_bo2': (0.0, 0.1),
     'L1_xattn_ln_mlp_scale': (1.0, 0.6),
     'L1_xattn_ln_mlp_offset': (0.0, 0.681),
     'L1_xattn_b_fc1': (0.0, 0.1),
     'L1_xattn_b_fc2': (0.0, 0.1),
     'L3_xattn_ln1_w': (1.0, 0.557),
     'L3_xattn_ln1_b': (0.0, 0.55),
     'L3_xattn_ln2_w': (1.0, 0.6),
     'L3_xattn_ln2_b': (0.0, 0.8),
     'L3_xattn_gn_w': (1.0, 0.6),
     'L3_xattn_gn_b': (0.0, 0.8)}
    factors = {'L0_xattn_w_qkv': 4.272,
     'L0_xattn_w_q': 8.0,
     'L1_xattn_wq1': 8.0,
     'L1_xattn_wk1': 8.0,
     'L1_xattn_bias_k1': 64.0,
     'L1_xattn_bias_v1': 64.0,
     'L1_xattn_wq2': 8.0,
     'L1_xattn_wk2': 8.0,
     'L1_xattn_bias_k2': 64.0,
     'L1_xattn_bias_v2': 64.0,
     'L2_xattn_w_q': 2.676,
     'L2_xattn_w_k': 2.705,
     'L3_xattn_maa_x': 8.0,
     'L3_xattn_maa_w1': 8.0,
     'L3_xattn_maa_w2': 8.0,
     'L3_xattn_maa_stack': 3.002,
     'L3_xattn_time_decay': 2.835,
     'L3_xattn_td_w1': 8.0,
     'L3_xattn_td_w2': 8.0,
     'L3_xattn_u': 5.764,
     'L3_xattn_ffn_maa_k': 8.0,
     'L3_xattn_ffn_maa_r': 8.0,
     'L3_xattn_Wfk': 2.918,
     'L3_xattn_Wfr': 8.0,
     'L3_xattn_Wfv': 2.711}
    for name, (base, spread) in spreads.items():
        noise = np.random.default_rng([zlib.crc32(name.encode()), seed]).standard_normal(out[name].shape)
        drawn = base * np.exp(spread * noise) if base else spread * noise
        out[name] = jnp.asarray(drawn.astype(out[name].dtype))
    for name, factor in factors.items():
        out[name] = (out[name] * factor).astype(out[name].dtype)
    return out
```

```python
from contextlib import ExitStack

import numpy as np

import concourse.bass as bass
from concourse import mybir

ALU = mybir.AluOpType
ACT = mybir.ActivationFunctionType
F32 = mybir.dt.float32
AX_X = mybir.AxisListType.X

P = 128
NB = 16
D = 256
KC = D // P
PAIR = 2
NP = NB // PAIR
TOK = NB * P
PT = PAIR * P
EPS = 1e-5
HG = 4
DMA = 16

COLUMNS = [
    ("L0_xattn_ln1_s", D), ("L0_xattn_ln1_b", D), ("L0_xattn_ln2_s", D), ("L0_xattn_ln2_b", D),
    ("L0_xattn_ln3_s", D), ("L0_xattn_ln3_b", D), ("L0_xattn_b_qkv", 3 * D), ("L0_xattn_b_q", D),
    ("L0_xattn_b_kv", 2 * D), ("L0_xattn_b1", 4 * D),
    ("L1_xattn_ln1_scale", D), ("L1_xattn_ln1_offset", D), ("L1_xattn_ln2_scale", D),
    ("L1_xattn_ln2_offset", D), ("L1_xattn_ln_mlp_scale", D), ("L1_xattn_ln_mlp_offset", D),
    ("L1_xattn_bq1", 2048), ("L1_xattn_bk1", 2048), ("L1_xattn_bv1", 2048),
    ("L1_xattn_bias_k1", 2048), ("L1_xattn_bias_v1", 2048),
    ("L1_xattn_bq2", 2048), ("L1_xattn_bk2", 2048), ("L1_xattn_bv2", 2048),
    ("L1_xattn_bias_k2", 2048), ("L1_xattn_bias_v2", 2048), ("L1_xattn_b_fc1", 4 * D),
    ("L3_xattn_ln1_w", D), ("L3_xattn_ln1_b", D), ("L3_xattn_ln2_w", D), ("L3_xattn_ln2_b", D),
    ("L3_xattn_maa_x", D), ("L3_xattn_maa_stack", 5 * D), ("L3_xattn_time_decay", D),
    ("L3_xattn_u", D), ("L3_xattn_ffn_maa_k", D), ("L3_xattn_ffn_maa_r", D),
]
ROWS = ["L0_xattn_b_ao", "L0_xattn_b_co", "L0_xattn_b2", "L1_xattn_bo1", "L1_xattn_bo2",
        "L1_xattn_b_fc2", "L3_xattn_gn_w", "L3_xattn_gn_b"]
COLUMN_AT, at = {}, 0
for name, size in COLUMNS:
    COLUMN_AT[name] = at
    at += size // P
N_COLUMNS = at

STAGES = ["l0_self", "l0_cross", "l0_mlp", "l1_first", "l1_second", "l1_mlp", "l2", "l3"]


def wait(eng, sem, value):
    if isinstance(value, int) and value <= 0:
        return
    eng.wait_ge(sem, value)


def over_pairs(eng, body):
    body(0)
    with eng.Fori(1, NP - 1) as p:
        body(p)
    body(NP - 1)


def over_steps(eng, body):
    def step(s):
        for par in range(2):
            body(s * 2 + par, par)
    step(0)
    with eng.Fori(1, NP // 2 - 1) as s:
        step(s)
    step(NP // 2 - 1)


class Core:

    def __init__(self, nc, ctx, dram, out):
        self.nc, self.dram, self.out = nc, dram, out
        sb = lambda name, shape: ctx.enter_context(nc.sbuf_tensor(name, shape, F32))
        self.x = sb("x", [P, NB, D])
        self.cT = sb("ctx_t", [P, KC, TOK])
        self.ident = sb("ident", [P, P])
        self.cols = sb("cols", [P, N_COLUMNS])
        self.rows = sb("rows", [P, len(ROWS), D])
        self.mv = sb("mean_var", [P, NB, 2])
        self.rstd = sb("rstd", [P, NB])
        self.std = sb("std", [P, NB])
        self.newton = sb("newton", [P, NB])
        self.stats = sb("bn_stats", [P, PAIR, 6])
        self.mv_new = sb("mean_var_new", [P, PAIR, 2])
        self.x_new = sb("x_new", [P, PAIR, D])
        self.eps = sb("eps", [P, 1])
        self.head_rows = sb("head_rows", [P, 8])
        self.head_rows2 = sb("head_rows2", [P, 16])
        self.banks = ctx.enter_context(nc.psum_tensor("banks", [P, 8, 512], F32))
        self.bank = [self.banks[:, i, :] for i in range(8)]

    def col(self, name, k=0, n=1):
        at = COLUMN_AT[name] + k
        return self.cols[:, at:at + n]

    def row(self, name):
        return self.rows[:, ROWS.index(name), :]


def zero_signals(core, signals):
    numbers = sorted(s.num for s in signals)
    starts = [n for n in numbers if n - 1 not in numbers]
    ends = [n + 1 for n in numbers if n + 1 not in numbers]
    with core.nc.Block() as block:
        @block.gpsimd
        def _(gp):
            for start, end in zip(starts, ends):
                gp.sem_clear(range(start, end))


class Signals:

    def __init__(self, core, ctx, prefix):
        self.core, self.nc, self.prefix, self.all = core, core.nc, prefix, []
        ctx.callback(self.close)
        self.holders = ExitStack()

    def __call__(self, name):
        self.all.append(self.holders.enter_context(self.nc.semaphore(self.prefix + name)))
        return self.all[-1]

    def close(self):
        zero_signals(self.core, self.all)
        self.holders.close()


def load_stage(core, reload_x=True):
    nc = core.nc
    with ExitStack() as ctx:
        sem = Signals(core, ctx, "")
        x_in, consts_in, filled = sem("ld_x"), sem("ld_consts"), sem("ld_filled")
        copied, stat = sem("ld_copied"), sem("ld_stat")
        block = ctx.enter_context(nc.Block())

        @block.sync
        def _(sp):
            sp.dma_start(core.x[:, :, :], core.dram["x"].rearrange("b t d -> t b d")).then_inc(x_in, DMA)
            sp.dma_start(core.cols[:, :], core.dram["columns"]).then_inc(consts_in, DMA)
            sp.dma_start(core.rows[:, :, :], core.dram["rows"]).then_inc(consts_in, DMA)
            sp.dma_start(core.cT[:, :, :], core.dram["ctx_t"].rearrange("(k p) t -> p k t", p=P)).then_inc(consts_in, DMA)
            sp.wait_ge(consts_in, 3 * DMA)

        @block.gpsimd
        def _(gp):
            gp.memset(core.eps[:, :], EPS).then_inc(filled, 1)
            gp.memset(core.ident[:, :], 0.0).then_inc(filled, 1)
            gp.wait_ge(filled, 2)
            gp.affine_select(out=core.ident[:, :], in_=core.ident[:, :], compare_op=ALU.not_equal, fill=1.0,
                             base=0, pattern=[[-1, P]], channel_multiplier=1).then_inc(filled, 1)
            gp.memset(core.head_rows2[:, :], 1.0).then_inc(filled, 1)
            gp.wait_ge(filled, 4)
            gp.affine_select(out=core.head_rows2[:, :], in_=core.head_rows2[:, :], compare_op=ALU.is_ge, fill=0.0,
                             base=0, pattern=[[0, 2], [-16, 8]], channel_multiplier=1).then_inc(filled, 1)
            gp.wait_ge(filled, 5)
            gp.affine_select(out=core.head_rows2[:, :], in_=core.head_rows2[:, :], compare_op=ALU.is_ge, fill=0.0,
                             base=15, pattern=[[0, 2], [16, 8]], channel_multiplier=-1).then_inc(filled, 1)
            gp.wait_ge(filled, 6)
            gp.tensor_copy(core.head_rows[:, :], core.head_rows2[:, 0:8]).then_inc(filled, 1)

        @block.vector
        def _(dve):
            dve.wait_ge(x_in, DMA)
            def body(p):
                wait(dve, stat, p * (2 * PAIR + 1))
                dve.tensor_copy(core.x_new[:, :, :], core.x[:, bass.ds(p * PAIR, PAIR), :]).then_inc(copied, 1)
                dve.wait_ge(copied, p + 1)
                row_stats(core, dve, stat, p, p * (2 * PAIR + 1))
            over_pairs(dve, body)


def row_stats(core, dve, stat, p, before):
    for b in range(PAIR):
        dve.bn_stats(core.stats[:, b, :], core.x_new[:, b, :]).then_inc(stat, 1)
    dve.wait_ge(stat, before + PAIR)
    dve.tensor_scalar(core.x[:, bass.ds(p * PAIR, PAIR), :], core.x_new[:, :, :], 1.0, None, ALU.mult)
    for b in range(PAIR):
        dve.bn_aggr(core.mv_new[:, b, :], core.stats[:, b, :]).then_inc(stat, 1)
    dve.wait_ge(stat, before + 2 * PAIR)
    dve.tensor_scalar(core.mv[:, bass.ds(p * PAIR, PAIR), :], core.mv_new[:, :, :], 1.0, None, ALU.mult).then_inc(stat, 1)


def new_rows(core, dve, step, stat, p, update, update_ready, bias=None):
    steps = 1 if bias is None else 2
    dve.wait_ge(update_ready, p + 1)
    wait(dve, stat, p * (2 * PAIR + 1))
    dve.tensor_tensor(core.x_new[:, :, :], core.x[:, bass.ds(p * PAIR, PAIR), :], update, ALU.add).then_inc(step, 1)
    dve.wait_ge(step, p * steps + 1)
    if bias is not None:
        dve.tensor_tensor(core.x_new[:, :, :], core.x_new[:, :, :], bias[:, None, :].to_broadcast([P, PAIR, D]), ALU.add).then_inc(step, 1)
        dve.wait_ge(step, p * steps + 2)
    row_stats(core, dve, stat, p, p * (2 * PAIR + 1))


def rstd_scalar(core, act, root):
    act.activation(core.std[:, :], core.mv[:, :, 1], ACT.Sqrt, bias=core.eps[:, 0:1]).then_inc(root, 1)


def rstd_vector(core, dve, root, step):
    dve.wait_ge(root, 1)
    dve.reciprocal(core.rstd[:, :], core.std[:, :]).then_inc(step, 1)
    dve.wait_ge(step, 1)
    dve.tensor_tensor(core.newton[:, :], core.rstd[:, :], core.rstd[:, :], ALU.mult).then_inc(step, 1)
    dve.tensor_scalar(core.std[:, :], core.mv[:, :, 1], EPS, -0.5, ALU.add, ALU.mult).then_inc(step, 1)
    dve.wait_ge(step, 3)
    dve.tensor_tensor(core.newton[:, :], core.newton[:, :], core.std[:, :], ALU.mult).then_inc(step, 1)
    dve.wait_ge(step, 4)
    dve.scalar_tensor_tensor(core.rstd[:, :], core.newton[:, :], 1.5, core.rstd[:, :],
                             ALU.add, ALU.mult).then_inc(step, 1)
    dve.wait_ge(step, 5)


def wide_attention(core, n):
    nc = core.nc
    H, HD = 16, P
    NHG = H // HG
    SCALE = float(HD) ** -0.5
    pre = "L1_xattn_"
    ln_s, ln_b = pre + f"ln{n}_scale", pre + f"ln{n}_offset"
    bq, bk, bv = pre + f"bq{n}", pre + f"bk{n}", pre + f"bv{n}"
    bias_k, bias_v = pre + f"bias_k{n}", pre + f"bias_v{n}"
    with ExitStack() as ctx:
        sb = lambda name, shape: ctx.enter_context(nc.sbuf_tensor(f"w{n}_{name}", shape, F32))
        sem = Signals(core, ctx, f"w{n}_")
        wq, wk, wv = (sb(w, [P, KC, H * HD]) for w in ("wq", "wk", "wv"))
        wo = sb("wo", [P, H, D])
        xn = sb("xn", [P, PAIR, D])
        hT = sb("hT", [P, KC, PT])
        kv_in = sb("kv_in", [P, KC, PT])
        qT, kT = sb("qT", [P, HG, PT]), sb("kT", [P, HG, PT])
        v = sb("v", [P, 2, PAIR, HG * HD])
        prob = sb("prob", [P, PAIR, HG, P])
        probT = sb("probT", [P, PAIR, HG, P])
        headT = sb("headT", [P, H, PT])
        own = sb("own", [P, PAIR, HG])
        top = sb("top", [P, PAIR, HG])
        shift = sb("shift", [P, PAIR, HG])
        own_e = sb("own_e", [P, PAIR, HG])
        total = sb("total", [P, PAIR, HG])
        inv = sb("inv", [P, PAIR, HG])
        own_p = sb("own_p", [P, PAIR, H])
        own_pT = sb("own_pT", [H, PT])
        dvz = sb("dvz", [P, H, H])
        bvo = sb("bvo", [H, D])
        obias = sb("obias", [P, D])
        bank = core.bank
        BL, LN = bank[2], bank[7]

        w_in = [sem(f"in_{w}") for w in ("wq", "wk", "wv", "wo")]
        root, rstep = sem("root"), sem("rstep")
        hn_ok, lt_ok, hT_ok = sem("hn_ok"), sem("lt_ok"), sem("hT_ok")
        kv_ok = sem("kv_ok")
        proj_ok, qk_ok, v_ok = sem("proj_ok"), sem("qk_ok"), sem("v_ok")
        own_ready, own_copied = sem("own_ready"), sem("own_copied")
        score_ok, top_step, shift_ok, exp_ok = sem("score_ok"), sem("top_step"), sem("shift_ok"), sem("exp_ok")
        norm_step, prob_ok = sem("norm_step"), sem("prob_ok")
        pt_ok, probT_ok, pv_ok, head_ok = sem("pt_ok"), sem("probT_ok"), sem("pv_ok"), sem("head_ok")
        ot_ok, own_pT_ok, out_ok = sem("ot_ok"), sem("own_pT_ok"), sem("out_ok")
        dv_step, const_ok, const_copied = sem("dv_step"), sem("const_ok"), sem("const_copied")
        res_ok, stat = sem("res_ok"), sem("stat")
        block = ctx.enter_context(nc.Block())

        @block.sync
        def _(sp):
            for i, (tile, w) in enumerate(((wq, "wq"), (wk, "wk"), (wv, "wv"))):
                sp.dma_start(tile[:, :, :], core.dram[pre + w + str(n)].rearrange("(k p) o -> p k o", p=P)).then_inc(w_in[i], DMA)
            sp.dma_start(wo[:, :, :], core.dram[pre + f"wo{n}"].rearrange("(h p) o -> p h o", p=P)).then_inc(w_in[3], DMA)

            def body(p):
                wait(sp, proj_ok, p * (6 * NHG))
                sp.dma_start(kv_in[:, :, :], core.cT[:, :, bass.ts(p, PT)]).then_inc(kv_ok, DMA)
            over_pairs(sp, body)

        @block.tensor
        def _(pe):
            def ln_transpose(p):
                if not isinstance(p, int) or p > 1:
                    wait(pe, res_ok, (p - 1) * 2 - 1)
                pe.wait_ge(hn_ok, p * PAIR + PAIR)
                for k in range(KC):
                    for b in range(PAIR):
                        mm = pe.transpose(LN[:, k * PT + b * P:k * PT + (b + 1) * P], xn[:, b, k * P:(k + 1) * P], core.ident[:, :])
                mm.then_inc(lt_ok, 1)

            def project_qk(p, g, u):
                if g == 0:
                    pe.wait_ge(hT_ok, p + 1)
                if isinstance(p, int) and p == 0 and g == 0:
                    pe.wait_ge(w_in[0], DMA)
                for use in range(4):
                    w, rhs = (wq, hT) if use < 2 else (wk, None)
                    if use == 2 and isinstance(p, int) and p == 0 and g == 0:
                        pe.wait_ge(w_in[1], DMA)
                    if use < 2:
                        wait(pe, v_ok, u * 2 - 1 + use)
                    else:
                        pe.wait_ge(qk_ok, u * 4 + use - 1)
                    for i in range(2):
                        h = g * HG + (use % 2) * 2 + i
                        for k in range(KC):
                            moving = hT[:, k, :] if use < 2 else core.cT[:, k, bass.ts(p, PT)]
                            mm = pe.matmul(bank[use % 2][:, i * PT:(i + 1) * PT], w[:, k, h * HD:(h + 1) * HD], moving,
                                           start=(k == 0), stop=(k == KC - 1))
                    mm.then_inc(proj_ok, 1)

            def project_v(p, g, u):
                if g == 0:
                    pe.wait_ge(kv_ok, p * DMA + DMA)
                if isinstance(p, int) and p == 0 and g == 0:
                    pe.wait_ge(w_in[2], DMA)
                for b in range(PAIR):
                    pe.wait_ge(qk_ok, u * 4 + 3 + b)
                    for k in range(KC):
                        mm = pe.matmul(bank[b][:, :], kv_in[:, k, b * P:(b + 1) * P], wv[:, k, g * HG * HD:(g + 1) * HG * HD],
                                       start=(k == 0), stop=(k == KC - 1))
                    mm.then_inc(proj_ok, 1)

            def scores(u, g):
                pe.wait_ge(qk_ok, u * 4 + 4)
                wait(pe, own_copied, u)
                for b in range(PAIR):
                    for i in range(HG):
                        mm = pe.matmul(BL[:, b * HG + i:b * HG + i + 1], qT[:, i, b * P:(b + 1) * P],
                                       core.col(bias_k, g * HG + i), start=True, stop=True)
                mm.then_inc(own_ready, 1)
                for b in range(PAIR):
                    wait(pe, exp_ok, u * 2 - 1 + b)
                    for i in range(HG):
                        mm = pe.matmul(bank[3 + b][:, i * P:(i + 1) * P], qT[:, i, b * P:(b + 1) * P], kT[:, i, b * P:(b + 1) * P],
                                       start=True, stop=True)
                    mm.then_inc(score_ok, 1)

            def prob_transpose(u):
                for b in range(PAIR):
                    pe.wait_ge(prob_ok, u * 2 + 1 + b)
                    wait(pe, head_ok, u * 2 - 1 + b)
                    for i in range(HG):
                        mm = pe.transpose(bank[5 + b][:, i * P:(i + 1) * P], prob[:, b, i, :], core.ident[:, :])
                    mm.then_inc(pt_ok, 1)

            def weigh_values(u, par):
                pe.wait_ge(probT_ok, u * 2 + 2)
                pe.wait_ge(v_ok, u * 2 + 2)
                for half in range(2):
                    for i in (half * 2, half * 2 + 1):
                        for b in range(PAIR):
                            at = (i % 2) * PT + b * P
                            mm = pe.matmul(bank[5 + half][:, at:at + P], v[:, par, b, i * HD:(i + 1) * HD], probT[:, b, i, :],
                                           start=True, stop=True)
                    mm.then_inc(pv_ok, 1)

            def own_transpose(p):
                pe.wait_ge(prob_ok, (p + 1) * (2 * NHG))
                if isinstance(p, int) and p == NP - 1:
                    pe.wait_ge(hT_ok, NP)
                else:
                    pe.wait_ge(hT_ok, p + 2)
                for b in range(PAIR):
                    mm = pe.transpose(LN[0:H, b * P:(b + 1) * P], own_p[:, b, :], core.ident[:, :])
                mm.then_inc(ot_ok, 1)

            def project_out(p):
                pe.wait_ge(own_pT_ok, p + 1)
                pe.wait_ge(head_ok, (p + 1) * (2 * NHG))
                for b in range(PAIR):
                    at = LN[:, b * D:(b + 1) * D]
                    pe.matmul(at, own_pT[:, b * P:(b + 1) * P], bvo[:, :], start=True, stop=False)
                    for h in range(H):
                        mm = pe.matmul(at, headT[:, h, b * P:(b + 1) * P], wo[:, h, :], start=False, stop=(h == H - 1))
                mm.then_inc(out_ok, 1)

            def constants():
                pe.wait_ge(w_in[3], DMA)
                pe.wait_ge(dv_step, 3)
                for h in range(H):
                    mm = pe.matmul(bank[5][0:H, 0:D], dvz[:, h, :], wo[:, h, :], start=(h == 0), stop=(h == H - 1))
                mm.then_inc(const_ok, 1)
                for h in range(H):
                    mm = pe.matmul(bank[6][:, 0:D], core.col(bv, h).to_broadcast([P, P]), wo[:, h, :],
                                   start=(h == 0), stop=(h == H - 1))
                mm.then_inc(const_ok, 1)

            def body(p):
                last = isinstance(p, int) and p == NP - 1
                for g in range(NHG):
                    u = p * NHG + g
                    p1, g1 = (p, g + 1) if g < NHG - 1 else (p + 1, 0)
                    if g == 0 and not (isinstance(p, int) and p == 0):
                        own_transpose(p - 1)
                    scores(u, g)
                    more = not (last and g == NHG - 1)
                    if more:
                        project_qk(p1, g1, u + 1)
                    if g == 0 and not (isinstance(p, int) and p == 0):
                        project_out(p - 1)
                    if g == NHG - 2 and not last:
                        ln_transpose(p + 1)
                    if isinstance(u, int) and u == 0:
                        constants()
                        pe.wait_ge(const_copied, 2)
                    prob_transpose(u)
                    if more:
                        project_v(p1, g1, u + 1)
                    weigh_values(u, g % 2)

            ln_transpose(0)
            project_qk(0, 0, 0)
            project_v(0, 0, 0)
            over_pairs(pe, body)
            own_transpose(NP - 1)
            project_out(NP - 1)

        @block.scalar
        def _(act):
            def layer_norm(p):
                act.wait_ge(lt_ok, p + 1)
                for k in range(KC):
                    done = act.activation(hT[:, k, :], LN[:, k * PT:(k + 1) * PT], ACT.Identity,
                                          scale=core.col(ln_s, k), bias=core.col(ln_b, k))
                done.then_inc(hT_ok, 1)

            def copy_v(u, par):
                for b in range(PAIR):
                    act.wait_ge(proj_ok, u * 6 + 5 + b)
                    act.activation(v[:, par, b, :], bank[b][:, :], ACT.Copy).then_inc(v_ok, 1)

            def body(p):
                last = isinstance(p, int) and p == NP - 1
                for g in range(NHG):
                    u = p * NHG + g
                    for b in range(PAIR):
                        act.wait_ge(shift_ok, u * 2 + 1 + b)
                        for i in range(HG):
                            act.activation(prob[:, b, i, :], bank[3 + b][:, i * P:(i + 1) * P], ACT.Exp, scale=SCALE,
                                           bias=shift[:, b, i:i + 1], accum_out=total[:, b, i:i + 1])
                        act.activation(own_e[:, b, :], own_e[:, b, :], ACT.Exp).then_inc(exp_ok, 1)
                    if g == NHG - 2 and not last:
                        layer_norm(p + 1)
                    for b in range(PAIR):
                        act.wait_ge(pt_ok, u * 2 + 1 + b)
                        act.activation(probT[:, b, :, :], bank[5 + b][:, :].rearrange("p (h q) -> p h q", h=HG),
                                       ACT.Copy).then_inc(probT_ok, 1)
                    if not (last and g == NHG - 1):
                        copy_v(u + 1, (g + 1) % 2)

            rstd_scalar(core, act, root)
            layer_norm(0)
            copy_v(0, 0)
            over_pairs(act, body)

        @block.vector
        def _(dve):
            def normalise(p):
                wait(dve, lt_ok, p)
                for b in range(PAIR):
                    i = p * PAIR + b
                    dve.tensor_scalar(xn[:, b, :], core.x[:, i, :], core.mv[:, i, 0:1], core.rstd[:, bass.ds(i, 1)],
                                      ALU.subtract, ALU.mult).then_inc(hn_ok, 1)

            def copy_qk(g, u, use):
                dve.wait_ge(proj_ok, u * 6 + 1 + use)
                h, to, bias = (use % 2) * 2, (qT, kT)[use // 2], (bq, bk)[use // 2]
                dve.tensor_tensor(to[:, h:h + 2, :], bank[use % 2][:, :].rearrange("p (h t) -> p h t", h=2),
                                  core.col(bias, g * HG + h, 2)[:, :, None].to_broadcast([P, 2, PT]), ALU.add).then_inc(qk_ok, 1)

            def row_max(u):
                dve.wait_ge(own_ready, u + 1)
                wait(dve, prob_ok, u * 2)
                dve.tensor_copy(own[:, :, :], BL[:, 0:PAIR * HG].rearrange("p (b h) -> p b h", b=PAIR)).then_inc(own_copied, 1)
                for b in range(PAIR):
                    step = u * 6 + b * 3
                    dve.wait_ge(score_ok, u * 2 + 1 + b)
                    dve.tensor_reduce(top[:, b, :], bank[3 + b][:, :].rearrange("p (h k) -> p h k", h=HG), AX_X,
                                      ALU.max).then_inc(top_step, 1)
                    dve.wait_ge(top_step, step + 1)
                    dve.wait_ge(own_copied, u + 1)
                    dve.tensor_tensor(top[:, b, :], top[:, b, :], own[:, b, :], ALU.max).then_inc(top_step, 1)
                    dve.wait_ge(top_step, step + 2)
                    dve.tensor_tensor(own_e[:, b, :], own[:, b, :], top[:, b, :], ALU.subtract).then_inc(top_step, 1)
                    dve.tensor_scalar(shift[:, b, :], top[:, b, :], -SCALE, None, ALU.mult)
                    dve.wait_ge(top_step, step + 3)
                    dve.tensor_scalar(own_e[:, b, :], own_e[:, b, :], SCALE, None, ALU.mult).then_inc(shift_ok, 1)

            def scale_probs(g, u, b):
                dve.wait_ge(exp_ok, u * 2 + 1 + b)
                step = u * 4 + b * 2
                dve.tensor_tensor(total[:, b, :], total[:, b, :], own_e[:, b, :], ALU.add).then_inc(norm_step, 1)
                dve.wait_ge(norm_step, step + 1)
                dve.reciprocal(inv[:, b, :], total[:, b, :]).then_inc(norm_step, 1)
                dve.wait_ge(norm_step, step + 2)
                dve.tensor_tensor(own_p[:, b, g * HG:(g + 1) * HG], own_e[:, b, :], inv[:, b, :], ALU.mult)
                dve.tensor_tensor(prob[:, b, :, :], prob[:, b, :, :], inv[:, b, :, None].to_broadcast([P, HG, P]),
                                  ALU.mult).then_inc(prob_ok, 1)

            def copy_heads(g, u):
                for half in range(2):
                    dve.wait_ge(pv_ok, u * 2 + 1 + half)
                    h = g * HG + half * 2
                    dve.tensor_copy(headT[:, h:h + 2, :], bank[5 + half][:, :].rearrange("p (h t) -> p h t", h=2)).then_inc(head_ok, 1)

            def copy_own(p):
                dve.wait_ge(ot_ok, p + 1)
                dve.tensor_copy(own_pT[:, :], LN[0:H, 0:PT]).then_inc(own_pT_ok, 1)

            def residual(p):
                new_rows(core, dve, res_ok, stat, p, LN[:, :].rearrange("p (b d) -> p b d", b=PAIR), out_ok, obias)

            def body(p):
                first = isinstance(p, int) and p == 0
                last = isinstance(p, int) and p == NP - 1
                for g in range(NHG):
                    u = p * NHG + g
                    g1 = (g + 1) % NHG
                    more = not (last and g == NHG - 1)
                    if g == 0 and not first:
                        copy_own(p - 1)
                    row_max(u)
                    if more:
                        copy_qk(g1, u + 1, 0)
                        copy_qk(g1, u + 1, 1)
                    scale_probs(g, u, 0)
                    if more:
                        copy_qk(g1, u + 1, 2)
                    scale_probs(g, u, 1)
                    if more:
                        copy_qk(g1, u + 1, 3)
                    if g == 0 and not first:
                        residual(p - 1)
                    if g == 1 and not last:
                        normalise(p + 1)
                    if isinstance(u, int) and u == 0:
                        dve.wait_ge(const_ok, 2)
                        dve.tensor_copy(bvo[:, :], bank[5][0:H, 0:D]).then_inc(const_copied, 1)
                        dve.tensor_tensor(obias[:, :], bank[6][:, 0:D], core.row(pre + f"bo{n}"), ALU.add).then_inc(const_copied, 1)
                    copy_heads(g, u)

            rstd_vector(core, dve, root, rstep)
            normalise(0)
            dve.memset(dvz[:, :, :], 0.0).then_inc(dv_step, 1)
            dve.tensor_tensor(own_p[:, 0, :], core.col(bias_v, 0, H), core.col(bv, 0, H), ALU.subtract).then_inc(dv_step, 1)
            dve.wait_ge(dv_step, 2)
            dve.tensor_copy(dvz[:, :, :].rearrange("p a b -> p (a b)")[:, 0:H * H:H + 1], own_p[:, 0, :]).then_inc(dv_step, 1)
            dve.wait_ge(dv_step, 3)
            for use in range(4):
                copy_qk(0, 0, use)
            over_pairs(dve, body)
            copy_own(NP - 1)
            residual(NP - 1)


def narrow_attention(core, kind):
    nc = core.nc
    H, HD = 16, 16
    NHG = H // HG
    TILE_HEADS = P // HD
    SCALE = 0.25
    MASKED = 10000.0 / SCALE
    pre = "L0_xattn_"
    self_attn = kind == "self"
    nln = 1 if self_attn else 2
    ln_s, ln_b = pre + f"ln{nln}_s", pre + f"ln{nln}_b"
    n_mask = 1 if self_attn else NB
    with ExitStack() as ctx:
        sb = lambda name, shape: ctx.enter_context(nc.sbuf_tensor(f"n{kind}_{name}", shape, F32))
        sem = Signals(core, ctx, f"n{kind}_")
        wqkv = sb("wqkv", [P, KC, 3 * D])
        wo = sb("wo", [P, KC, D])
        mask = sb("mask", [P, n_mask, P])
        less = sb("less", [P, n_mask, P])
        less_pair = None if self_attn else sb("less_pair", [P, 2, PAIR, P])
        q_bias = sb("q_bias", [P, H])
        xn = sb("xn", [P, PAIR, D])
        hT = sb("hT", [P, KC, PT])
        kv_in = hT if self_attn else sb("kv_in", [P, KC, PT])
        qT = sb("qT", [P, H, PT])
        kT = sb("kT", [P, KC, PT])
        v = sb("v", [P, PAIR, D])
        prob = sb("prob", [P, 2, PAIR, HG, P])
        probT = sb("probT", [P, PAIR, HG, P])
        top = sb("top", [P, PAIR, HG])
        shift = sb("shift", [P, 2, PAIR, HG])
        total = sb("total", [P, PAIR, H])
        inv = sb("inv", [P, PAIR, H])
        head = sb("head", [P, PAIR, D])
        headT = sb("headT", [P, KC, PT])
        bank = core.bank
        CTX, OUT = bank[6], bank[7]

        if self_attn:
            bias_q, bias_k, bias_v = [(pre + "b_qkv", i * KC) for i in range(3)]
            out_bias, w_out = pre + "b_ao", pre + "w_ao"
        else:
            bias_q, bias_k, bias_v = (pre + "b_q", 0), (pre + "b_kv", 0), (pre + "b_kv", KC)
            out_bias, w_out = pre + "b_co", pre + "w_co"

        w_in, wo_in, mask_in = sem("w_in"), sem("wo_in"), sem("mask_in")
        root, rstep, less_ok, q_bias_ok = sem("root"), sem("rstep"), sem("less_ok"), sem("q_bias_ok")
        pair_ok = [sem(f"pair_ok{par}") for par in range(2)]
        hn_ok, lt_ok, hT_ok, kv_ok = sem("hn_ok"), sem("lt_ok"), sem("hT_ok"), sem("kv_ok")
        proj_ok = sem("proj_ok")
        q0_ok, q1_ok, k_ok, v_ok = sem("q0_ok"), sem("q1_ok"), sem("k_ok"), sem("v_ok")
        score_ok, kept_ok, masked_ok, top_ok, shift_ok = (sem(s) for s in ("score", "kept", "masked", "top", "shift_ok"))
        exp_ok, inv_ok = sem("exp_ok"), sem("inv_ok")
        pt_ok, probT_ok, pv_ok, head_ok = sem("pt_ok"), sem("probT_ok"), sem("pv_ok"), sem("head_ok")
        ht_ok, headT_ok, out_ok, res_ok, stat = sem("ht_ok"), sem("headT_ok"), sem("out_ok"), sem("res_ok"), sem("stat")
        block = ctx.enter_context(nc.Block())

        @block.sync
        def _(sp):
            if self_attn:
                sp.dma_start(wqkv[:, :, :], core.dram[pre + "w_qkv"].rearrange("(k p) o -> p k o", p=P)).then_inc(w_in, DMA)
                sp.dma_start(mask[:, 0, :], core.dram["mask_self"]).then_inc(mask_in, DMA)
            else:
                sp.dma_start(wqkv[:, :, 0:D], core.dram[pre + "w_q"].rearrange("(k p) o -> p k o", p=P)).then_inc(w_in, DMA)
                sp.dma_start(wqkv[:, :, D:3 * D], core.dram[pre + "w_kv"].rearrange("(k p) o -> p k o", p=P)).then_inc(w_in, DMA)
                sp.dma_start(mask[:, :, :], core.dram["mask_cross"].rearrange("b q k -> q b k")).then_inc(mask_in, DMA)
            sp.dma_start(wo[:, :, :], core.dram[w_out].rearrange("(k p) o -> p k o", p=P)).then_inc(wo_in, DMA)
            if not self_attn:
                def part_of_less(p, par):
                    if not isinstance(p, int) or p > 1:
                        wait(sp, masked_ok, (p - 1) * (2 * NHG))
                    sp.dma_start(less_pair[:, par, :, :], less[:, bass.ds(p * PAIR, PAIR), :]).then_inc(pair_ok[par], DMA)

                def body(p, par):
                    wait(sp, proj_ok, p * 4)
                    sp.dma_start(kv_in[:, :, :], core.cT[:, :, bass.ts(p, PT)]).then_inc(kv_ok, DMA)
                    if not (isinstance(p, int) and p == NP - 1):
                        part_of_less(p + 1, 1 - par)
                sp.wait_ge(less_ok, 1)
                part_of_less(0, 0)
                over_steps(sp, body)

        @block.gpsimd
        def _(gp):
            gp.wait_ge(mask_in, DMA)
            gp.tensor_scalar(less[:, :, :], mask[:, :, :], MASKED, -MASKED, ALU.mult, ALU.add).then_inc(less_ok, 1)
            gp.wait_ge(less_ok, 1)

            def body(p, par):
                if not self_attn:
                    gp.wait_ge(pair_ok[par], (p - par) * (DMA // 2) + DMA)
                for g in range(NHG):
                    for b in range(PAIR):
                        gp.wait_ge(kept_ok, p * (NHG * 2) + (g * 2 + 1 + b))
                        m = less[:, 0:1, :] if self_attn else less_pair[:, par, b:b + 1, :]
                        gp.tensor_tensor(prob[:, g % 2, b, :, :], prob[:, g % 2, b, :, :], m.to_broadcast([P, HG, P]),
                                         ALU.add).then_inc(masked_ok, 1)
            over_steps(gp, body)

        @block.tensor
        def _(pe):
            def ln_transpose(p):
                pe.wait_ge(hn_ok, p * PAIR + PAIR)
                wait(pe, v_ok, p)
                for k in range(KC):
                    for b in range(PAIR):
                        mm = pe.transpose(bank[1][:, k * PT + b * P:k * PT + (b + 1) * P], xn[:, b, k * P:(k + 1) * P], core.ident[:, :])
                mm.then_inc(lt_ok, 1)

            def project_tile(to, part, tile, moving):
                for k in range(KC):
                    mm = pe.matmul(to, wqkv[:, k, part * D + tile * P:part * D + (tile + 1) * P], moving(k), start=(k == 0), stop=(k == KC - 1))
                return mm

            def project_qk(p):
                q_in = lambda k: hT[:, k, :]
                k_in = q_in if self_attn else lambda k: core.cT[:, k, bass.ts(p, PT)]
                if isinstance(p, int) and p == 0:
                    pe.wait_ge(w_in, DMA if self_attn else 2 * DMA)
                pe.wait_ge(hT_ok, p + 1)
                wait(pe, k_ok, p)
                project_tile(bank[0][:, 0:PT], 0, 0, q_in).then_inc(proj_ok, 1)
                project_tile(bank[1][:, 0:PT], 0, 1, q_in).then_inc(proj_ok, 1)
                pe.wait_ge(q0_ok, p + 1)
                for t in range(KC):
                    mm = project_tile(bank[0][:, t * PT:(t + 1) * PT], 1, t, k_in)
                mm.then_inc(proj_ok, 1)

            def project_v(p):
                if not self_attn:
                    pe.wait_ge(kv_ok, p * DMA + DMA)
                pe.wait_ge(q1_ok, p + 1)
                for b in range(PAIR):
                    for k in range(KC):
                        mm = pe.matmul(bank[1][:, b * D:(b + 1) * D], kv_in[:, k, b * P:(b + 1) * P], wqkv[:, k, 2 * D:3 * D],
                                       start=(k == 0), stop=(k == KC - 1))
                mm.then_inc(proj_ok, 1)

            def scores(p, g):
                u = p * NHG + g
                if g == 0:
                    pe.wait_ge(k_ok, p + 1)
                    pe.wait_ge(q0_ok, p + 1)
                if g == NHG // 2:
                    pe.wait_ge(q1_ok, p + 1)
                for b in range(PAIR):
                    wait(pe, kept_ok, u * 2 - 1 + b)
                    for i in range(HG):
                        h = g * HG + i
                        mm = pe.matmul(bank[2 + b][:, i * P:(i + 1) * P], qT[:, h, b * P:(b + 1) * P],
                                       kT[:, h // TILE_HEADS, b * P:(b + 1) * P], start=True, stop=True)
                    mm.then_inc(score_ok, 1)

            def prob_transpose(u, par):
                for b in range(PAIR):
                    pe.wait_ge(exp_ok, u * 2 + 1 + b)
                    for i in range(HG):
                        mm = pe.transpose(bank[4 + b][:, i * P:(i + 1) * P], prob[:, par, b, i, :], core.ident[:, :])
                    mm.then_inc(pt_ok, 1)

            def weigh_values(p, g, u):
                if g == 0:
                    pe.wait_ge(v_ok, p + 1)
                    wait(pe, head_ok, p)
                pe.wait_ge(probT_ok, u * 2 + 2)
                for b in range(PAIR):
                    for i in range(HG):
                        h = g * HG + i
                        mm = pe.matmul(CTX[:, b * D + h * HD:b * D + (h + 1) * HD], probT[:, b, i, :], v[:, b, h * HD:(h + 1) * HD],
                                       start=True, stop=True)
                mm.then_inc(pv_ok, 1)

            def head_transpose(p):
                pe.wait_ge(head_ok, p + 1)
                for k in range(KC):
                    for b in range(PAIR):
                        mm = pe.transpose(OUT[:, k * PT + b * P:k * PT + (b + 1) * P], head[:, b, k * P:(k + 1) * P], core.ident[:, :])
                mm.then_inc(ht_ok, 1)

            def project_out(p):
                pe.wait_ge(headT_ok, p + 1)
                for b in range(PAIR):
                    for k in range(KC):
                        mm = pe.matmul(OUT[:, b * D:(b + 1) * D], headT[:, k, b * P:(b + 1) * P], wo[:, k, :], start=(k == 0), stop=(k == KC - 1))
                mm.then_inc(out_ok, 1)

            def body(p):
                first = isinstance(p, int) and p == 0
                last = isinstance(p, int) and p == NP - 1
                for g in range(NHG):
                    u = p * NHG + g
                    if g < NHG - 1:
                        scores(p, g + 1)
                    elif not last:
                        scores(p + 1, 0)
                    if g == 0 and not first:
                        head_transpose(p - 1)
                    if g == 1 and not last:
                        ln_transpose(p + 1)
                    if g == 2 and not last:
                        project_qk(p + 1)
                    prob_transpose(u, g % 2)
                    if g == 1 and not first:
                        project_out(p - 1)
                    weigh_values(p, g, u)
                    if g == NHG - 1 and not last:
                        project_v(p + 1)
                    if g == NHG - 1 and not first:
                        pe.wait_ge(res_ok, p * 2 - 1)

            ln_transpose(0)
            project_qk(0)
            project_v(0)
            scores(0, 0)
            pe.wait_ge(wo_in, DMA)
            over_pairs(pe, body)
            head_transpose(NP - 1)
            project_out(NP - 1)

        @block.scalar
        def _(act):
            def layer_norm(p):
                act.wait_ge(lt_ok, p + 1)
                for k in range(KC):
                    done = act.activation(hT[:, k, :], bank[1][:, k * PT:(k + 1) * PT], ACT.Identity,
                                          scale=core.col(ln_s, k), bias=core.col(ln_b, k))
                done.then_inc(hT_ok, 1)

            def spread_q0(p):
                act.wait_ge(proj_ok, p * 4 + 1)
                for h in range(TILE_HEADS):
                    done = act.activation(qT[:, h, :], bank[0][:, 0:PT], ACT.Identity, scale=core.head_rows[:, h:h + 1], bias=q_bias[:, h:h + 1])
                done.then_inc(q0_ok, 1)

            def copy_v(p):
                act.wait_ge(proj_ok, p * 4 + 4)
                act.activation(v[:, :, :], bank[1][:, :].rearrange("p (b d) -> p b d", b=PAIR), ACT.Copy).then_inc(v_ok, 1)

            def copy_head(p):
                act.wait_ge(ht_ok, p + 1)
                for k in range(KC):
                    done = act.activation(headT[:, k, :], OUT[:, k * PT:(k + 1) * PT], ACT.Identity, bias=core.col(bias_v[0], bias_v[1] + k))
                done.then_inc(headT_ok, 1)

            def body(p):
                first = isinstance(p, int) and p == 0
                last = isinstance(p, int) and p == NP - 1
                for g in range(NHG):
                    u = p * NHG + g
                    par = g % 2
                    act.wait_ge(shift_ok, u + 1)
                    for b in range(PAIR):
                        for i in range(HG):
                            done = act.activation(prob[:, par, b, i, :], prob[:, par, b, i, :], ACT.Exp, scale=SCALE,
                                                  bias=shift[:, par, b, i:i + 1], accum_out=total[:, b, g * HG + i:g * HG + i + 1])
                        done.then_inc(exp_ok, 1)
                    if g == 0 and not first:
                        copy_head(p - 1)
                    if g == 1 and not last:
                        layer_norm(p + 1)
                    if g == 2 and not last:
                        spread_q0(p + 1)
                    for b in range(PAIR):
                        act.wait_ge(pt_ok, u * 2 + 1 + b)
                        act.activation(probT[:, b, :, :], bank[4 + b][:, :].rearrange("p (h q) -> p h q", h=HG), ACT.Copy).then_inc(probT_ok, 1)
                    if g == NHG - 1 and not last:
                        copy_v(p + 1)

            rstd_scalar(core, act, root)
            act.wait_ge(q_bias_ok, 1)
            layer_norm(0)
            spread_q0(0)
            copy_v(0)
            over_pairs(act, body)
            copy_head(NP - 1)

        @block.vector
        def _(dve):
            def normalise(p):
                wait(dve, lt_ok, p)
                for b in range(PAIR):
                    i = p * PAIR + b
                    dve.tensor_scalar(xn[:, b, :], core.x[:, i, :], core.mv[:, i, 0:1], core.rstd[:, bass.ds(i, 1)],
                                      ALU.subtract, ALU.mult).then_inc(hn_ok, 1)

            def keep_scores(p, g, par):
                u = p * NHG + g
                for b in range(PAIR):
                    dve.wait_ge(score_ok, u * 2 + 1 + b)
                    wait(dve, pt_ok, u * 2 - 4 + 1 + b)
                    m = mask[:, 0:1, :] if self_attn else mask[:, bass.ds(p * PAIR + b, 1), :]
                    dve.tensor_tensor(prob[:, par, b, :, :], bank[2 + b][:, :].rearrange("p (h k) -> p h k", h=HG),
                                      m.to_broadcast([P, HG, P]), ALU.mult).then_inc(kept_ok, 1)

            def row_max(u, par):
                for b in range(PAIR):
                    dve.wait_ge(masked_ok, u * 2 + 1 + b)
                    dve.tensor_reduce(top[:, b, :], prob[:, par, b, :, :], AX_X, ALU.max).then_inc(top_ok, 1)
                dve.wait_ge(top_ok, u * 2 + 2)
                dve.tensor_scalar(shift[:, par, :, :], top[:, :, :], -SCALE, None, ALU.mult).then_inc(shift_ok, 1)

            def invert(u, g):
                dve.wait_ge(exp_ok, u * 2 + 2)
                dve.reciprocal(inv[:, :, g * HG:(g + 1) * HG], total[:, :, g * HG:(g + 1) * HG]).then_inc(inv_ok, 1)

            def spread_q1(p):
                dve.wait_ge(proj_ok, p * 4 + 2)
                for h in range(TILE_HEADS):
                    done = dve.tensor_scalar(qT[:, TILE_HEADS + h, :], bank[1][:, 0:PT], core.col(bias_q[0], bias_q[1] + 1),
                                             core.head_rows[:, h:h + 1], ALU.add, ALU.mult)
                done.then_inc(q1_ok, 1)

            def copy_k(p):
                dve.wait_ge(proj_ok, p * 4 + 3)
                dve.tensor_tensor(kT[:, :, :], bank[0][:, :].rearrange("p (k t) -> p k t", k=KC),
                                  core.col(bias_k[0], bias_k[1], KC)[:, :, None].to_broadcast([P, KC, PT]), ALU.add).then_inc(k_ok, 1)

            def divide(p):
                dve.wait_ge(pv_ok, p * NHG + NHG)
                dve.wait_ge(inv_ok, p * NHG + NHG)
                wait(dve, ht_ok, p)
                dve.tensor_tensor(head[:, :, :].rearrange("p b (h d) -> p (b h) d", d=HD),
                                  CTX[:, :].rearrange("p (n d) -> p n d", d=HD),
                                  inv[:, :, :].rearrange("p b h -> p (b h)")[:, :, None].to_broadcast([P, PAIR * H, HD]), ALU.mult).then_inc(head_ok, 1)

            def body(p):
                first = isinstance(p, int) and p == 0
                last = isinstance(p, int) and p == NP - 1
                for g in range(NHG):
                    u = p * NHG + g
                    more = not (last and g == NHG - 1)
                    par1 = (g + 1) % 2
                    if more:
                        if g < NHG - 1:
                            keep_scores(p, g + 1, par1)
                        else:
                            keep_scores(p + 1, 0, par1)
                    if g == 0 and not first:
                        invert(p * NHG - 1, NHG - 1)
                        divide(p - 1)
                    if g > 0:
                        invert(u - 1, g - 1)
                    if more:
                        row_max(u + 1, par1)
                    if g == 0 and not last:
                        normalise(p + 1)
                    if g == 2 and not first:
                        new_rows(core, dve, res_ok, stat, p - 1, OUT[:, :].rearrange("p (b d) -> p b d", b=PAIR), out_ok, core.row(out_bias))
                    if g == 2 and not last:
                        spread_q1(p + 1)
                        copy_k(p + 1)

            rstd_vector(core, dve, root, rstep)
            normalise(0)
            dve.tensor_scalar(q_bias[:, :], core.head_rows2[:, :], 1.0, None, ALU.mult).then_inc(rstep, 1)
            dve.wait_ge(rstep, 6)
            for t in range(KC):
                done = dve.tensor_scalar(q_bias[:, t * TILE_HEADS:(t + 1) * TILE_HEADS], q_bias[:, t * TILE_HEADS:(t + 1) * TILE_HEADS],
                                         core.col(bias_q[0], bias_q[1] + t), None, ALU.mult)
            done.then_inc(q_bias_ok, 1)
            dve.wait_ge(mask_in, DMA)
            spread_q1(0)
            copy_k(0)
            keep_scores(0, 0, 0)
            row_max(0, 0)
            over_pairs(dve, body)
            invert(NP * NHG - 1, NHG - 1)
            divide(NP - 1)
            new_rows(core, dve, res_ok, stat, NP - 1, OUT[:, :].rearrange("p (b d) -> p b d", b=PAIR), out_ok, core.row(out_bias))


def mlp(core, pre, ln_s, ln_b, w1_name, b1_name, w2_name, b2_name, gelu):
    nc = core.nc
    NF = 4 * D // P
    with ExitStack() as ctx:
        sb = lambda name, shape: ctx.enter_context(nc.sbuf_tensor(f"m{pre}{name}", shape, F32))
        sem = Signals(core, ctx, f"m{pre}")
        w1 = sb("w1", [P, KC, 4 * D])
        w2 = sb("w2", [P, NF, D])
        xn = sb("xn", [P, PAIR, D])
        hT = sb("hT", [P, KC, PT])
        gT = sb("gT", [P, 2, NF, PT])
        bank = core.bank
        w1_in, w2_in, root, rstep = sem("w1_in"), sem("w2_in"), sem("root"), sem("rstep")
        hn_ok, lt_ok, hT_ok = sem("hn_ok"), sem("lt_ok"), sem("hT_ok")
        up_ok, gelu_ok, out_ok, res_ok, stat = sem("up_ok"), sem("gelu_ok"), sem("out_ok"), sem("res_ok"), sem("stat")
        block = ctx.enter_context(nc.Block())

        def within(p, ahead):
            return not isinstance(p, int) or p + ahead < NP

        @block.sync
        def _(sp):
            sp.dma_start(w1[:, :, :], core.dram[pre + w1_name].rearrange("(k p) o -> p k o", p=P)).then_inc(w1_in, DMA)
            sp.dma_start(w2[:, :, :], core.dram[pre + w2_name].rearrange("(f p) o -> p f o", p=P)).then_inc(w2_in, DMA)

        @block.tensor
        def _(pe):
            def ln_transpose(p):
                pe.wait_ge(hn_ok, p * PAIR + PAIR)
                wait(pe, hT_ok, p)
                for k in range(KC):
                    for b in range(PAIR):
                        mm = pe.transpose(bank[6][:, k * PT + b * P:k * PT + (b + 1) * P], xn[:, b, k * P:(k + 1) * P], core.ident[:, :])
                mm.then_inc(lt_ok, 1)

            def up(p):
                pe.wait_ge(hT_ok, p + 1)
                for f in range(NF):
                    if f % 2 == 0:
                        wait(pe, gelu_ok, (p - 1) * NF + f + 2)
                    at = bank[f // 2][:, (f % 2) * PT:(f % 2 + 1) * PT]
                    for k in range(KC):
                        mm = pe.matmul(at, w1[:, k, f * P:(f + 1) * P], hT[:, k, :], start=(k == 0), stop=(k == KC - 1))
                    if f % 2:
                        mm.then_inc(up_ok, 1)

            def down(p, par):
                pe.wait_ge(gelu_ok, p * NF + NF)
                wait(pe, res_ok, p * 2 - 3)
                for b in range(PAIR):
                    for f in range(NF):
                        mm = pe.matmul(bank[4 + par][:, b * D:(b + 1) * D], gT[:, par, f, b * P:(b + 1) * P], w2[:, f, :],
                                       start=(f == 0), stop=(f == NF - 1))
                mm.then_inc(out_ok, 1)

            def body(p, par):
                if within(p, 1):
                    up(p + 1)
                if within(p, 2):
                    ln_transpose(p + 2)
                if isinstance(p, int) and p == 0:
                    pe.wait_ge(w2_in, DMA)
                down(p, par)

            ln_transpose(0)
            pe.wait_ge(w1_in, DMA)
            up(0)
            ln_transpose(1)
            over_steps(pe, body)

        @block.scalar
        def _(act):
            def layer_norm(p):
                act.wait_ge(lt_ok, p + 1)
                for k in range(KC):
                    done = act.activation(hT[:, k, :], bank[6][:, k * PT:(k + 1) * PT], ACT.Identity,
                                          scale=core.col(pre + ln_s, k), bias=core.col(pre + ln_b, k))
                done.then_inc(hT_ok, 1)

            def activate(p, par):
                for f in range(NF):
                    if f % 2 == 0:
                        act.wait_ge(up_ok, p * (NF // 2) + f // 2 + 1)
                    act.activation(gT[:, par, f, :], bank[f // 2][:, (f % 2) * PT:(f % 2 + 1) * PT], gelu,
                                   bias=core.col(pre + b1_name, f)).then_inc(gelu_ok, 1)

            def body(p, par):
                if within(p, 1):
                    activate(p + 1, 1 - par)
                if within(p, 2):
                    layer_norm(p + 2)

            rstd_scalar(core, act, root)
            layer_norm(0)
            activate(0, 0)
            layer_norm(1)
            over_steps(act, body)

        @block.vector
        def _(dve):
            def normalise(p):
                wait(dve, lt_ok, p)
                for b in range(PAIR):
                    i = p * PAIR + b
                    dve.tensor_scalar(xn[:, b, :], core.x[:, i, :], core.mv[:, i, 0:1], core.rstd[:, bass.ds(i, 1)],
                                      ALU.subtract, ALU.mult).then_inc(hn_ok, 1)

            def body(p, par):
                if within(p, 2):
                    normalise(p + 2)
                new_rows(core, dve, res_ok, stat, p, bank[4 + par][:, :].rearrange("p (b d) -> p b d", b=PAIR), out_ok, core.row(pre + b2_name))

            rstd_vector(core, dve, root, rstep)
            normalise(0)
            normalise(1)
            over_steps(dve, body)


def single_attention(core):
    nc = core.nc
    SCALE = float(D) ** -0.5
    pre = "L2_xattn_"
    with ExitStack() as ctx:
        sb = lambda name, shape: ctx.enter_context(nc.sbuf_tensor(f"s_{name}", shape, F32))
        sem = Signals(core, ctx, f"s_")
        wq, wk, wv, wo = (sb(w, [P, KC, D]) for w in ("wq", "wk", "wv", "wo"))
        alpha = sb("alpha", [P, 1])
        x_in = sb("x_in", [P, PAIR, D])
        xT, kv_in, qT, kT = (sb(t, [P, KC, PT]) for t in ("xT", "kv_in", "qT", "kT"))
        v = sb("v", [P, PAIR, D])
        prob, probT = sb("prob", [P, PAIR, P]), sb("probT", [P, PAIR, P])
        headT = sb("headT", [P, KC, PT])
        scaled = sb("scaled", [P, PAIR, D])
        top, shift, total, inv = (sb(t, [P, PAIR]) for t in ("top", "shift", "total", "inv"))
        bank = core.bank
        w_in, consts = sem("w_in"), sem("consts")
        xi_ok, xt_ok, xT_ok, kv_ok = sem("xi_ok"), sem("xt_ok"), sem("xT_ok"), sem("kv_ok")
        q_ready, k_ready, v_ready = sem("q_ready"), sem("k_ready"), sem("v_ready")
        q_ok, k_ok, v_ok = sem("q_ok"), sem("k_ok"), sem("v_ok")
        score_ok, top_ok, shift_ok, exp_ok, inv_ok, prob_ok = (sem(s) for s in ("score", "top_ok", "shift_ok", "exp", "inv_ok", "prob_ok"))
        pt_ok, probT_ok, pv_ok, headT_ok, out_ok = (sem(s) for s in ("pt", "probT_ok", "pv", "headT_ok", "out"))
        scaled_ok, res_ok, stat = sem("scaled_ok"), sem("res_ok"), sem("stat")
        block = ctx.enter_context(nc.Block())
        halves = lambda t, n: t[:, :].rearrange("p (k t) -> p k t", k=n)

        @block.sync
        def _(sp):
            for tile, w in ((wq, "w_q"), (wk, "w_k"), (wv, "w_v"), (wo, "w_o")):
                sp.dma_start(tile[:, :, :], core.dram[pre + w].rearrange("(k p) o -> p k o", p=P)).then_inc(w_in, DMA)
            sp.dma_start(alpha[:, :], core.dram["alpha"]).then_inc(consts, DMA)

            def body(p):
                wait(sp, v_ready, p)
                sp.dma_start(kv_in[:, :, :], core.cT[:, :, bass.ts(p, PT)]).then_inc(kv_ok, DMA)
            over_pairs(sp, body)

        @block.tensor
        def _(pe):
            def x_transpose(p):
                pe.wait_ge(xi_ok, p + 1)
                wait(pe, xT_ok, p)
                for k in range(KC):
                    for b in range(PAIR):
                        mm = pe.transpose(bank[0][:, k * PT + b * P:k * PT + (b + 1) * P], x_in[:, b, k * P:(k + 1) * P], core.ident[:, :])
                mm.then_inc(xt_ok, 1)

            def project(p, to, w, moving, ready):
                for t in range(KC):
                    for k in range(KC):
                        mm = pe.matmul(to[:, t * PT:(t + 1) * PT], w[:, k, t * P:(t + 1) * P], moving(k), start=(k == 0), stop=(k == KC - 1))
                mm.then_inc(ready, 1)

            def project_qk(p):
                pe.wait_ge(xT_ok, p + 1)
                wait(pe, q_ok, p)
                project(p, bank[1], wq, lambda k: xT[:, k, :], q_ready)
                wait(pe, k_ok, p)
                project(p, bank[2], wk, lambda k: core.cT[:, k, bass.ts(p, PT)], k_ready)

            def project_v(p):
                pe.wait_ge(kv_ok, p * DMA + DMA)
                wait(pe, v_ok, p)
                for b in range(PAIR):
                    for k in range(KC):
                        mm = pe.matmul(bank[3][:, b * D:(b + 1) * D], kv_in[:, k, b * P:(b + 1) * P], wv[:, k, :], start=(k == 0), stop=(k == KC - 1))
                mm.then_inc(v_ready, 1)

            def scores(p):
                pe.wait_ge(q_ok, p + 1)
                pe.wait_ge(k_ok, p + 1)
                wait(pe, exp_ok, p)
                for b in range(PAIR):
                    for k in range(KC):
                        mm = pe.matmul(bank[4][:, b * P:(b + 1) * P], qT[:, k, b * P:(b + 1) * P], kT[:, k, b * P:(b + 1) * P],
                                       start=(k == 0), stop=(k == KC - 1))
                mm.then_inc(score_ok, 1)

            def attend(p):
                pe.wait_ge(prob_ok, p + 1)
                for b in range(PAIR):
                    mm = pe.transpose(bank[5][:, b * P:(b + 1) * P], prob[:, b, :], core.ident[:, :])
                mm.then_inc(pt_ok, 1)
                pe.wait_ge(probT_ok, p + 1)
                pe.wait_ge(v_ok, p + 1)
                wait(pe, headT_ok, p)
                for k in range(KC):
                    for b in range(PAIR):
                        mm = pe.matmul(bank[6][:, k * PT + b * P:k * PT + (b + 1) * P], v[:, b, k * P:(k + 1) * P], probT[:, b, :], start=True, stop=True)
                mm.then_inc(pv_ok, 1)

            def project_out(p):
                pe.wait_ge(headT_ok, p + 1)
                wait(pe, scaled_ok, p)
                for b in range(PAIR):
                    for k in range(KC):
                        mm = pe.matmul(bank[7][:, b * D:(b + 1) * D], headT[:, k, b * P:(b + 1) * P], wo[:, k, :], start=(k == 0), stop=(k == KC - 1))
                mm.then_inc(out_ok, 1)

            def body(p):
                last = isinstance(p, int) and p == NP - 1
                if not last:
                    x_transpose(p + 1)
                scores(p)
                if not last:
                    project_qk(p + 1)
                attend(p)
                if not last:
                    project_v(p + 1)
                project_out(p)

            x_transpose(0)
            pe.wait_ge(w_in, 4 * DMA)
            project_qk(0)
            project_v(0)
            over_pairs(pe, body)

        @block.scalar
        def _(act):
            def copy_x(p):
                act.wait_ge(xt_ok, p + 1)
                act.activation(xT[:, :, :], halves(bank[0], KC), ACT.Copy).then_inc(xT_ok, 1)

            def copy_v(p):
                act.wait_ge(v_ready, p + 1)
                act.activation(v[:, :, :], halves(bank[3], PAIR), ACT.Copy).then_inc(v_ok, 1)

            def body(p):
                last = isinstance(p, int) and p == NP - 1
                if not last:
                    copy_x(p + 1)
                act.wait_ge(shift_ok, p + 1)
                for b in range(PAIR):
                    done = act.activation(prob[:, b, :], bank[4][:, b * P:(b + 1) * P], ACT.Exp, scale=SCALE, bias=shift[:, b:b + 1],
                                          accum_out=total[:, b:b + 1])
                done.then_inc(exp_ok, 1)
                act.wait_ge(pt_ok, p + 1)
                act.activation(probT[:, :, :], bank[5][:, 0:PT].rearrange("p (b t) -> p b t", b=PAIR), ACT.Copy).then_inc(probT_ok, 1)
                if not last:
                    copy_v(p + 1)

            copy_x(0)
            copy_v(0)
            over_pairs(act, body)

        @block.vector
        def _(dve):
            def fetch(p):
                wait(dve, xt_ok, p)
                dve.tensor_scalar(x_in[:, :, :], core.x[:, bass.ds(p * PAIR, PAIR), :], 1.0, None, ALU.mult).then_inc(xi_ok, 1)

            def copy_qk(p):
                dve.wait_ge(q_ready, p + 1)
                dve.tensor_copy(qT[:, :, :], halves(bank[1], KC)).then_inc(q_ok, 1)
                dve.wait_ge(k_ready, p + 1)
                dve.tensor_copy(kT[:, :, :], halves(bank[2], KC)).then_inc(k_ok, 1)

            def body(p):
                last = isinstance(p, int) and p == NP - 1
                if not last:
                    fetch(p + 1)
                dve.wait_ge(score_ok, p + 1)
                dve.tensor_reduce(top[:, :], bank[4][:, 0:PT].rearrange("p (b t) -> p b t", b=PAIR), AX_X, ALU.max).then_inc(top_ok, 1)
                dve.wait_ge(top_ok, p + 1)
                dve.tensor_scalar(shift[:, :], top[:, :], -SCALE, None, ALU.mult).then_inc(shift_ok, 1)
                if not last:
                    copy_qk(p + 1)
                dve.wait_ge(exp_ok, p + 1)
                dve.reciprocal(inv[:, :], total[:, :]).then_inc(inv_ok, 1)
                dve.wait_ge(inv_ok, p + 1)
                dve.tensor_tensor(prob[:, :, :], prob[:, :, :], inv[:, :, None].to_broadcast([P, PAIR, P]), ALU.mult).then_inc(prob_ok, 1)
                dve.wait_ge(pv_ok, p + 1)
                dve.tensor_copy(headT[:, :, :], halves(bank[6], KC)).then_inc(headT_ok, 1)
                dve.wait_ge(out_ok, p + 1)
                dve.tensor_scalar(scaled[:, :, :], halves(bank[7], PAIR), alpha[:, 0:1], None, ALU.mult).then_inc(scaled_ok, 1)
                new_rows(core, dve, res_ok, stat, p, scaled[:, :, :], scaled_ok)

            fetch(0)
            dve.wait_ge(consts, DMA)
            copy_qk(0)
            over_pairs(dve, body)


def recurrence(core):
    nc = core.nc
    J = 8
    HT = P // J
    F = 5
    FK, FW, FV, FR, FG = range(F)
    R = 32
    RD = 64
    UNITS = KC * PAIR
    pre = "L3_xattn_"
    with ExitStack() as ctx:
        sb = lambda name, shape: ctx.enter_context(nc.sbuf_tensor(f"r_{name}", shape, F32))
        sem = Signals(core, ctx, f"r_")
        maa_w1 = sb("maa_w1", [P, KC, F * R])
        maa_w2 = sb("maa_w2", [P, D])
        maa_w2g = sb("maa_w2g", [R, D])
        td_w1, td_w2 = sb("td_w1", [P, KC, RD]), sb("td_w2", [RD, D])
        w = {n: sb(n, [P, KC, D]) for n in ("Wk", "Wv", "Wr", "Wg", "Wo", "Wfk", "Wfr", "Wfv")}
        state0 = sb("state0", [P, KC, NB, J])
        pick = sb("pick", [P, J, P])
        head_sum = sb("head_sum", [P, HT])
        xn = sb("xn", [P, PAIR, D])
        xa = sb("xa", [P, KC, PAIR, P + 1])
        sx = sb("sx", [P, KC, PAIR, P])
        xmaa = sb("xmaa", [P, KC, PAIR, P])
        low, low_g = sb("low", [P, PT]), sb("low_g", [R, PT])
        mixed = sb("mixed", [P, F, KC, PT])
        td_low = sb("td_low", [RD, PT])
        kT, vT, rT = (sb(n, [P, 2, KC, PT]) for n in ("kT", "vT", "rT"))
        rate = sb("rate", [P, 2, KC, PT])
        g_tanh = sb("g_tanh", [P, PAIR, D])
        gate = sb("gate", [P, 2, PAIR, D])
        decay = sb("decay", [P, 2, J, P + 1])
        kv = sb("kv", [P, J, P + 1])
        states = sb("states", [P, J, P + 1])
        prod = sb("prod", [P, 2, J, P])
        og = sb("og", [P, UNITS, HT, J])
        sq = sb("sq", [P, UNITS, HT, J])
        msum, mean, vsum, gstd, grstd = (sb(n, [P, UNITS * HT]) for n in ("msum", "mean", "vsum", "gstd", "grstd"))
        zT = sb("zT", [P, KC, PT])
        std2, rstd2 = sb("std2", [P, PAIR]), sb("rstd2", [P, PAIR])
        xn2 = sb("xn2", [P, PAIR, D])
        xc = sb("xc", [P, KC, PAIR, P + 1])
        sx2 = sb("sx2", [P, KC, PAIR, P])
        xk2, xr2 = sb("xk2", [P, KC, PT]), sb("xr2", [P, KC, PT])
        relu, kkT = sb("relu", [P, KC, PT]), sb("kkT", [P, KC, PT])
        r_tanh = sb("r_tanh", [P, PAIR, D])
        gated = sb("gated", [P, PAIR, D])
        result = sb("result", [P, PAIR, D])
        bank = core.bank
        VB = core.banks[:, 0:2, :].rearrange("p n c -> p (n c)").rearrange("p (j t) -> p j t", j=J)
        OG = bank[2]

        w1_in, wp_in, w2_in, s0_in = sem("w1_in"), sem("wp_in"), sem("w2_in"), sem("s0_in")
        root, rstep, made = sem("root"), sem("rstep"), sem("made")
        TILES = ["xa", "low", "td", "k", "r", "v", "rate", "g", "z", "out", "xc", "kk", "rr", "ff"]
        ready = {n: sem(n + "_ready") for n in TILES}
        read = {n: sem(n + "_read") for n in TILES}
        f_ready, f_read = sem("f_ready"), sem("f_read")
        xn_ok, first_ok, xmaa_ok, mix_ok = sem("xn_ok"), sem("first_ok"), sem("xmaa_ok"), sem("mix_ok")
        mid_ok = sem("mid_ok")
        vb_ready, kv_ok, decay_ok, scan_ok, q_ok, prod_ok, sum_ready = (sem(n) for n in ("vb", "kv_ok", "decay_ok", "scan_ok", "q_ok", "prod_ok", "sum"))
        og_read, gn_step, vsum_ok, gstd_ok, z_ok = sem("og_read"), sem("gn_step"), sem("vsum_ok"), sem("gstd_ok"), sem("z_ok")
        st_ok, mv2_ok, std2_ok, c_step, xn2_ok, c_first = sem("st_ok"), sem("mv2_ok"), sem("std2_ok"), sem("c_step"), sem("xn2_ok"), sem("c_first")
        xk_step, xk_ok, relu_ok, ff_step, result_ok, stored = (sem(n) for n in ("xk_step", "xk_ok", "relu_ok", "ff_step", "result_ok", "stored"))
        g_tanh_ok = sem("g_tanh_ok")
        block = ctx.enter_context(nc.Block())
        ctx_rows = core.cT[:, :, :].rearrange("p k (b t) -> p k b t", b=NB)

        def static(p):
            return isinstance(p, int)

        def exists(p):
            return not static(p) or 0 <= p < NP

        def over_slots(eng, slot):
            over_steps(eng, slot)
            slot(NP, NP % 2)

        flat = lambda t: t.rearrange("p k b t -> p k (b t)")
        halves = lambda t, n=2: t[:, :].rearrange("p (k t) -> p k t", k=n)

        @block.sync
        def _(sp):
            sp.dma_start(maa_w1[:, :, :], core.dram[pre + "maa_w1"].rearrange("(k p) o -> p k o", p=P)).then_inc(w1_in, DMA)
            sp.dma_start(maa_w2[:, :], core.dram["maa_w2"][0:P, :]).then_inc(w1_in, DMA)
            sp.dma_start(maa_w2g[:, :], core.dram["maa_w2"][P:F * R, :]).then_inc(w1_in, DMA)
            sp.dma_start(td_w1[:, :, :], core.dram[pre + "td_w1"].rearrange("(k p) o -> p k o", p=P)).then_inc(wp_in, DMA)
            sp.dma_start(td_w2[:, :], core.dram[pre + "td_w2"]).then_inc(wp_in, DMA)
            for n in ("Wk", "Wv", "Wr", "Wg"):
                sp.dma_start(w[n][:, :, :], core.dram[pre + n].rearrange("(k p) o -> p k o", p=P)).then_inc(wp_in, DMA)
            sp.dma_start(state0[:, :, :, :], core.dram["state0"]).then_inc(s0_in, DMA)
            for n in ("Wo", "Wfk", "Wfr", "Wfv"):
                sp.dma_start(w[n][:, :, :], core.dram[pre + n].rearrange("(k p) o -> p k o", p=P)).then_inc(w2_in, DMA)

            def slot(p, par):
                if exists(p - 1):
                    sp.wait_ge(result_ok, p)
                    sp.dma_start(core.out[bass.ds((p - 1) * PAIR, PAIR), :, :].rearrange("b t d -> t b d"), result[:, :, :]).then_inc(stored, DMA)
            over_slots(sp, slot)
            sp.wait_ge(stored, NP * DMA)

        @block.gpsimd
        def _(gp):
            gp.memset(pick[:, :, :], 0.0).then_inc(made, 1)
            gp.memset(head_sum[:, :], 1.0).then_inc(made, 1)
            gp.memset(decay[:, :, :, :], 0.0).then_inc(made, 1)
            gp.wait_ge(made, 3)
            gp.affine_select(out=pick[:, :, :].rearrange("p j (h i) -> p j h i", i=J), in_=pick[:, :, :].rearrange("p j (h i) -> p j h i", i=J),
                             compare_op=ALU.not_equal, fill=1.0, base=0, pattern=[[-1, J], [-J, HT], [0, J]], channel_multiplier=1).then_inc(made, 1)
            gp.affine_select(out=head_sum[:, :], in_=head_sum[:, :], compare_op=ALU.is_ge, fill=0.0,
                             base=0, pattern=[[-J, HT]], channel_multiplier=1).then_inc(made, 1)
            gp.wait_ge(made, 5)
            gp.affine_select(out=head_sum[:, :], in_=head_sum[:, :], compare_op=ALU.is_ge, fill=0.0,
                             base=J - 1, pattern=[[J, HT]], channel_multiplier=-1).then_inc(made, 1)

            def times_r(p, par, s):
                k, b = s // PAIR, s % PAIR
                gp.wait_ge(read["r"], p + 1)
                gp.wait_ge(q_ok, p * UNITS + (s + 1))
                gp.tensor_tensor(prod[:, s % 2, :, :], prod[:, s % 2, :, :],
                                 rT[:, par, k, b * P:(b + 1) * P][:, None, :].to_broadcast([P, J, P]), ALU.mult).then_inc(prod_ok, 1)

            def add_xa(a):
                for f in range(F):
                    gp.wait_ge(f_read, a * F + (f + 1))
                    gp.tensor_tensor(mixed[:, f, :, :].rearrange("p k (b t) -> p k b t", b=PAIR), mixed[:, f, :, :].rearrange("p k (b t) -> p k b t", b=PAIR),
                                     xa[:, :, :, 1:P + 1], ALU.add).then_inc(mix_ok, 1)

            def slot(p, par):
                for s in range(UNITS):
                    if exists(p):
                        if s == UNITS - 1 and exists(p + 1):
                            add_xa(p + 1)
                        times_r(p, par, s)
            add_xa(0)
            over_steps(gp, slot)

        @block.tensor
        def _(pe):
            def spread_v(p, par, s):
                k, b = s // PAIR, s % PAIR
                pe.wait_ge(read["v"], p + 1)
                if not (static(p) and p == 0 and s == 0):
                    pe.wait_ge(kv_ok, p * (2 * UNITS) + (2 * s - 1))
                for j in range(J):
                    mm = pe.matmul(VB[:, j, :], pick[:, j, :], vT[:, par, k, b * P:(b + 1) * P], start=True, stop=True)
                mm.then_inc(vb_ready, 1)

            def sum_heads(p, s):
                pe.wait_ge(prod_ok, p * UNITS + (s + 1))
                if s == 0:
                    wait(pe, og_read, p)
                b, k = s % PAIR, s // PAIR
                for j in range(J):
                    at = (b * KC + k) * P + j * HT
                    mm = pe.matmul(OG[:, at:at + HT], prod[:, s % 2, j, :], head_sum[:, :], start=True, stop=True)
                mm.then_inc(sum_ready, 1)

            def transposes(to, src):
                for k in range(KC):
                    for b in range(PAIR):
                        mm = pe.transpose(to[:, k * PT + b * P:k * PT + (b + 1) * P], src[:, b, k * P:(k + 1) * P], core.ident[:, :])
                return mm

            def feature_major(to, weight, moving):
                for t in range(KC):
                    for k in range(KC):
                        mm = pe.matmul(to[:, t * PT:(t + 1) * PT], weight[:, k, t * P:(t + 1) * P], moving[:, k, :], start=(k == 0), stop=(k == KC - 1))
                return mm

            def token_major(to, source, weight):
                for b in range(PAIR):
                    for k in range(KC):
                        mm = pe.matmul(to[:, b * D:(b + 1) * D], source[:, k, b * P:(b + 1) * P], weight[:, k, :], start=(k == 0), stop=(k == KC - 1))
                return mm

            def a_transpose(a):
                pe.wait_ge(xn_ok, a * PAIR + PAIR)
                wait(pe, read["v"], a)
                transposes(bank[3], xn).then_inc(ready["xa"], 1)

            def a_low(a):
                pe.wait_ge(xmaa_ok, a * KC + KC)
                pe.wait_ge(read["xa"], a + 1)
                for m0, m1 in ((0, P), (P, F * R)):
                    at = 0 if m0 == 0 else PT
                    for k in range(KC):
                        mm = pe.matmul(bank[3][0:m1 - m0, at:at + PT], maa_w1[:, k, m0:m1], flat(xmaa[:, :, :, :])[:, k, :], start=(k == 0), stop=(k == KC - 1))
                mm.then_inc(ready["low"], 1)

            def a_mix(a):
                pe.wait_ge(read["low"], a + 1)
                for f in range(F):
                    if f == 0:
                        wait(pe, read["g"], a)
                    elif f == 1:
                        wait(pe, read["rate"], a)
                    else:
                        pe.wait_ge(f_read, a * F + (f - 1))
                    r0 = R * f if f < FG else 0
                    src, rhs = (maa_w2, low) if f < FG else (maa_w2g, low_g)
                    for k in range(KC):
                        mm = pe.matmul(bank[4 + f % 2][:, k * PT:(k + 1) * PT], src[r0:r0 + R, k * P:(k + 1) * P], rhs[r0:r0 + R, :], start=True, stop=True)
                    mm.then_inc(f_ready, 1)

            def a_project(a):
                pe.wait_ge(mix_ok, a * F + FW + 1)
                for k in range(KC):
                    mm = pe.matmul(bank[3][0:RD, 0:PT], td_w1[:, k, :], mixed[:, FW, k, :], start=(k == 0), stop=(k == KC - 1))
                mm.then_inc(ready["td"], 1)
                pe.wait_ge(f_read, a * F + F)
                feature_major(bank[5], w["Wk"], mixed[:, FK, :, :]).then_inc(ready["k"], 1)
                pe.wait_ge(mix_ok, a * F + FR + 1)
                feature_major(bank[4], w["Wr"], mixed[:, FR, :, :]).then_inc(ready["r"], 1)
                pe.wait_ge(read["td"], a + 1)
                feature_major(bank[3], w["Wv"], mixed[:, FV, :, :]).then_inc(ready["v"], 1)
                pe.wait_ge(read["k"], a + 1)
                for t in range(KC):
                    mm = pe.matmul(bank[5][:, t * PT:(t + 1) * PT], td_w2[:, t * P:(t + 1) * P], td_low[:, :], start=True, stop=True)
                mm.then_inc(ready["rate"], 1)
                pe.wait_ge(read["r"], a + 1)
                pe.wait_ge(mix_ok, a * F + FG + 1)
                token_major(bank[4], mixed[:, FG, :, :], w["Wg"]).then_inc(ready["g"], 1)

            def slot(p, par):
                u, a, c = exists(p), exists(p + 1), exists(p - 1)
                if u:
                    spread_v(p, par, 0)
                if c:
                    pe.wait_ge(z_ok, p)
                    if not static(p) or p > 1:
                        pe.wait_ge(read["rr"], p - 1)
                    transposes(bank[6], og[:, :, :, :].rearrange("p (b k) h j -> p b (k h j)", b=PAIR)).then_inc(ready["z"], 1)
                    pe.wait_ge(read["z"], p)
                    if not static(p) or p > 1:
                        pe.wait_ge(read["ff"], p - 1)
                    token_major(bank[7], zT, w["Wo"]).then_inc(ready["out"], 1)
                if u:
                    spread_v(p, par, 1)
                if a:
                    a_transpose(p + 1)
                if u:
                    sum_heads(p, 0)
                    spread_v(p, par, 2)
                if a:
                    a_low(p + 1)
                if u:
                    sum_heads(p, 1)
                if c:
                    pe.wait_ge(xn2_ok, p * PAIR)
                    transposes(bank[6], xn2).then_inc(ready["xc"], 1)
                if u:
                    spread_v(p, par, 3)
                if a:
                    a_mix(p + 1)
                if u:
                    sum_heads(p, 2)
                if c:
                    pe.wait_ge(xk_ok, p * (2 * KC))
                    pe.wait_ge(read["out"], p)
                    feature_major(bank[7], w["Wfk"], xk2).then_inc(ready["kk"], 1)
                    pe.wait_ge(read["xc"], p)
                    token_major(bank[6], xr2, w["Wfr"]).then_inc(ready["rr"], 1)
                if a:
                    a_project(p + 1)
                if u:
                    sum_heads(p, 3)
                if c:
                    pe.wait_ge(read["kk"], p)
                    token_major(bank[7], kkT, w["Wfv"]).then_inc(ready["ff"], 1)

            pe.wait_ge(w1_in, 3 * DMA)
            a_transpose(0)
            a_low(0)
            a_mix(0)
            pe.wait_ge(wp_in, 6 * DMA)
            a_project(0)
            pe.wait_ge(made, 6)
            pe.wait_ge(w2_in, 4 * DMA)
            over_slots(pe, slot)

        @block.scalar
        def _(act):
            def copy_xa(a):
                act.wait_ge(ready["xa"], a + 1)
                wait(act, mix_ok, a * F)
                for k in range(KC):
                    done = act.activation(xa[:, k, :, 1:P + 1], halves(bank[3])[:, k, :].rearrange("p (b t) -> p b t", b=PAIR), ACT.Identity,
                                          scale=core.col(pre + "ln1_w", k), bias=core.col(pre + "ln1_b", k))
                done.then_inc(read["xa"], 1)

            def tanh_low(a):
                act.wait_ge(ready["low"], a + 1)
                act.activation(low[:, :], bank[3][:, 0:PT], ACT.Tanh)
                act.activation(low_g[:, :], bank[3][0:R, PT:2 * PT], ACT.Tanh).then_inc(read["low"], 1)

            def projections(a, par):
                act.wait_ge(ready["td"], a + 1)
                act.activation(td_low[:, :], bank[3][0:RD, 0:PT], ACT.Tanh).then_inc(read["td"], 1)
                act.wait_ge(ready["r"], a + 1)
                act.activation(rT[:, par, :, :], halves(bank[4]), ACT.Copy).then_inc(read["r"], 1)
                act.wait_ge(ready["rate"], a + 1)
                for t in range(KC):
                    done = act.activation(rate[:, par, t, :], bank[5][:, t * PT:(t + 1) * PT], ACT.Exp, bias=core.col(pre + "time_decay", t))
                done.then_inc(read["rate"], 1)
                act.wait_ge(ready["g"], a + 1)
                wait(act, read["g"], a)
                act.activation(g_tanh[:, :, :], halves(bank[4]), ACT.Tanh, scale=0.5).then_inc(g_tanh_ok, 1)

            def make_decay(p, par, s):
                k, b = s // PAIR, s % PAIR
                if not (static(p) and p == 0 and s < 2):
                    act.wait_ge(scan_ok, p * UNITS + (s - 1))
                if s == 0:
                    act.wait_ge(read["rate"], p + 1)
                act.activation(decay[:, s % 2, :, 1:P + 1], rate[:, par, k, b * P:(b + 1) * P][:, None, :].to_broadcast([P, J, P]),
                               ACT.Exp, scale=-1.0).then_inc(decay_ok, 1)

            def slot(p, par):
                u, a, c = exists(p), exists(p + 1), exists(p - 1)
                if c:
                    act.wait_ge(vsum_ok, p)
                    act.activation(gstd[:, :], vsum[:, :], ACT.Sqrt, scale=1.0 / J, bias=core.eps[:, 0:1]).then_inc(gstd_ok, 1)
                if u:
                    make_decay(p, par, 1)
                if c:
                    act.wait_ge(ready["z"], p)
                    act.activation(zT[:, :, :], halves(bank[6]), ACT.Copy, scale=0.5).then_inc(read["z"], 1)
                if a:
                    copy_xa(p + 1)
                if u:
                    make_decay(p, par, 2)
                if c:
                    act.wait_ge(mv2_ok, p * PAIR)
                    act.activation(std2[:, :], core.mv_new[:, :, 1], ACT.Sqrt, bias=core.eps[:, 0:1]).then_inc(std2_ok, 1)
                if a:
                    tanh_low(p + 1)
                if u:
                    make_decay(p, par, 3)
                if c:
                    act.wait_ge(ready["xc"], p)
                    for k in range(KC):
                        done = act.activation(xc[:, k, :, 1:P + 1], halves(bank[6])[:, k, :].rearrange("p (b t) -> p b t", b=PAIR), ACT.Identity,
                                              scale=core.col(pre + "ln2_w", k), bias=core.col(pre + "ln2_b", k))
                    done.then_inc(read["xc"], 1)
                    act.wait_ge(ready["kk"], p)
                    act.activation(relu[:, :, :], halves(bank[7]), ACT.Relu).then_inc(relu_ok, 1)
                    act.wait_ge(relu_ok, p)
                    act.activation(kkT[:, :, :], relu[:, :, :], ACT.Square).then_inc(read["kk"], 1)
                    act.wait_ge(ready["rr"], p)
                    act.activation(r_tanh[:, :, :], halves(bank[6]), ACT.Tanh, scale=0.5).then_inc(read["rr"], 1)
                if a:
                    projections(p + 1, 1 - par)
                    make_decay(p + 1, 1 - par, 0)

            rstd_scalar(core, act, root)
            copy_xa(0)
            tanh_low(0)
            projections(0, 0)
            act.wait_ge(made, 6)
            make_decay(0, 0, 0)
            over_slots(act, slot)

        @block.vector
        def _(dve):
            def normalise(a):
                wait(dve, ready["xa"], a)
                for b in range(PAIR):
                    i = a * PAIR + b
                    dve.tensor_scalar(xn[:, b, :], core.x[:, i, :], core.mv[:, i, 0:1], core.rstd[:, bass.ds(i, 1)],
                                      ALU.subtract, ALU.mult).then_inc(xn_ok, 1)
                wait(dve, mix_ok, a * F)
                dve.tensor_scalar(xa[:, :, :, 0:1], ctx_rows[:, :, bass.ds(a * PAIR, PAIR), 1:2], 1.0, None, ALU.mult).then_inc(first_ok, 1)

            def shift_a(a):
                dve.wait_ge(first_ok, a * 2 + 1)
                dve.wait_ge(read["xa"], a + 1)
                dve.tensor_tensor(sx[:, :, :, :].rearrange("p k b t -> p (k b) t"), xa[:, :, :, 0:P].rearrange("p k b t -> p (k b) t"),
                                  xa[:, :, :, 1:P + 1].rearrange("p k b t -> p (k b) t"), ALU.subtract).then_inc(first_ok, 1)
                dve.wait_ge(first_ok, a * 2 + 2)
                for k in range(KC):
                    dve.scalar_tensor_tensor(xmaa[:, k, :, :], sx[:, k, :, :], core.col(pre + "maa_x", k), xa[:, k, :, 1:P + 1],
                                             ALU.mult, ALU.add).then_inc(xmaa_ok, 1)

            def mix(a):
                for f in range(F):
                    dve.wait_ge(f_ready, a * F + (f + 1))
                    for k in range(KC):
                        done = dve.scalar_tensor_tensor(mixed[:, f, k, :], bank[4 + f % 2][:, k * PT:(k + 1) * PT],
                                                        core.col(pre + "maa_stack", f * KC + k), flat(sx[:, :, :, :])[:, k, :], ALU.add, ALU.mult)
                    done.then_inc(f_read, 1)

            def copy_kv(a, par):
                dve.wait_ge(ready["k"], a + 1)
                dve.tensor_copy(kT[:, par, :, :], halves(bank[5])).then_inc(read["k"], 1)
                dve.wait_ge(ready["v"], a + 1)
                dve.tensor_copy(vT[:, par, :, :], halves(bank[3])).then_inc(read["v"], 1)
                dve.wait_ge(g_tanh_ok, a + 1)
                dve.scalar_tensor_tensor(gate[:, par, :, :], g_tanh[:, :, :], 1.0, halves(bank[4]), ALU.add, ALU.mult).then_inc(read["g"], 1)

            def scan(p, par, s):
                k, b = s // PAIR, s % PAIR
                n = p * UNITS + s
                wait(dve, q_ok, n)
                dve.wait_ge(vb_ready, n + 1)
                dve.tensor_tensor(kv[:, :, 1:P + 1], VB, kT[:, par, k, b * P:(b + 1) * P][:, None, :].to_broadcast([P, J, P]), ALU.mult).then_inc(kv_ok, 1)
                dve.tensor_scalar(kv[:, :, 0:1], state0[:, k, bass.ds(p * PAIR + b, 1), :].rearrange("p b j -> p j b"), 1.0, None, ALU.mult).then_inc(kv_ok, 1)
                dve.wait_ge(kv_ok, n * 2 + 2)
                dve.wait_ge(decay_ok, n + 1)
                dve.tensor_tensor_scan(states[:, :, :].rearrange("p j t -> p (j t)"), decay[:, s % 2, :, :].rearrange("p j t -> p (j t)"),
                                       kv[:, :, :].rearrange("p j t -> p (j t)"), 0.0, ALU.mult, ALU.add).then_inc(scan_ok, 1)
                dve.wait_ge(scan_ok, n + 1)
                if not (static(p) and p == 0 and s < 2):
                    dve.wait_ge(sum_ready, p * UNITS + (s - 1))
                dve.scalar_tensor_tensor(prod[:, s % 2, :, :], kv[:, :, 1:P + 1], core.col(pre + "u", k), states[:, :, 0:P],
                                         ALU.mult, ALU.add).then_inc(q_ok, 1)

            def group_norm(c, par):
                dve.wait_ge(sum_ready, c * UNITS + UNITS)
                wait(dve, ready["z"], c)
                dve.tensor_copy(og[:, :, :, :], OG[:, :].rearrange("p (n j h) -> p n h j", j=J, h=HT)).then_inc(og_read, 1)
                heads = og[:, :, :, :].rearrange("p n h j -> p (n h) j")
                squares = sq[:, :, :, :].rearrange("p n h j -> p (n h) j")
                over_j = lambda t: t[:, :, None].to_broadcast([P, UNITS * HT, J])
                s0 = c * 8
                dve.wait_ge(og_read, c + 1)
                dve.tensor_reduce(msum[:, :], heads, AX_X, ALU.add).then_inc(gn_step, 1)
                dve.wait_ge(gn_step, s0 + 1)
                dve.tensor_scalar(mean[:, :], msum[:, :], 1.0 / J, None, ALU.mult).then_inc(gn_step, 1)
                dve.wait_ge(gn_step, s0 + 2)
                dve.tensor_tensor(heads, heads, over_j(mean), ALU.subtract).then_inc(gn_step, 1)
                dve.wait_ge(gn_step, s0 + 3)
                dve.tensor_tensor(squares, heads, heads, ALU.mult).then_inc(gn_step, 1)
                dve.wait_ge(gn_step, s0 + 4)
                dve.tensor_reduce(vsum[:, :], squares, AX_X, ALU.add).then_inc(vsum_ok, 1)
                dve.wait_ge(gstd_ok, c + 1)
                dve.reciprocal(grstd[:, :], gstd[:, :]).then_inc(gn_step, 1)
                dve.wait_ge(gn_step, s0 + 5)
                dve.tensor_tensor(heads, heads, over_j(grstd), ALU.mult).then_inc(gn_step, 1)
                per_token = og[:, :, :, :].rearrange("p (b k) h j -> p b (k h j)", b=PAIR)
                row = lambda n: core.row(pre + n)[:, None, :].to_broadcast([P, PAIR, D])
                dve.wait_ge(gn_step, s0 + 6)
                dve.tensor_tensor(per_token, per_token, row("gn_w"), ALU.mult).then_inc(gn_step, 1)
                dve.wait_ge(gn_step, s0 + 7)
                dve.tensor_tensor(per_token, per_token, row("gn_b"), ALU.add).then_inc(gn_step, 1)
                dve.wait_ge(gn_step, s0 + 8)
                dve.wait_ge(read["g"], c + 1)
                dve.tensor_tensor(per_token, per_token, gate[:, par, :, :], ALU.mult).then_inc(z_ok, 1)

            def residual(c):
                dve.wait_ge(ready["out"], c + 1)
                dve.tensor_tensor(core.x_new[:, :, :], core.x[:, bass.ds(c * PAIR, PAIR), :], halves(bank[7]), ALU.add).then_inc(read["out"], 1)
                dve.wait_ge(read["out"], c + 1)
                for b in range(PAIR):
                    dve.bn_stats(core.stats[:, b, :], core.x_new[:, b, :]).then_inc(st_ok, 1)
                wait(dve, std2_ok, c)
                dve.wait_ge(st_ok, c * PAIR + PAIR)
                dve.tensor_scalar(xc[:, :, :, 0:1], ctx_rows[:, :, bass.ds(c * PAIR, PAIR), 0:1], 1.0, None, ALU.mult).then_inc(c_first, 1)
                for b in range(PAIR):
                    dve.bn_aggr(core.mv_new[:, b, :], core.stats[:, b, :]).then_inc(mv2_ok, 1)

            def normalise2(c):
                dve.wait_ge(std2_ok, c + 1)
                dve.wait_ge(mv2_ok, c * PAIR + PAIR)
                dve.reciprocal(rstd2[:, :], std2[:, :]).then_inc(c_step, 1)
                dve.wait_ge(c_step, c + 1)
                for b in range(PAIR):
                    dve.tensor_scalar(xn2[:, b, :], core.x_new[:, b, :], core.mv_new[:, b, 0:1], rstd2[:, b:b + 1],
                                      ALU.subtract, ALU.mult).then_inc(xn2_ok, 1)

            def shift_c(c):
                dve.wait_ge(read["xc"], c + 1)
                dve.wait_ge(c_first, c + 1)
                dve.tensor_tensor(sx2[:, :, :, :].rearrange("p k b t -> p (k b) t"), xc[:, :, :, 0:P].rearrange("p k b t -> p (k b) t"),
                                  xc[:, :, :, 1:P + 1].rearrange("p k b t -> p (k b) t"), ALU.subtract).then_inc(xk_step, 1)
                dve.wait_ge(xk_step, c + 1)
                for to, n in ((xk2, "ffn_maa_k"), (xr2, "ffn_maa_r")):
                    for k in range(KC):
                        dve.scalar_tensor_tensor(to[:, k, :].rearrange("p (b t) -> p b t", b=PAIR), sx2[:, k, :, :], core.col(pre + n, k),
                                                 xc[:, k, :, 1:P + 1], ALU.mult, ALU.add).then_inc(xk_ok, 1)

            def finish(c):
                dve.wait_ge(read["rr"], c + 1)
                dve.wait_ge(ready["ff"], c + 1)
                dve.scalar_tensor_tensor(gated[:, :, :], r_tanh[:, :, :], 1.0, halves(bank[7]), ALU.add, ALU.mult).then_inc(read["ff"], 1)
                wait(dve, stored, c * DMA)
                dve.wait_ge(read["ff"], c + 1)
                dve.scalar_tensor_tensor(result[:, :, :], gated[:, :, :], 0.5, core.x_new[:, :, :], ALU.mult, ALU.add).then_inc(result_ok, 1)

            def slot(p, par):
                u, a, c = exists(p), exists(p + 1), exists(p - 1)
                if c:
                    group_norm(p - 1, 1 - par)
                if u:
                    scan(p, par, 0)
                if a:
                    normalise(p + 1)
                if c:
                    residual(p - 1)
                if u:
                    scan(p, par, 1)
                if a:
                    shift_a(p + 1)
                if c:
                    normalise2(p - 1)
                if u:
                    scan(p, par, 2)
                if a:
                    mix(p + 1)
                if c:
                    shift_c(p - 1)
                if u:
                    scan(p, par, 3)
                if a:
                    copy_kv(p + 1, 1 - par)
                if c:
                    finish(p - 1)

            rstd_vector(core, dve, root, rstep)
            normalise(0)
            shift_a(0)
            mix(0)
            copy_kv(0, 0)
            dve.wait_ge(s0_in, DMA)
            over_slots(dve, slot)


def store_stage(core):
    nc = core.nc
    with ExitStack() as ctx:
        stored = ctx.enter_context(nc.semaphore("stored"))
        block = ctx.enter_context(nc.Block())

        @block.sync
        def _(sp):
            sp.dma_start(core.out.rearrange("b t d -> t b d"), core.x[:, :, :]).then_inc(stored, DMA)
            sp.wait_ge(stored, DMA)


def build_program(nc, dram, out):
    with ExitStack() as ctx:
        core = Core(nc, ctx, dram, out)
        load_stage(core)
        for stage in STAGES:
            if stage == "l1_first":
                wide_attention(core, 1)
            elif stage == "l1_second":
                wide_attention(core, 2)
            elif stage == "l0_self":
                narrow_attention(core, "self")
            elif stage == "l0_cross":
                narrow_attention(core, "cross")
            elif stage == "l0_mlp":
                mlp(core, "L0_xattn_", "ln3_s", "ln3_b", "w1", "b1", "w2", "b2", ACT.Gelu_apprx_tanh)
            elif stage == "l1_mlp":
                mlp(core, "L1_xattn_", "ln_mlp_scale", "ln_mlp_offset", "w_fc1", "b_fc1", "w_fc2", "b_fc2", ACT.Gelu)
            elif stage == "l2":
                single_attention(core)
            elif stage == "l3":
                recurrence(core)
        if STAGES[-1] != "l3":
            store_stage(core)


PLAIN = ["L0_xattn_w_qkv", "L0_xattn_w_ao", "L0_xattn_w_q", "L0_xattn_w_kv", "L0_xattn_w_co", "L0_xattn_w1", "L0_xattn_w2",
         "L1_xattn_wq1", "L1_xattn_wk1", "L1_xattn_wv1", "L1_xattn_wo1", "L1_xattn_wq2", "L1_xattn_wk2", "L1_xattn_wv2",
         "L1_xattn_wo2", "L1_xattn_w_fc1", "L1_xattn_w_fc2", "L3_xattn_maa_w1", "L3_xattn_td_w1", "L3_xattn_td_w2"]
TRANSPOSED = ["L2_xattn_w_q", "L2_xattn_w_k", "L2_xattn_w_v", "L2_xattn_w_o", "L3_xattn_Wr", "L3_xattn_Wk", "L3_xattn_Wv",
              "L3_xattn_Wg", "L3_xattn_Wo", "L3_xattn_Wfk", "L3_xattn_Wfr", "L3_xattn_Wfv"]


def kernel(**inputs):
    import concourse.bacc as bacc
    from concourse.bass_utils import run_bass_kernel_spmd

    a = {k: np.asarray(v) for k, v in inputs.items()}
    arrays = {
        "x": a["x"],
        "ctx_t": np.ascontiguousarray(a["ctx_2048"].reshape(TOK, D).T),
        "state0": np.ascontiguousarray(a["ctx_2048"][:, 2:10, :].reshape(NB, KC, P, 8).transpose(2, 1, 0, 3)),
        "mask_self": a["mask_1x1xSxS2_fc1"].reshape(P, P),
        "mask_cross": np.ascontiguousarray(a["mask_Bx1xSxS2_ff1"].reshape(NB, P, P)),
        "columns": np.ascontiguousarray(np.concatenate([a[n].reshape(-1, P) for n, _ in COLUMNS]).T),
        "rows": np.ascontiguousarray(np.broadcast_to(np.stack([a[n] for n in ROWS]), (P, len(ROWS), D))),
        "maa_w2": a["L3_xattn_maa_w2"].reshape(5 * 32, D),
        "alpha": np.ascontiguousarray(np.broadcast_to(a["L2_xattn_alpha"].reshape(1, 1), (P, 1))),
    }
    for n in PLAIN:
        arrays[n] = a[n]
    for n in TRANSPOSED:
        arrays[n] = np.ascontiguousarray(a[n].T)
    nc = bacc.Bacc("TRN2", target_bir_lowering=False, num_devices=1)
    dram = {n: nc.dram_tensor("in_" + n, v.shape, mybir.dt.from_np(v.dtype), kind="ExternalInput").ap()
            for n, v in arrays.items()}
    out = nc.dram_tensor("out", (NB, P, D), F32, kind="ExternalOutput").ap()
    build_program(nc, dram, out)
    r = run_bass_kernel_spmd(nc, [{"in_" + n: v for n, v in arrays.items()}], core_ids=[0])
    return r.results[0]["out"]
```

```python
from contextlib import ExitStack

import numpy as np

import concourse.bass as bass
from concourse import mybir

ALU = mybir.AluOpType
ACT = mybir.ActivationFunctionType
F32 = mybir.dt.float32
F32R = mybir.dt.float32r
AX_X = mybir.AxisListType.X

P = 128
NB = 16
D = 256
KC = D // P
PAIR = 2
NP = NB // PAIR
TOK = NB * P
PT = PAIR * P
EPS = 1e-5
HG = 4
NHG = 4
DMA = 16

COLUMNS = [
    ("L0_xattn_ln1_s", D), ("L0_xattn_ln1_b", D), ("L0_xattn_ln2_s", D), ("L0_xattn_ln2_b", D),
    ("L0_xattn_ln3_s", D), ("L0_xattn_ln3_b", D), ("L0_xattn_b_qkv", 3 * D), ("L0_xattn_b_q", D),
    ("L0_xattn_b_kv", 2 * D), ("L0_xattn_b1", 4 * D),
    ("L1_xattn_ln1_scale", D), ("L1_xattn_ln1_offset", D), ("L1_xattn_ln2_scale", D),
    ("L1_xattn_ln2_offset", D), ("L1_xattn_ln_mlp_scale", D), ("L1_xattn_ln_mlp_offset", D),
    ("L1_xattn_bq1", 2048), ("L1_xattn_bk1", 2048), ("L1_xattn_bv1", 2048),
    ("L1_xattn_bias_k1", 2048), ("L1_xattn_bias_v1", 2048),
    ("L1_xattn_bq2", 2048), ("L1_xattn_bk2", 2048), ("L1_xattn_bv2", 2048),
    ("L1_xattn_bias_k2", 2048), ("L1_xattn_bias_v2", 2048), ("L1_xattn_b_fc1", 4 * D),
    ("L3_xattn_ln1_w", D), ("L3_xattn_ln1_b", D), ("L3_xattn_ln2_w", D), ("L3_xattn_ln2_b", D),
    ("L3_xattn_maa_x", D), ("L3_xattn_maa_stack", 5 * D), ("L3_xattn_time_decay", D),
    ("L3_xattn_u", D), ("L3_xattn_ffn_maa_k", D), ("L3_xattn_ffn_maa_r", D),
]
ROWS = {"b_ao": "L0_xattn_b_ao", "b_co": "L0_xattn_b_co", "b2": "L0_xattn_b2", "bo1": "L1_xattn_bo1", "bo2": "L1_xattn_bo2",
        "b_fc2": "L1_xattn_b_fc2", "gn_w": "L3_xattn_gn_w", "gn_b": "L3_xattn_gn_b"}
COLUMN_AT, at = {}, 0
for name, size in COLUMNS:
    COLUMN_AT[name] = at
    at += size // P
N_COLUMNS = at

LATE, EARLY, WO, WORK, ARENA = 0, 12288, 24576, 28672, 42496
GROUP = 3 * KC * HG * P
FREE = {
    "l0_self": [(EARLY, ARENA)], "l0_cross": [(EARLY, ARENA)], "l0_mlp": [(WORK, ARENA)],
    "l1_first": [(WORK, ARENA)], "l1_second": [(WORK, ARENA)], "l1_mlp": [(WORK, ARENA)],
    "l2": [(WORK, ARENA)], "l3": [(LATE, EARLY), (WO, ARENA)],
}


def matrix(name, dram, at, rows, cols):
    return name, dram, at, rows, cols


WEIGHTS = {
    "l0_self": [matrix("w_qkv", "L0_xattn_w_qkv", LATE, D, 3 * D), matrix("w_out", "L0_xattn_w_ao", LATE + 1536, D, D),
                matrix("row", "row_b_ao", LATE + 8192, P, D)],
    "l0_cross": [matrix("w_q", "L0_xattn_w_q", LATE + 2048, D, D), matrix("w_kv", "L0_xattn_w_kv", LATE + 2560, D, 2 * D),
                 matrix("w_out", "L0_xattn_w_co", LATE + 3584, D, D), matrix("row", "row_b_co", LATE + 8448, P, D)],
    "l0_mlp": [matrix("w1", "L0_xattn_w1", LATE + 4096, D, 4 * D), matrix("w2", "L0_xattn_w2", LATE + 6144, 4 * D, D),
               matrix("row", "row_b2", LATE + 8704, P, D)],
    "l1_first": [matrix("wo", "L1_xattn_wo1", WO, 2048, D)],
    "l1_second": [matrix("wo", "L1_xattn_wo2", WO, 2048, D)],
    "l1_mlp": [matrix("w1", "L1_xattn_w_fc1", EARLY, D, 4 * D), matrix("row", "row_b_fc2", EARLY + 2048, P, D),
               matrix("w2", "L1_xattn_w_fc2", EARLY + GROUP, 4 * D, D)],
    "l2": [matrix(w, "L2_xattn_" + w, EARLY + 5120 + 512 * i, D, D) for i, w in enumerate(("w_q", "w_k", "w_v", "w_o"))]
          + [matrix("alpha", "alpha", EARLY + 2944, P, 1)],
    "l3": [matrix("maa_w1", "L3_xattn_maa_w1", EARLY + 7168, D, 160), matrix("maa_w2", "maa_w2", EARLY + 2304, P, D),
           matrix("maa_w2g", "maa_w2g", EARLY + 2560, 32, D), matrix("td_w1", "L3_xattn_td_w1", EARLY + 2816, D, 64),
           matrix("td_w2", "L3_xattn_td_w2", EARLY + 7488, 64, D), matrix("state0", "state0", EARLY + 7744, P, D)]
          + [matrix(w, "L3_xattn_" + w, EARLY + 8000 + 512 * i, D, D)
             for i, w in enumerate(("Wk", "Wv", "Wr", "Wg", "Wo", "Wfk", "Wfr", "Wfv"))],
}
LOADED_IN = {"load": ["l0_self", "l0_cross", "l0_mlp"], "l0_mlp": ["l1_first"]}
LOADED_AFTER_GROUP = {0: [("l1_mlp", "w1"), ("l1_mlp", "row")], 1: [("l1_mlp", "w2")], 3: [("l2", None), ("l3", None)]}

STAGES = ["l0_self", "l0_cross", "l0_mlp", "l1_first", "l1_second", "l1_mlp", "l2", "l3"]


def wait(eng, sem, value):
    if isinstance(value, int) and value <= 0:
        return
    eng.wait_ge(sem, value)


def over_pairs(eng, body):
    body(0)
    with eng.Fori(1, NP - 1) as p:
        body(p)
    body(NP - 1)


def split_product(pe, out, stationary, moving, start, stop):
    (s_hi, s_lo), (m_hi, m_lo) = stationary, moving
    pe.matmul(out, s_hi, m_lo, start=start, stop=False)
    pe.matmul(out, s_lo, m_hi, start=False, stop=False)
    return pe.matmul(out, s_hi, m_hi, start=False, stop=stop)


def over_steps(eng, body):
    def step(s):
        for par in range(2):
            body(s * 2 + par, par)
    step(0)
    with eng.Fori(1, NP // 2 - 1) as s:
        step(s)
    step(NP // 2 - 1)


GROUPS = {"l1_first": [f"group{g}" for g in range(NHG)], "l1_second": [f"group{g}" for g in range(NHG)]}


class Core:

    def __init__(self, nc, ctx, dram, out):
        self.nc, self.dram, self.out = nc, dram, out
        sb = lambda name, shape: ctx.enter_context(nc.sbuf_tensor(name, shape, F32))
        self.x = sb("x", [P, NB, D])
        self.cT = sb("ctx_t", [P, KC, TOK])
        self.ident = sb("ident", [P, P])
        self.cols = sb("cols", [P, N_COLUMNS])
        self.arena_at = nc.sbuf_base
        self.arena = sb("arena", [P, ARENA])
        self.loaded = {(stage, name): ctx.enter_context(nc.semaphore(f"loaded_{stage}_{name}"))
                       for stage in STAGES for name in [w[0] for w in WEIGHTS[stage]] + GROUPS.get(stage, [])}
        self.begun = set()
        self.mv = sb("mean_var", [P, NB, 2])
        self.rstd = sb("rstd", [P, NB])
        self.std = sb("std", [P, NB])
        self.newton = sb("newton", [P, NB])
        self.stats = sb("bn_stats", [P, PAIR, 6])
        self.mv_new = sb("mean_var_new", [P, PAIR, 2])
        self.x_new = sb("x_new", [P, PAIR, D])
        self.eps = sb("eps", [P, 1])
        self.head_rows = sb("head_rows", [P, 8])
        self.head_rows2 = sb("head_rows2", [P, 16])
        self.banks = ctx.enter_context(nc.psum_tensor("banks", [P, 8, 512], F32))
        self.bank = [self.banks[:, i, :] for i in range(8)]

    def col(self, name, k=0, n=1):
        at = COLUMN_AT[name] + k
        return self.cols[:, at:at + n]

    def place(self, at, shape):
        size = int(np.prod(shape[1:]))
        flat = self.arena[0:shape[0], at:at + size]
        if len(shape) == 2:
            return flat
        names = "abcd"[:len(shape) - 1]
        return flat.rearrange(f"p ({' '.join(names)}) -> p {' '.join(names)}", **dict(zip(names, shape[1:])))

    def place_r(self, name, at, shape):
        return self.nc.alloc_sbuf_tensor_at(name, shape, F32R, offset=self.arena_at + 4 * at)

    def weight(self, stage, name):
        _, _, at, rows, cols = next(w for w in WEIGHTS[stage] if w[0] == name)
        return self.place(at, [rows, cols] if rows <= P else [P, rows // P, cols])

    def wait_loaded(self, eng, stage, *names, times=1):
        for name in names:
            eng.wait_ge(self.loaded[stage, name], DMA * times)

    def load_one(self, sp, stage, wanted=None):
        for name, dram, at, rows, cols in WEIGHTS.get(stage, []):
            if stage not in STAGES or (stage, name) in self.begun or wanted not in (None, name):
                continue
            self.begun.add((stage, name))
            source = self.dram[dram]
            if rows > P:
                source = source.rearrange("(k p) o -> p k o", p=P)
            sp.dma_start(self.weight(stage, name), source).then_inc(self.loaded[stage, name], DMA)

    def load_group(self, sp, stage, g):
        name = GROUPS[stage][g]
        if stage not in STAGES or (stage, name) in self.begun:
            return
        self.begun.add((stage, name))
        n = 1 + list(GROUPS).index(stage)
        for i, w in enumerate("qkv"):
            source = self.dram[f"L1_xattn_w{w}{n}"].rearrange("(k p) o -> p k o", p=P)[:, :, g * HG * P:(g + 1) * HG * P]
            sp.dma_start(self.group_weight(EARLY, i, g), source).then_inc(self.loaded[stage, name], DMA)

    def group_weight(self, region, i, g):
        return self.place(region + self.group_at(i, g), [P, KC, HG * P])

    def group_at(self, i, g):
        return g * GROUP + i * KC * HG * P

    def load(self, sp, stage):
        for of in [stage] + LOADED_IN.get(stage, []):
            for g in range(len(GROUPS.get(of, []))):
                self.load_group(sp, of, g)
            self.load_one(sp, of)


class Space:

    def __init__(self, core, stage):
        self.core, self.free = core, [list(r) for r in FREE[stage]]

    def __call__(self, name, shape):
        size = int(np.prod(shape[1:]))
        for r in self.free:
            if r[1] - r[0] >= size:
                at = r[0]
                r[0] += size
                return self.core.place(at, shape)
        raise AssertionError(f"no room for {name}: {size} of {self.free}")

    def split(self, name, shape):
        before = [r[0] for r in self.free]
        full = self(name, shape)
        at = next(b for b, r in zip(before, self.free) if r[0] != b)
        before = [r[0] for r in self.free]
        self(name + "_hi", shape)
        hi_at = next(b for b, r in zip(before, self.free) if r[0] != b)
        return full, (self.core.place_r(name + "_hi", hi_at, shape), self.core.place_r(name + "_lo", at, shape))


def zero_signals(core, signals):
    numbers = sorted(s.num for s in signals)
    starts = [n for n in numbers if n - 1 not in numbers]
    ends = [n + 1 for n in numbers if n + 1 not in numbers]
    with core.nc.Block() as block:
        @block.gpsimd
        def _(gp):
            for start, end in zip(starts, ends):
                gp.sem_clear(range(start, end))


class Signals:

    def __init__(self, core, ctx, prefix):
        self.core, self.nc, self.prefix, self.all = core, core.nc, prefix, []
        ctx.callback(self.close)
        self.holders = ExitStack()

    def __call__(self, name):
        self.all.append(self.holders.enter_context(self.nc.semaphore(self.prefix + name)))
        return self.all[-1]

    def close(self):
        zero_signals(self.core, self.all)
        self.holders.close()


def load_stage(core, reload_x=True):
    nc = core.nc
    with ExitStack() as ctx:
        sem = Signals(core, ctx, "")
        x_in, consts_in, filled = sem("ld_x"), sem("ld_consts"), sem("ld_filled")
        copied, stat = sem("ld_copied"), sem("ld_stat")
        block = ctx.enter_context(nc.Block())

        @block.sync
        def _(sp):
            sp.dma_start(core.x[:, :, :], core.dram["x"].rearrange("b t d -> t b d")).then_inc(x_in, DMA)
            sp.dma_start(core.cols[:, :], core.dram["columns"]).then_inc(consts_in, DMA)
            core.load(sp, "load")
            sp.dma_start(core.cT[:, :, :], core.dram["ctx_t"].rearrange("(k p) t -> p k t", p=P)).then_inc(consts_in, DMA)
            sp.wait_ge(consts_in, 2 * DMA)

        @block.gpsimd
        def _(gp):
            gp.memset(core.eps[:, :], EPS).then_inc(filled, 1)
            gp.memset(core.ident[:, :], 0.0).then_inc(filled, 1)
            gp.wait_ge(filled, 2)
            gp.affine_select(out=core.ident[:, :], in_=core.ident[:, :], compare_op=ALU.not_equal, fill=1.0,
                             base=0, pattern=[[-1, P]], channel_multiplier=1).then_inc(filled, 1)
            gp.memset(core.head_rows2[:, :], 1.0).then_inc(filled, 1)
            gp.wait_ge(filled, 4)
            gp.affine_select(out=core.head_rows2[:, :], in_=core.head_rows2[:, :], compare_op=ALU.is_ge, fill=0.0,
                             base=0, pattern=[[0, 2], [-16, 8]], channel_multiplier=1).then_inc(filled, 1)
            gp.wait_ge(filled, 5)
            gp.affine_select(out=core.head_rows2[:, :], in_=core.head_rows2[:, :], compare_op=ALU.is_ge, fill=0.0,
                             base=15, pattern=[[0, 2], [16, 8]], channel_multiplier=-1).then_inc(filled, 1)
            gp.wait_ge(filled, 6)
            gp.tensor_copy(core.head_rows[:, :], core.head_rows2[:, 0:8]).then_inc(filled, 1)

        @block.vector
        def _(dve):
            dve.wait_ge(x_in, DMA)
            def body(p):
                wait(dve, stat, p * (2 * PAIR + 1))
                dve.tensor_copy(core.x_new[:, :, :], core.x[:, bass.ds(p * PAIR, PAIR), :]).then_inc(copied, 1)
                dve.wait_ge(copied, p + 1)
                row_stats(core, dve, stat, p, p * (2 * PAIR + 1))
            over_pairs(dve, body)


def row_stats(core, dve, stat, p, before):
    for b in range(PAIR):
        dve.bn_stats(core.stats[:, b, :], core.x_new[:, b, :]).then_inc(stat, 1)
    dve.wait_ge(stat, before + PAIR)
    dve.tensor_scalar(core.x[:, bass.ds(p * PAIR, PAIR), :], core.x_new[:, :, :], 1.0, None, ALU.mult)
    for b in range(PAIR):
        dve.bn_aggr(core.mv_new[:, b, :], core.stats[:, b, :]).then_inc(stat, 1)
    dve.wait_ge(stat, before + 2 * PAIR)
    dve.tensor_scalar(core.mv[:, bass.ds(p * PAIR, PAIR), :], core.mv_new[:, :, :], 1.0, None, ALU.mult).then_inc(stat, 1)


def new_rows(core, dve, step, stat, p, update, update_ready, bias=None):
    steps = 1 if bias is None else 2
    dve.wait_ge(update_ready, p + 1)
    wait(dve, stat, p * (2 * PAIR + 1))
    dve.tensor_tensor(core.x_new[:, :, :], core.x[:, bass.ds(p * PAIR, PAIR), :], update, ALU.add).then_inc(step, 1)
    dve.wait_ge(step, p * steps + 1)
    if bias is not None:
        dve.tensor_tensor(core.x_new[:, :, :], core.x_new[:, :, :], bias[:, None, :].to_broadcast([P, PAIR, D]), ALU.add).then_inc(step, 1)
        dve.wait_ge(step, p * steps + 2)
    row_stats(core, dve, stat, p, p * (2 * PAIR + 1))


def rstd_scalar(core, act, root):
    act.activation(core.std[:, :], core.mv[:, :, 1], ACT.Sqrt, bias=core.eps[:, 0:1]).then_inc(root, 1)


def rstd_vector(core, dve, root, step):
    dve.wait_ge(root, 1)
    dve.reciprocal(core.rstd[:, :], core.std[:, :]).then_inc(step, 1)
    dve.wait_ge(step, 1)
    dve.tensor_tensor(core.newton[:, :], core.rstd[:, :], core.rstd[:, :], ALU.mult).then_inc(step, 1)
    dve.tensor_scalar(core.std[:, :], core.mv[:, :, 1], EPS, -0.5, ALU.add, ALU.mult).then_inc(step, 1)
    dve.wait_ge(step, 3)
    dve.tensor_tensor(core.newton[:, :], core.newton[:, :], core.std[:, :], ALU.mult).then_inc(step, 1)
    dve.wait_ge(step, 4)
    dve.scalar_tensor_tensor(core.rstd[:, :], core.newton[:, :], 1.5, core.rstd[:, :],
                             ALU.add, ALU.mult).then_inc(step, 1)
    dve.wait_ge(step, 5)


def wide_attention(core, stage, n):
    nc = core.nc
    H, HD = 16, P
    SCALE = float(HD) ** -0.5
    pre = "L1_xattn_"
    ln_s, ln_b = pre + f"ln{n}_scale", pre + f"ln{n}_offset"
    bq, bk, bv = pre + f"bq{n}", pre + f"bk{n}", pre + f"bv{n}"
    bias_k, bias_v = pre + f"bias_k{n}", pre + f"bias_v{n}"
    with ExitStack() as ctx:
        sb = Space(core, stage)
        sem = Signals(core, ctx, f"w{n}_")
        wo = core.weight(stage, "wo")
        w_full = [[core.group_weight(EARLY, i, g) for i in range(3)] for g in range(NHG)]
        w_hi, w_lo = ([[core.place_r(f"w{n}_{part}_{g}_{i}", region + core.group_at(i, g), [P, KC, HG * HD]) for i in range(3)]
                       for g in range(NHG)] for part, region in (("hi", LATE), ("lo", EARLY)))
        xn = sb("xn", [P, PAIR, D])
        hT, (hT_hi, hT_lo) = sb.split(f"w{n}_hT", [P, KC, PT])
        kv_in, (kv_hi, kv_lo) = sb.split(f"w{n}_kv", [P, KC, PT])
        qT, kT = sb("qT", [P, HG, PT]), sb("kT", [P, HG, PT])
        v = sb("v", [P, 2, PAIR, HG * HD])
        prob = sb("prob", [P, PAIR, HG, P])
        probT = sb("probT", [P, PAIR, HG, P])
        headT = sb("headT", [P, H, PT])
        own = sb("own", [P, PAIR, HG])
        top = sb("top", [P, PAIR, HG])
        shift = sb("shift", [P, PAIR, HG])
        own_e = sb("own_e", [P, PAIR, HG])
        total = sb("total", [P, PAIR, HG])
        inv = sb("inv", [P, PAIR, HG])
        own_p = sb("own_p", [P, PAIR, H])
        early = sb("early", [P, H * H])
        dvz = early.rearrange("p (a b) -> p a b", a=H)
        own_pT = early[0:H, 0:PT]
        bvo = sb("bvo", [H, D])
        obias = sb("obias", [P, D])
        bank = core.bank
        BL, LN = bank[2], bank[7]

        row_in = sem("row_in")
        root, rstep = sem("root"), sem("rstep")
        hn_ok, lt_ok, hT_ok = sem("hn_ok"), sem("lt_ok"), sem("hT_ok")
        kv_in_ok, kv_hi_ok, kv_ok = sem("kv_in_ok"), sem("kv_hi_ok"), sem("kv_ok")
        hT_raw, hT_hi_ok, w_hi_ok, w_ok = sem("hT_raw"), sem("hT_hi_ok"), sem("w_hi_ok"), sem("w_ok")
        proj_ok, qk_ok, v_ok = sem("proj_ok"), sem("qk_ok"), sem("v_ok")
        own_ready, own_copied = sem("own_ready"), sem("own_copied")
        score_ok, top_step, shift_ok, exp_ok = sem("score_ok"), sem("top_step"), sem("shift_ok"), sem("exp_ok")
        norm_step, prob_ok = sem("norm_step"), sem("prob_ok")
        pt_ok, probT_ok, pv_ok, head_ok = sem("pt_ok"), sem("probT_ok"), sem("pv_ok"), sem("head_ok")
        ot_ok, own_pT_ok, out_ok = sem("ot_ok"), sem("own_pT_ok"), sem("out_ok")
        dv_step, const_ok, const_copied = sem("dv_step"), sem("const_ok"), sem("const_copied")
        res_ok, stat = sem("res_ok"), sem("stat")
        block = ctx.enter_context(nc.Block())

        @block.sync
        def _(sp):
            core.load(sp, stage)
            sp.dma_start(obias, core.dram[f"row_bo{n}"]).then_inc(row_in, DMA)

            def body(p):
                wait(sp, proj_ok, p * (6 * NHG))
                sp.dma_start(kv_in[:, :, :], core.cT[:, :, bass.ts(p, PT)]).then_inc(kv_in_ok, DMA)
            over_pairs(sp, body)
            for g in range(NHG):
                sp.wait_ge(proj_ok, ((NP - 1) * NHG + g + 1) * 6)
                if n == 1:
                    core.load_group(sp, "l1_second", g)
                else:
                    for of, name in LOADED_AFTER_GROUP.get(g, []):
                        core.load_one(sp, of, name)

        @block.gpsimd
        def _(gp):
            def weight_lo(g):
                for i in range(3):
                    gp.wait_ge(w_hi_ok, g * 3 + i + 1)
                    gp.tensor_tensor(w_lo[g][i][:, :, :], w_full[g][i], w_hi[g][i][:, :, :], ALU.subtract).then_inc(w_ok, 1)

            def context_lo(p):
                gp.wait_ge(kv_hi_ok, p + 1)
                gp.tensor_tensor(kv_lo[:, :, :], kv_in, kv_hi[:, :, :], ALU.subtract).then_inc(kv_ok, 1)

            def rows_lo(p):
                gp.wait_ge(hT_hi_ok, p + 1)
                gp.tensor_tensor(hT_lo[:, :, :], hT, hT_hi[:, :, :], ALU.subtract).then_inc(hT_ok, 1)

            def body(p):
                if isinstance(p, int) and p == NP - 1:
                    return
                if isinstance(p, int) and p == 0:
                    weight_lo(2)
                    weight_lo(3)
                rows_lo(p + 1)
                context_lo(p + 1)

            weight_lo(0)
            rows_lo(0)
            context_lo(0)
            weight_lo(1)
            over_pairs(gp, body)

        @block.tensor
        def _(pe):
            def ln_transpose(p):
                if not isinstance(p, int) or p > 1:
                    wait(pe, res_ok, (p - 1) * 2 - 1)
                pe.wait_ge(hn_ok, p * PAIR + PAIR)
                for k in range(KC):
                    for b in range(PAIR):
                        mm = pe.transpose(LN[:, k * PT + b * P:k * PT + (b + 1) * P], xn[:, b, k * P:(k + 1) * P], core.ident[:, :])
                mm.then_inc(lt_ok, 1)

            def project_qk(p, g, u):
                if g == 0:
                    pe.wait_ge(hT_ok, p + 1)
                for use in range(4):
                    i_w, hi, lo = (0, hT_hi, hT_lo) if use < 2 else (1, kv_hi, kv_lo)
                    if use == 2 and g == 0:
                        pe.wait_ge(kv_ok, p + 1)
                    if isinstance(p, int) and p == 0 and use % 2 == 0:
                        pe.wait_ge(w_ok, g * 3 + i_w + 1)
                    if use < 2:
                        wait(pe, v_ok, u * 2 - 1 + use)
                    else:
                        pe.wait_ge(qk_ok, u * 4 + use - 1)
                    for i in range(2):
                        h = (use % 2) * 2 + i
                        for k in range(KC):
                            mm = split_product(pe, bank[use % 2][:, i * PT:(i + 1) * PT],
                                               [w[g][i_w][:, k, h * HD:(h + 1) * HD] for w in (w_hi, w_lo)],
                                               [m[:, k, :] for m in (hi, lo)], k == 0, k == KC - 1)
                    mm.then_inc(proj_ok, 1)

            def project_v(p, g, u):
                if isinstance(p, int) and p == 0:
                    pe.wait_ge(w_ok, g * 3 + 3)
                for b in range(PAIR):
                    pe.wait_ge(qk_ok, u * 4 + 3 + b)
                    for k in range(KC):
                        mm = split_product(pe, bank[b][:, :], [m[:, k, b * P:(b + 1) * P] for m in (kv_hi, kv_lo)],
                                           [w[g][2][:, k, :] for w in (w_hi, w_lo)], k == 0, k == KC - 1)
                    mm.then_inc(proj_ok, 1)

            def scores(u, g):
                pe.wait_ge(qk_ok, u * 4 + 4)
                wait(pe, own_copied, u)
                for b in range(PAIR):
                    for i in range(HG):
                        mm = pe.matmul(BL[:, b * HG + i:b * HG + i + 1], qT[:, i, b * P:(b + 1) * P],
                                       core.col(bias_k, g * HG + i), start=True, stop=True)
                mm.then_inc(own_ready, 1)
                for b in range(PAIR):
                    wait(pe, exp_ok, u * 2 - 1 + b)
                    for i in range(HG):
                        mm = pe.matmul(bank[3 + b][:, i * P:(i + 1) * P], qT[:, i, b * P:(b + 1) * P], kT[:, i, b * P:(b + 1) * P],
                                       start=True, stop=True)
                    mm.then_inc(score_ok, 1)

            def prob_transpose(u):
                for b in range(PAIR):
                    pe.wait_ge(prob_ok, u * 2 + 1 + b)
                    wait(pe, head_ok, u * 2 - 1 + b)
                    for i in range(HG):
                        mm = pe.transpose(bank[5 + b][:, i * P:(i + 1) * P], prob[:, b, i, :], core.ident[:, :])
                    mm.then_inc(pt_ok, 1)

            def weigh_values(u, par):
                pe.wait_ge(probT_ok, u * 2 + 2)
                pe.wait_ge(v_ok, u * 2 + 2)
                for half in range(2):
                    for i in (half * 2, half * 2 + 1):
                        for b in range(PAIR):
                            at = (i % 2) * PT + b * P
                            mm = pe.matmul(bank[5 + half][:, at:at + P], v[:, par, b, i * HD:(i + 1) * HD], probT[:, b, i, :],
                                           start=True, stop=True)
                    mm.then_inc(pv_ok, 1)

            def own_transpose(p):
                pe.wait_ge(prob_ok, (p + 1) * (2 * NHG))
                if isinstance(p, int) and p == NP - 1:
                    pe.wait_ge(hT_raw, NP)
                else:
                    pe.wait_ge(hT_raw, p + 2)
                for b in range(PAIR):
                    mm = pe.transpose(LN[0:H, b * P:(b + 1) * P], own_p[:, b, :], core.ident[:, :])
                mm.then_inc(ot_ok, 1)

            def project_out(p):
                pe.wait_ge(own_pT_ok, p + 1)
                pe.wait_ge(head_ok, (p + 1) * (2 * NHG))
                for b in range(PAIR):
                    at = LN[:, b * D:(b + 1) * D]
                    pe.matmul(at, own_pT[:, b * P:(b + 1) * P], bvo[:, :], start=True, stop=False)
                    for h in range(H):
                        mm = pe.matmul(at, headT[:, h, b * P:(b + 1) * P], wo[:, h, :], start=False, stop=(h == H - 1))
                mm.then_inc(out_ok, 1)

            def constants():
                pe.wait_ge(head_ok, 2 * (NHG - 1))
                core.wait_loaded(pe, stage, "wo")
                pe.wait_ge(dv_step, 3)
                for h in range(H):
                    mm = pe.matmul(bank[5][0:H, 0:D], dvz[:, h, :], wo[:, h, :], start=(h == 0), stop=(h == H - 1))
                mm.then_inc(const_ok, 1)
                for h in range(H):
                    mm = pe.matmul(bank[6][:, 0:D], core.col(bv, h).to_broadcast([P, P]), wo[:, h, :],
                                   start=(h == 0), stop=(h == H - 1))
                mm.then_inc(const_ok, 1)

            def body(p):
                last = isinstance(p, int) and p == NP - 1
                for g in range(NHG):
                    u = p * NHG + g
                    p1, g1 = (p, g + 1) if g < NHG - 1 else (p + 1, 0)
                    if g == 0 and not (isinstance(p, int) and p == 0):
                        own_transpose(p - 1)
                    scores(u, g)
                    more = not (last and g == NHG - 1)
                    if more:
                        project_qk(p1, g1, u + 1)
                    if g == 0 and not (isinstance(p, int) and p == 0):
                        project_out(p - 1)
                    if g == NHG - 2 and not last:
                        ln_transpose(p + 1)
                    if isinstance(u, int) and u == NHG - 1:
                        constants()
                        pe.wait_ge(const_copied, 2)
                    prob_transpose(u)
                    if more:
                        project_v(p1, g1, u + 1)
                    weigh_values(u, g % 2)

            ln_transpose(0)
            project_qk(0, 0, 0)
            project_v(0, 0, 0)
            over_pairs(pe, body)
            own_transpose(NP - 1)
            project_out(NP - 1)

        @block.scalar
        def _(act):
            def layer_norm(p):
                act.wait_ge(lt_ok, p + 1)
                for k in range(KC):
                    done = act.activation(hT[:, k, :], LN[:, k * PT:(k + 1) * PT], ACT.Identity,
                                          scale=core.col(ln_s, k), bias=core.col(ln_b, k))
                done.then_inc(hT_raw, 1)
                act.wait_ge(hT_raw, p + 1)
                act.activation(hT_hi[:, :, :], hT, ACT.Copy).then_inc(hT_hi_ok, 1)

            def context_hi(p):
                act.wait_ge(kv_in_ok, p * DMA + DMA)
                act.activation(kv_hi[:, :, :], kv_in, ACT.Copy).then_inc(kv_hi_ok, 1)

            def weight_hi(g):
                core.wait_loaded(act, stage, GROUPS[stage][g], times=3)
                for i in range(3):
                    act.activation(w_hi[g][i][:, :, :], w_full[g][i], ACT.Copy).then_inc(w_hi_ok, 1)

            def copy_v(u, par):
                for b in range(PAIR):
                    act.wait_ge(proj_ok, u * 6 + 5 + b)
                    act.activation(v[:, par, b, :], bank[b][:, :], ACT.Copy).then_inc(v_ok, 1)

            def body(p):
                last = isinstance(p, int) and p == NP - 1
                for g in range(NHG):
                    u = p * NHG + g
                    if g == NHG - 1 and not last:
                        context_hi(p + 1)
                    for b in range(PAIR):
                        act.wait_ge(shift_ok, u * 2 + 1 + b)
                        for i in range(HG):
                            act.activation(prob[:, b, i, :], bank[3 + b][:, i * P:(i + 1) * P], ACT.Exp, scale=SCALE,
                                           bias=shift[:, b, i:i + 1], accum_out=total[:, b, i:i + 1])
                        act.activation(own_e[:, b, :], own_e[:, b, :], ACT.Exp).then_inc(exp_ok, 1)
                    if g == NHG - 2 and not last:
                        layer_norm(p + 1)
                    for b in range(PAIR):
                        act.wait_ge(pt_ok, u * 2 + 1 + b)
                        act.activation(probT[:, b, :, :], bank[5 + b][:, :].rearrange("p (h q) -> p h q", h=HG),
                                       ACT.Copy).then_inc(probT_ok, 1)
                    if isinstance(u, int) and u < 2:
                        weight_hi(u + 2)
                    if not (last and g == NHG - 1):
                        copy_v(u + 1, (g + 1) % 2)

            rstd_scalar(core, act, root)
            weight_hi(0)
            layer_norm(0)
            context_hi(0)
            weight_hi(1)
            copy_v(0, 0)
            over_pairs(act, body)

        @block.vector
        def _(dve):
            def normalise(p):
                wait(dve, lt_ok, p)
                for b in range(PAIR):
                    i = p * PAIR + b
                    dve.tensor_scalar(xn[:, b, :], core.x[:, i, :], core.mv[:, i, 0:1], core.rstd[:, bass.ds(i, 1)],
                                      ALU.subtract, ALU.mult).then_inc(hn_ok, 1)

            def copy_qk(g, u, use):
                dve.wait_ge(proj_ok, u * 6 + 1 + use)
                h, to, bias = (use % 2) * 2, (qT, kT)[use // 2], (bq, bk)[use // 2]
                dve.tensor_tensor(to[:, h:h + 2, :], bank[use % 2][:, :].rearrange("p (h t) -> p h t", h=2),
                                  core.col(bias, g * HG + h, 2)[:, :, None].to_broadcast([P, 2, PT]), ALU.add).then_inc(qk_ok, 1)

            def row_max(u):
                dve.wait_ge(own_ready, u + 1)
                wait(dve, prob_ok, u * 2)
                dve.tensor_copy(own[:, :, :], BL[:, 0:PAIR * HG].rearrange("p (b h) -> p b h", b=PAIR)).then_inc(own_copied, 1)
                for b in range(PAIR):
                    step = u * 6 + b * 3
                    dve.wait_ge(score_ok, u * 2 + 1 + b)
                    dve.tensor_reduce(top[:, b, :], bank[3 + b][:, :].rearrange("p (h k) -> p h k", h=HG), AX_X,
                                      ALU.max).then_inc(top_step, 1)
                    dve.wait_ge(top_step, step + 1)
                    dve.wait_ge(own_copied, u + 1)
                    dve.tensor_tensor(top[:, b, :], top[:, b, :], own[:, b, :], ALU.max).then_inc(top_step, 1)
                    dve.wait_ge(top_step, step + 2)
                    dve.tensor_tensor(own_e[:, b, :], own[:, b, :], top[:, b, :], ALU.subtract).then_inc(top_step, 1)
                    dve.tensor_scalar(shift[:, b, :], top[:, b, :], -SCALE, None, ALU.mult)
                    dve.wait_ge(top_step, step + 3)
                    dve.tensor_scalar(own_e[:, b, :], own_e[:, b, :], SCALE, None, ALU.mult).then_inc(shift_ok, 1)

            def scale_probs(g, u, b):
                dve.wait_ge(exp_ok, u * 2 + 1 + b)
                step = u * 4 + b * 2
                dve.tensor_tensor(total[:, b, :], total[:, b, :], own_e[:, b, :], ALU.add).then_inc(norm_step, 1)
                dve.wait_ge(norm_step, step + 1)
                dve.reciprocal(inv[:, b, :], total[:, b, :]).then_inc(norm_step, 1)
                dve.wait_ge(norm_step, step + 2)
                dve.tensor_tensor(own_p[:, b, g * HG:(g + 1) * HG], own_e[:, b, :], inv[:, b, :], ALU.mult)
                dve.tensor_tensor(prob[:, b, :, :], prob[:, b, :, :], inv[:, b, :, None].to_broadcast([P, HG, P]),
                                  ALU.mult).then_inc(prob_ok, 1)

            def copy_heads(g, u):
                for half in range(2):
                    dve.wait_ge(pv_ok, u * 2 + 1 + half)
                    h = g * HG + half * 2
                    dve.tensor_copy(headT[:, h:h + 2, :], bank[5 + half][:, :].rearrange("p (h t) -> p h t", h=2)).then_inc(head_ok, 1)

            def copy_own(p):
                dve.wait_ge(ot_ok, p + 1)
                dve.tensor_copy(own_pT[:, :], LN[0:H, 0:PT]).then_inc(own_pT_ok, 1)

            def residual(p):
                new_rows(core, dve, res_ok, stat, p, LN[:, :].rearrange("p (b d) -> p b d", b=PAIR), out_ok, obias)

            def body(p):
                first = isinstance(p, int) and p == 0
                last = isinstance(p, int) and p == NP - 1
                for g in range(NHG):
                    u = p * NHG + g
                    g1 = (g + 1) % NHG
                    more = not (last and g == NHG - 1)
                    if g == 0 and not first:
                        copy_own(p - 1)
                    row_max(u)
                    if more:
                        copy_qk(g1, u + 1, 0)
                        copy_qk(g1, u + 1, 1)
                    scale_probs(g, u, 0)
                    if more:
                        copy_qk(g1, u + 1, 2)
                    scale_probs(g, u, 1)
                    if more:
                        copy_qk(g1, u + 1, 3)
                    if g == 0 and not first:
                        residual(p - 1)
                    if g == 1 and not last:
                        normalise(p + 1)
                    if isinstance(u, int) and u == NHG - 1:
                        dve.wait_ge(const_ok, 2)
                        dve.tensor_copy(bvo[:, :], bank[5][0:H, 0:D]).then_inc(const_copied, 1)
                        dve.wait_ge(row_in, DMA)
                        dve.tensor_tensor(obias[:, :], bank[6][:, 0:D], obias[:, :], ALU.add).then_inc(const_copied, 1)
                    copy_heads(g, u)

            rstd_vector(core, dve, root, rstep)
            normalise(0)
            dve.memset(dvz[:, :, :], 0.0).then_inc(dv_step, 1)
            dve.tensor_tensor(own_p[:, 0, :], core.col(bias_v, 0, H), core.col(bv, 0, H), ALU.subtract).then_inc(dv_step, 1)
            dve.wait_ge(dv_step, 2)
            dve.tensor_copy(dvz[:, :, :].rearrange("p a b -> p (a b)")[:, 0:H * H:H + 1], own_p[:, 0, :]).then_inc(dv_step, 1)
            dve.wait_ge(dv_step, 3)
            for use in range(4):
                copy_qk(0, 0, use)
            over_pairs(dve, body)
            copy_own(NP - 1)
            residual(NP - 1)


def narrow_attention(core, stage, kind):
    nc = core.nc
    H, HD = 16, 16
    NHG = H // HG
    TILE_HEADS = P // HD
    SCALE = 0.25
    MASKED = 10000.0 / SCALE
    pre = "L0_xattn_"
    self_attn = kind == "self"
    nln = 1 if self_attn else 2
    ln_s, ln_b = pre + f"ln{nln}_s", pre + f"ln{nln}_b"
    n_mask = 1 if self_attn else NB
    AHEAD = 2
    with ExitStack() as ctx:
        sb = Space(core, stage)
        sem = Signals(core, ctx, f"n{kind}_")
        if self_attn:
            wqkv = core.weight(stage, "w_qkv")
            parts = [wqkv[:, :, i * D:(i + 1) * D] for i in range(3)]
        else:
            wkv = core.weight(stage, "w_kv")
            parts = [core.weight(stage, "w_q"), wkv[:, :, 0:D], wkv[:, :, D:2 * D]]
        wo, out_row = core.weight(stage, "w_out"), core.weight(stage, "row")
        mask = sb("mask", [P, n_mask, P])
        less = sb("less", [P, n_mask, P])
        less_pair = None if self_attn else sb("less_pair", [P, 2, PAIR, P])
        xn = sb("xn", [P, PAIR, D])
        hT = sb("hT", [P, KC, PT])
        kv_in = hT if self_attn else sb("kv_in", [P, KC, PT])
        q_tile = sb("q_tile", [P, KC, PT])
        qT = sb("qT", [P, 2, H, PT])
        kT = sb("kT", [P, 2, KC, PT])
        v = sb("v", [P, 2, PAIR, D])
        prob = sb("prob", [P, NHG, PAIR, HG, P])
        probT = sb("probT", [P, PAIR, HG, P])
        top = sb("top", [P, PAIR, HG])
        shift = sb("shift", [P, 2, PAIR, HG])
        total = sb("total", [P, PAIR, H])
        inv = sb("inv", [P, PAIR, H])
        head = sb("head", [P, PAIR, D])
        headT = sb("headT", [P, KC, PT])
        bank = core.bank
        CTX, OUT = bank[6], bank[7]

        if self_attn:
            bias_q, bias_k, bias_v = [(pre + "b_qkv", i * KC) for i in range(3)]
        else:
            bias_q, bias_k, bias_v = (pre + "b_q", 0), (pre + "b_kv", 0), (pre + "b_kv", KC)

        mask_in = sem("mask_in")
        root, rstep, less_ok = sem("root"), sem("rstep"), sem("less_ok")
        pair_ok = [sem(f"pair_ok{par}") for par in range(2)]
        hn_ok, lt_ok, hT_ok, kv_ok = sem("hn_ok"), sem("lt_ok"), sem("hT_ok"), sem("kv_ok")
        proj_ok = sem("proj_ok")
        q_copied, q_ok, k_ok, v_ok = sem("q_copied"), sem("q_ok"), sem("k_ok"), sem("v_ok")
        score_ok, kept_ok, masked_ok, top_ok, shift_ok = (sem(s) for s in ("score", "kept", "masked", "top", "shift_ok"))
        exp_ok, inv_ok = sem("exp_ok"), sem("inv_ok")
        pt_ok, probT_ok, pv_ok, head_ok = sem("pt_ok"), sem("probT_ok"), sem("pv_ok"), sem("head_ok")
        ht_ok, headT_ok, out_ok, res_ok, stat = sem("ht_ok"), sem("headT_ok"), sem("out_ok"), sem("res_ok"), sem("stat")
        block = ctx.enter_context(nc.Block())

        @block.sync
        def _(sp):
            if self_attn:
                sp.dma_start(mask[:, 0, :], core.dram["mask_self"]).then_inc(mask_in, DMA)
            else:
                sp.dma_start(mask[:, :, :], core.dram["mask_cross"].rearrange("b q k -> q b k")).then_inc(mask_in, DMA)
            core.load(sp, stage)
            if not self_attn:
                def part_of_less(p, par):
                    if not isinstance(p, int) or p > 1:
                        sp.wait_ge(masked_ok, (p - 1) * (2 * NHG))
                    sp.dma_start(less_pair[:, par, :, :], less[:, bass.ds(p * PAIR, PAIR), :]).then_inc(pair_ok[par], DMA)

                def body(p, par):
                    if not (isinstance(p, int) and p == NP - 1):
                        sp.wait_ge(proj_ok, p * 4 + 4)
                        sp.dma_start(kv_in[:, :, :], core.cT[:, :, bass.ts(p + 1, PT)]).then_inc(kv_ok, DMA)
                        part_of_less(p + 1, 1 - par)
                sp.dma_start(kv_in[:, :, :], core.cT[:, :, 0:PT]).then_inc(kv_ok, DMA)
                sp.wait_ge(less_ok, 1)
                part_of_less(0, 0)
                over_steps(sp, body)

        @block.gpsimd
        def _(gp):
            gp.wait_ge(mask_in, DMA)
            gp.tensor_scalar(less[:, :, :], mask[:, :, :], MASKED, -MASKED, ALU.mult, ALU.add).then_inc(less_ok, 1)
            gp.wait_ge(less_ok, 1)

            def spread_q(p, par, t):
                n = p * KC + (t + 1)
                gp.wait_ge(q_copied, n)
                gp.tensor_tensor(qT[:, par, t * TILE_HEADS:(t + 1) * TILE_HEADS, :],
                                 q_tile[:, t, None, :].to_broadcast([P, TILE_HEADS, PT]),
                                 core.head_rows[:, :, None].to_broadcast([P, TILE_HEADS, PT]), ALU.mult).then_inc(q_ok, 1)

            def add_mask(p, par, g):
                for b in range(PAIR):
                    gp.wait_ge(kept_ok, p * (NHG * 2) + (g * 2 + 1 + b))
                    m = less[:, 0:1, :] if self_attn else less_pair[:, par, b:b + 1, :]
                    gp.tensor_tensor(prob[:, g, b, :, :], prob[:, g, b, :, :], m.to_broadcast([P, HG, P]),
                                     ALU.add).then_inc(masked_ok, 1)

            def body(p, par):
                last = isinstance(p, int) and p == NP - 1
                for g in range(NHG):
                    if g < NHG - AHEAD:
                        add_mask(p, par, g + AHEAD)
                    elif not last:
                        if not self_attn and g == NHG - AHEAD:
                            gp.wait_ge(pair_ok[1 - par], (p + 1 - (1 - par)) * (DMA // 2) + DMA)
                        add_mask(p + 1, 1 - par, g + AHEAD - NHG)
                    if not last and g in (0, 1):
                        spread_q(p + 1, 1 - par, g)

            spread_q(0, 0, 0)
            spread_q(0, 0, 1)
            if not self_attn:
                gp.wait_ge(pair_ok[0], DMA)
            for g in range(AHEAD):
                add_mask(0, 0, g)
            over_steps(gp, body)

        @block.tensor
        def _(pe):
            def ln_transpose(p):
                pe.wait_ge(hn_ok, p * PAIR + PAIR)
                wait(pe, v_ok, p)
                for k in range(KC):
                    for b in range(PAIR):
                        mm = pe.transpose(bank[1][:, k * PT + b * P:k * PT + (b + 1) * P], xn[:, b, k * P:(k + 1) * P], core.ident[:, :])
                mm.then_inc(lt_ok, 1)

            def project_tile(to, part, tile, moving):
                for k in range(KC):
                    mm = pe.matmul(to, parts[part][:, k, tile * P:(tile + 1) * P], moving(k), start=(k == 0), stop=(k == KC - 1))
                return mm

            def project_q(p):
                pe.wait_ge(hT_ok, p + 1)
                wait(pe, k_ok, p)
                for t in range(KC):
                    mm = project_tile(bank[0][:, t * PT:(t + 1) * PT], 0, t, lambda k: hT[:, k, :])
                mm.then_inc(proj_ok, 1)

            def project_k(p):
                pe.wait_ge(q_copied, p * KC + KC)
                k_in = (lambda k: hT[:, k, :]) if self_attn else (lambda k: core.cT[:, k, bass.ts(p, PT)])
                for t in range(KC):
                    mm = project_tile(bank[0][:, t * PT:(t + 1) * PT], 1, t, k_in)
                mm.then_inc(proj_ok, 1)

            def project_v(p):
                if not self_attn:
                    pe.wait_ge(kv_ok, p * DMA + DMA)
                for b in range(PAIR):
                    for k in range(KC):
                        mm = pe.matmul(bank[1][:, b * D:(b + 1) * D], kv_in[:, k, b * P:(b + 1) * P], parts[2][:, k, :],
                                       start=(k == 0), stop=(k == KC - 1))
                mm.then_inc(proj_ok, 2)

            def scores(p, par, g):
                u = p * NHG + g
                if g == 0:
                    pe.wait_ge(k_ok, p + 1)
                if g % (NHG // KC) == 0:
                    pe.wait_ge(q_ok, p * KC + (g // (NHG // KC) + 1))
                for b in range(PAIR):
                    wait(pe, kept_ok, u * 2 - 1 + b)
                    for i in range(HG):
                        h = g * HG + i
                        mm = pe.matmul(bank[2 + b][:, i * P:(i + 1) * P], qT[:, par, h, b * P:(b + 1) * P],
                                       kT[:, par, h // TILE_HEADS, b * P:(b + 1) * P], start=True, stop=True)
                    mm.then_inc(score_ok, 1)

            def scores_ahead(p, par, g):
                if g < NHG - AHEAD:
                    scores(p, par, g + AHEAD)
                elif not (isinstance(p, int) and p == NP - 1):
                    scores(p + 1, 1 - par, g + AHEAD - NHG)

            def prob_transpose(u, g):
                for b in range(PAIR):
                    pe.wait_ge(exp_ok, u * 2 + 1 + b)
                    wait(pe, probT_ok, u * 2 - 1 + b)
                    for i in range(HG):
                        mm = pe.transpose(bank[4 + b][:, i * P:(i + 1) * P], prob[:, g, b, i, :], core.ident[:, :])
                    mm.then_inc(pt_ok, 1)

            def weigh_values(p, par, g):
                u = p * NHG + g
                if g == 0:
                    pe.wait_ge(v_ok, p + 1)
                    wait(pe, head_ok, p)
                for b in range(PAIR):
                    pe.wait_ge(probT_ok, u * 2 + 1 + b)
                    for i in range(HG):
                        h = g * HG + i
                        mm = pe.matmul(CTX[:, b * D + h * HD:b * D + (h + 1) * HD], probT[:, b, i, :], v[:, par, b, h * HD:(h + 1) * HD],
                                       start=True, stop=True)
                mm.then_inc(pv_ok, 1)

            def head_transpose(p):
                pe.wait_ge(head_ok, p + 1)
                for k in range(KC):
                    for b in range(PAIR):
                        mm = pe.transpose(OUT[:, k * PT + b * P:k * PT + (b + 1) * P], head[:, b, k * P:(k + 1) * P], core.ident[:, :])
                mm.then_inc(ht_ok, 1)

            def project_out(p):
                pe.wait_ge(headT_ok, p + 1)
                for b in range(PAIR):
                    for k in range(KC):
                        mm = pe.matmul(OUT[:, b * D:(b + 1) * D], headT[:, k, b * P:(b + 1) * P], wo[:, k, :], start=(k == 0), stop=(k == KC - 1))
                mm.then_inc(out_ok, 1)

            def body(p, par):
                first = isinstance(p, int) and p == 0
                last = isinstance(p, int) and p == NP - 1
                for g in range(NHG):
                    scores_ahead(p, par, g)
                    if g > 0:
                        weigh_values(p, par, g - 1)
                    elif not first:
                        weigh_values(p - 1, 1 - par, NHG - 1)
                    if g == 0 and not last:
                        project_q(p + 1)
                        project_k(p + 1)
                    if g == 1:
                        if not last:
                            project_v(p + 1)
                        if not first:
                            head_transpose(p - 1)
                    if g == 2 and not first:
                        project_out(p - 1)
                    if g == NHG - 1:
                        if not (isinstance(p, int) and p >= NP - 2):
                            ln_transpose(p + 2)
                        if not first:
                            pe.wait_ge(res_ok, p * 2 - 1)
                    prob_transpose(p * NHG + g, g)

            core.wait_loaded(pe, stage, *(["w_qkv"] if self_attn else ["w_q", "w_kv"]))
            ln_transpose(0)
            project_q(0)
            project_k(0)
            project_v(0)
            ln_transpose(1)
            for g in range(AHEAD):
                scores(0, 0, g)
            core.wait_loaded(pe, stage, "w_out")
            over_steps(pe, body)
            weigh_values(NP - 1, 1, NHG - 1)
            head_transpose(NP - 1)
            project_out(NP - 1)

        @block.scalar
        def _(act):
            def layer_norm(p):
                act.wait_ge(lt_ok, p + 1)
                for k in range(KC):
                    done = act.activation(hT[:, k, :], bank[1][:, k * PT:(k + 1) * PT], ACT.Identity,
                                          scale=core.col(ln_s, k), bias=core.col(ln_b, k))
                done.then_inc(hT_ok, 1)

            def copy_q(p):
                act.wait_ge(proj_ok, p * 4 + 1)
                wait(act, q_ok, p * KC)
                for t in range(KC):
                    act.activation(q_tile[:, t, :], bank[0][:, t * PT:(t + 1) * PT], ACT.Identity,
                                   bias=core.col(bias_q[0], bias_q[1] + t)).then_inc(q_copied, 1)

            def copy_v(p, par):
                act.wait_ge(proj_ok, p * 4 + 4)
                act.activation(v[:, par, :, :], bank[1][:, :].rearrange("p (b d) -> p b d", b=PAIR), ACT.Copy).then_inc(v_ok, 1)

            def copy_head(p):
                act.wait_ge(ht_ok, p + 1)
                for k in range(KC):
                    done = act.activation(headT[:, k, :], OUT[:, k * PT:(k + 1) * PT], ACT.Identity, bias=core.col(bias_v[0], bias_v[1] + k))
                done.then_inc(headT_ok, 1)

            def copy_probs(u):
                for b in range(PAIR):
                    act.wait_ge(pt_ok, u * 2 + 1 + b)
                    wait(act, pv_ok, u)
                    act.activation(probT[:, b, :, :], bank[4 + b][:, :].rearrange("p (h q) -> p h q", h=HG), ACT.Copy).then_inc(probT_ok, 1)

            def body(p, par):
                first = isinstance(p, int) and p == 0
                last = isinstance(p, int) and p == NP - 1
                for g in range(NHG):
                    u = p * NHG + g
                    if not (first and g == 0):
                        copy_probs(u - 1)
                    act.wait_ge(shift_ok, u + 1)
                    for b in range(PAIR):
                        for i in range(HG):
                            done = act.activation(prob[:, g, b, i, :], prob[:, g, b, i, :], ACT.Exp, scale=SCALE,
                                                  bias=shift[:, g % 2, b, i:i + 1], accum_out=total[:, b, g * HG + i:g * HG + i + 1])
                        done.then_inc(exp_ok, 1)
                    if g == 0 and not last:
                        copy_q(p + 1)
                    if g == 1:
                        if not last:
                            copy_v(p + 1, 1 - par)
                        if not first:
                            copy_head(p - 1)
                    if g == NHG - 1 and not (isinstance(p, int) and p >= NP - 2):
                        layer_norm(p + 2)

            rstd_scalar(core, act, root)
            layer_norm(0)
            copy_q(0)
            copy_v(0, 0)
            layer_norm(1)
            over_steps(act, body)
            copy_probs(NP * NHG - 1)
            copy_head(NP - 1)

        @block.vector
        def _(dve):
            def normalise(p):
                wait(dve, lt_ok, p)
                for b in range(PAIR):
                    i = p * PAIR + b
                    dve.tensor_scalar(xn[:, b, :], core.x[:, i, :], core.mv[:, i, 0:1], core.rstd[:, bass.ds(i, 1)],
                                      ALU.subtract, ALU.mult).then_inc(hn_ok, 1)

            def keep_scores(p, par, g):
                u = p * NHG + g
                if not (isinstance(p, int) and p == 0):
                    dve.wait_ge(pt_ok, u * 2 - 2 * NHG + 2)
                for b in range(PAIR):
                    dve.wait_ge(score_ok, u * 2 + 1 + b)
                    m = mask[:, 0:1, :] if self_attn else mask[:, bass.ds(p * PAIR + b, 1), :]
                    dve.tensor_tensor(prob[:, g, b, :, :], bank[2 + b][:, :].rearrange("p (h k) -> p h k", h=HG),
                                      m.to_broadcast([P, HG, P]), ALU.mult).then_inc(kept_ok, 1)

            def row_max(u, g):
                for b in range(PAIR):
                    dve.wait_ge(masked_ok, u * 2 + 1 + b)
                    wait(dve, shift_ok, u)
                    dve.tensor_reduce(top[:, b, :], prob[:, g, b, :, :], AX_X, ALU.max).then_inc(top_ok, 1)
                dve.wait_ge(top_ok, u * 2 + 2)
                wait(dve, exp_ok, u * 2 - 2)
                dve.tensor_scalar(shift[:, g % 2, :, :], top[:, :, :], -SCALE, None, ALU.mult).then_inc(shift_ok, 1)

            def invert(u, g):
                dve.wait_ge(exp_ok, u * 2 + 2)
                dve.reciprocal(inv[:, :, g * HG:(g + 1) * HG], total[:, :, g * HG:(g + 1) * HG]).then_inc(inv_ok, 1)

            def copy_k(p, par):
                dve.wait_ge(proj_ok, p * 4 + 2)
                dve.tensor_tensor(kT[:, par, :, :], bank[0][:, :].rearrange("p (k t) -> p k t", k=KC),
                                  core.col(bias_k[0], bias_k[1], KC)[:, :, None].to_broadcast([P, KC, PT]), ALU.add).then_inc(k_ok, 1)

            def divide(p):
                dve.wait_ge(pv_ok, p * NHG + NHG)
                dve.wait_ge(inv_ok, p * NHG + NHG)
                wait(dve, ht_ok, p)
                dve.tensor_tensor(head[:, :, :].rearrange("p b (h d) -> p (b h) d", d=HD),
                                  CTX[:, :].rearrange("p (n d) -> p n d", d=HD),
                                  inv[:, :, :].rearrange("p b h -> p (b h)")[:, :, None].to_broadcast([P, PAIR * H, HD]), ALU.mult).then_inc(head_ok, 1)

            def body(p, par):
                first = isinstance(p, int) and p == 0
                last = isinstance(p, int) and p == NP - 1
                for g in range(NHG):
                    u = p * NHG + g
                    if g < NHG - AHEAD:
                        keep_scores(p, par, g + AHEAD)
                    elif not last:
                        keep_scores(p + 1, 1 - par, g + AHEAD - NHG)
                    if not (last and g == NHG - 1):
                        row_max(u + 1, (g + 1) % NHG)
                    if g == 0 and not last:
                        copy_k(p + 1, 1 - par)
                    if g > 0:
                        invert(u - 1, g - 1)
                    elif not first:
                        invert(u - 1, NHG - 1)
                        divide(p - 1)
                    if g == 2 and not (isinstance(p, int) and p >= NP - 2):
                        normalise(p + 2)
                    if g == NHG - 1 and not first:
                        new_rows(core, dve, res_ok, stat, p - 1, OUT[:, :].rearrange("p (b d) -> p b d", b=PAIR), out_ok, out_row)

            rstd_vector(core, dve, root, rstep)
            normalise(0)
            dve.wait_ge(mask_in, DMA)
            core.wait_loaded(dve, stage, "row")
            copy_k(0, 0)
            normalise(1)
            for g in range(AHEAD):
                keep_scores(0, 0, g)
            row_max(0, 0)
            over_steps(dve, body)
            invert(NP * NHG - 1, NHG - 1)
            divide(NP - 1)
            new_rows(core, dve, res_ok, stat, NP - 1, OUT[:, :].rearrange("p (b d) -> p b d", b=PAIR), out_ok, out_row)


def mlp(core, stage, ln_s, ln_b, b1, gelu):
    nc = core.nc
    NF = 4 * D // P
    with ExitStack() as ctx:
        sb = Space(core, stage)
        sem = Signals(core, ctx, f"m{stage}_")
        w1, w2, out_row = (core.weight(stage, w) for w in ("w1", "w2", "row"))
        xn = sb("xn", [P, PAIR, D])
        hT = sb("hT", [P, KC, PT])
        gT = sb("gT", [P, 2, NF, PT])
        bank = core.bank
        root, rstep = sem("root"), sem("rstep")
        hn_ok, lt_ok, hT_ok = sem("hn_ok"), sem("lt_ok"), sem("hT_ok")
        up_ok, gelu_ok, out_ok, res_ok, stat = sem("up_ok"), sem("gelu_ok"), sem("out_ok"), sem("res_ok"), sem("stat")
        block = ctx.enter_context(nc.Block())

        def within(p, ahead):
            return not isinstance(p, int) or p + ahead < NP

        @block.sync
        def _(sp):
            core.load(sp, stage)

        @block.tensor
        def _(pe):
            def ln_transpose(p):
                pe.wait_ge(hn_ok, p * PAIR + PAIR)
                wait(pe, hT_ok, p)
                for k in range(KC):
                    for b in range(PAIR):
                        mm = pe.transpose(bank[6][:, k * PT + b * P:k * PT + (b + 1) * P], xn[:, b, k * P:(k + 1) * P], core.ident[:, :])
                mm.then_inc(lt_ok, 1)

            def up(p):
                pe.wait_ge(hT_ok, p + 1)
                for f in range(NF):
                    if f % 2 == 0:
                        wait(pe, gelu_ok, (p - 1) * NF + f + 2)
                    at = bank[f // 2][:, (f % 2) * PT:(f % 2 + 1) * PT]
                    for k in range(KC):
                        mm = pe.matmul(at, w1[:, k, f * P:(f + 1) * P], hT[:, k, :], start=(k == 0), stop=(k == KC - 1))
                    if f % 2:
                        mm.then_inc(up_ok, 1)

            def down(p, par):
                pe.wait_ge(gelu_ok, p * NF + NF)
                wait(pe, res_ok, p * 2 - 3)
                for b in range(PAIR):
                    for f in range(NF):
                        mm = pe.matmul(bank[4 + par][:, b * D:(b + 1) * D], gT[:, par, f, b * P:(b + 1) * P], w2[:, f, :],
                                       start=(f == 0), stop=(f == NF - 1))
                mm.then_inc(out_ok, 1)

            def body(p, par):
                if within(p, 1):
                    up(p + 1)
                if within(p, 2):
                    ln_transpose(p + 2)
                if isinstance(p, int) and p == 0:
                    core.wait_loaded(pe, stage, "w2")
                down(p, par)

            ln_transpose(0)
            core.wait_loaded(pe, stage, "w1")
            up(0)
            ln_transpose(1)
            over_steps(pe, body)

        @block.scalar
        def _(act):
            def layer_norm(p):
                act.wait_ge(lt_ok, p + 1)
                for k in range(KC):
                    done = act.activation(hT[:, k, :], bank[6][:, k * PT:(k + 1) * PT], ACT.Identity,
                                          scale=core.col(ln_s, k), bias=core.col(ln_b, k))
                done.then_inc(hT_ok, 1)

            def activate(p, par):
                for f in range(NF):
                    if f % 2 == 0:
                        act.wait_ge(up_ok, p * (NF // 2) + f // 2 + 1)
                    act.activation(gT[:, par, f, :], bank[f // 2][:, (f % 2) * PT:(f % 2 + 1) * PT], gelu,
                                   bias=core.col(b1, f)).then_inc(gelu_ok, 1)

            def body(p, par):
                if within(p, 1):
                    activate(p + 1, 1 - par)
                if within(p, 2):
                    layer_norm(p + 2)

            rstd_scalar(core, act, root)
            layer_norm(0)
            activate(0, 0)
            layer_norm(1)
            over_steps(act, body)

        @block.vector
        def _(dve):
            def normalise(p):
                wait(dve, lt_ok, p)
                for b in range(PAIR):
                    i = p * PAIR + b
                    dve.tensor_scalar(xn[:, b, :], core.x[:, i, :], core.mv[:, i, 0:1], core.rstd[:, bass.ds(i, 1)],
                                      ALU.subtract, ALU.mult).then_inc(hn_ok, 1)

            def body(p, par):
                if within(p, 2):
                    normalise(p + 2)
                new_rows(core, dve, res_ok, stat, p, bank[4 + par][:, :].rearrange("p (b d) -> p b d", b=PAIR), out_ok, out_row)

            rstd_vector(core, dve, root, rstep)
            normalise(0)
            normalise(1)
            core.wait_loaded(dve, stage, "row")
            over_steps(dve, body)


def single_attention(core, stage):
    nc = core.nc
    SCALE = float(D) ** -0.5
    pre = "L2_xattn_"
    with ExitStack() as ctx:
        sb = Space(core, stage)
        sem = Signals(core, ctx, f"s_")
        wq, wk, wv, wo, alpha = (core.weight(stage, w) for w in ("w_q", "w_k", "w_v", "w_o", "alpha"))
        x_in = sb("x_in", [P, PAIR, D])
        xT, kv_in, qT, kT = (sb(t, [P, KC, PT]) for t in ("xT", "kv_in", "qT", "kT"))
        v = sb("v", [P, PAIR, D])
        prob, probT = sb("prob", [P, PAIR, P]), sb("probT", [P, PAIR, P])
        headT = sb("headT", [P, KC, PT])
        scaled = sb("scaled", [P, PAIR, D])
        top, shift, total, inv = (sb(t, [P, PAIR]) for t in ("top", "shift", "total", "inv"))
        bank = core.bank
        xi_ok, xt_ok, xT_ok, kv_ok = sem("xi_ok"), sem("xt_ok"), sem("xT_ok"), sem("kv_ok")
        q_ready, k_ready, v_ready = sem("q_ready"), sem("k_ready"), sem("v_ready")
        q_ok, k_ok, v_ok = sem("q_ok"), sem("k_ok"), sem("v_ok")
        score_ok, top_ok, shift_ok, exp_ok, inv_ok, prob_ok = (sem(s) for s in ("score", "top_ok", "shift_ok", "exp", "inv_ok", "prob_ok"))
        pt_ok, probT_ok, pv_ok, headT_ok, out_ok = (sem(s) for s in ("pt", "probT_ok", "pv", "headT_ok", "out"))
        scaled_ok, res_ok, stat = sem("scaled_ok"), sem("res_ok"), sem("stat")
        block = ctx.enter_context(nc.Block())
        halves = lambda t, n: t[:, :].rearrange("p (k t) -> p k t", k=n)

        @block.sync
        def _(sp):
            core.load(sp, stage)

            def body(p):
                wait(sp, v_ready, p)
                sp.dma_start(kv_in[:, :, :], core.cT[:, :, bass.ts(p, PT)]).then_inc(kv_ok, DMA)
            over_pairs(sp, body)

        @block.tensor
        def _(pe):
            def x_transpose(p):
                pe.wait_ge(xi_ok, p + 1)
                wait(pe, xT_ok, p)
                for k in range(KC):
                    for b in range(PAIR):
                        mm = pe.transpose(bank[0][:, k * PT + b * P:k * PT + (b + 1) * P], x_in[:, b, k * P:(k + 1) * P], core.ident[:, :])
                mm.then_inc(xt_ok, 1)

            def project(p, to, w, moving, ready):
                for t in range(KC):
                    for k in range(KC):
                        mm = pe.matmul(to[:, t * PT:(t + 1) * PT], w[:, k, t * P:(t + 1) * P], moving(k), start=(k == 0), stop=(k == KC - 1))
                mm.then_inc(ready, 1)

            def project_qk(p):
                pe.wait_ge(xT_ok, p + 1)
                wait(pe, q_ok, p)
                project(p, bank[1], wq, lambda k: xT[:, k, :], q_ready)
                wait(pe, k_ok, p)
                project(p, bank[2], wk, lambda k: core.cT[:, k, bass.ts(p, PT)], k_ready)

            def project_v(p):
                pe.wait_ge(kv_ok, p * DMA + DMA)
                wait(pe, v_ok, p)
                for b in range(PAIR):
                    for k in range(KC):
                        mm = pe.matmul(bank[3][:, b * D:(b + 1) * D], kv_in[:, k, b * P:(b + 1) * P], wv[:, k, :], start=(k == 0), stop=(k == KC - 1))
                mm.then_inc(v_ready, 1)

            def scores(p):
                pe.wait_ge(q_ok, p + 1)
                pe.wait_ge(k_ok, p + 1)
                wait(pe, exp_ok, p)
                for b in range(PAIR):
                    for k in range(KC):
                        mm = pe.matmul(bank[4][:, b * P:(b + 1) * P], qT[:, k, b * P:(b + 1) * P], kT[:, k, b * P:(b + 1) * P],
                                       start=(k == 0), stop=(k == KC - 1))
                mm.then_inc(score_ok, 1)

            def attend(p):
                pe.wait_ge(prob_ok, p + 1)
                for b in range(PAIR):
                    mm = pe.transpose(bank[5][:, b * P:(b + 1) * P], prob[:, b, :], core.ident[:, :])
                mm.then_inc(pt_ok, 1)
                pe.wait_ge(probT_ok, p + 1)
                pe.wait_ge(v_ok, p + 1)
                wait(pe, headT_ok, p)
                for k in range(KC):
                    for b in range(PAIR):
                        mm = pe.matmul(bank[6][:, k * PT + b * P:k * PT + (b + 1) * P], v[:, b, k * P:(k + 1) * P], probT[:, b, :], start=True, stop=True)
                mm.then_inc(pv_ok, 1)

            def project_out(p):
                pe.wait_ge(headT_ok, p + 1)
                wait(pe, scaled_ok, p)
                for b in range(PAIR):
                    for k in range(KC):
                        mm = pe.matmul(bank[7][:, b * D:(b + 1) * D], headT[:, k, b * P:(b + 1) * P], wo[:, k, :], start=(k == 0), stop=(k == KC - 1))
                mm.then_inc(out_ok, 1)

            def body(p):
                last = isinstance(p, int) and p == NP - 1
                if not last:
                    x_transpose(p + 1)
                scores(p)
                if not last:
                    project_qk(p + 1)
                attend(p)
                if not last:
                    project_v(p + 1)
                project_out(p)

            x_transpose(0)
            core.wait_loaded(pe, stage, "w_q", "w_k", "w_v", "w_o")
            project_qk(0)
            project_v(0)
            over_pairs(pe, body)

        @block.scalar
        def _(act):
            def copy_x(p):
                act.wait_ge(xt_ok, p + 1)
                act.activation(xT[:, :, :], halves(bank[0], KC), ACT.Copy).then_inc(xT_ok, 1)

            def copy_v(p):
                act.wait_ge(v_ready, p + 1)
                act.activation(v[:, :, :], halves(bank[3], PAIR), ACT.Copy).then_inc(v_ok, 1)

            def body(p):
                last = isinstance(p, int) and p == NP - 1
                if not last:
                    copy_x(p + 1)
                act.wait_ge(shift_ok, p + 1)
                for b in range(PAIR):
                    done = act.activation(prob[:, b, :], bank[4][:, b * P:(b + 1) * P], ACT.Exp, scale=SCALE, bias=shift[:, b:b + 1],
                                          accum_out=total[:, b:b + 1])
                done.then_inc(exp_ok, 1)
                act.wait_ge(pt_ok, p + 1)
                act.activation(probT[:, :, :], bank[5][:, 0:PT].rearrange("p (b t) -> p b t", b=PAIR), ACT.Copy).then_inc(probT_ok, 1)
                if not last:
                    copy_v(p + 1)

            copy_x(0)
            copy_v(0)
            over_pairs(act, body)

        @block.vector
        def _(dve):
            def fetch(p):
                wait(dve, xt_ok, p)
                dve.tensor_scalar(x_in[:, :, :], core.x[:, bass.ds(p * PAIR, PAIR), :], 1.0, None, ALU.mult).then_inc(xi_ok, 1)

            def copy_qk(p):
                dve.wait_ge(q_ready, p + 1)
                dve.tensor_copy(qT[:, :, :], halves(bank[1], KC)).then_inc(q_ok, 1)
                dve.wait_ge(k_ready, p + 1)
                dve.tensor_copy(kT[:, :, :], halves(bank[2], KC)).then_inc(k_ok, 1)

            def body(p):
                last = isinstance(p, int) and p == NP - 1
                if not last:
                    fetch(p + 1)
                dve.wait_ge(score_ok, p + 1)
                dve.tensor_reduce(top[:, :], bank[4][:, 0:PT].rearrange("p (b t) -> p b t", b=PAIR), AX_X, ALU.max).then_inc(top_ok, 1)
                dve.wait_ge(top_ok, p + 1)
                dve.tensor_scalar(shift[:, :], top[:, :], -SCALE, None, ALU.mult).then_inc(shift_ok, 1)
                if not last:
                    copy_qk(p + 1)
                dve.wait_ge(exp_ok, p + 1)
                dve.reciprocal(inv[:, :], total[:, :]).then_inc(inv_ok, 1)
                dve.wait_ge(inv_ok, p + 1)
                dve.tensor_tensor(prob[:, :, :], prob[:, :, :], inv[:, :, None].to_broadcast([P, PAIR, P]), ALU.mult).then_inc(prob_ok, 1)
                dve.wait_ge(pv_ok, p + 1)
                dve.tensor_copy(headT[:, :, :], halves(bank[6], KC)).then_inc(headT_ok, 1)
                dve.wait_ge(out_ok, p + 1)
                dve.tensor_scalar(scaled[:, :, :], halves(bank[7], PAIR), alpha[:, 0:1], None, ALU.mult).then_inc(scaled_ok, 1)
                new_rows(core, dve, res_ok, stat, p, scaled[:, :, :], scaled_ok)

            fetch(0)
            core.wait_loaded(dve, stage, "alpha")
            copy_qk(0)
            over_pairs(dve, body)


def recurrence(core, stage):
    nc = core.nc
    J = 8
    HT = P // J
    F = 5
    FK, FW, FV, FR, FG = range(F)
    R = 32
    RD = 64
    UNITS = KC * PAIR
    pre = "L3_xattn_"
    with ExitStack() as ctx:
        sb = Space(core, stage)
        sem = Signals(core, ctx, f"r_")
        maa_w1, maa_w2, maa_w2g, td_w1, td_w2 = (core.weight(stage, n) for n in ("maa_w1", "maa_w2", "maa_w2g", "td_w1", "td_w2"))
        w = {n: core.weight(stage, n) for n in ("Wk", "Wv", "Wr", "Wg", "Wo", "Wfk", "Wfr", "Wfv")}
        state0 = core.weight(stage, "state0").rearrange("p (k b j) -> p k b j", k=KC, b=NB)
        gn_rows = sb("gn_rows", [P, 2, D])
        pick = sb("pick", [P, J, P])
        head_sum = sb("head_sum", [P, HT])
        xn = sb("xn", [P, PAIR, D])
        xa = sb("xa", [P, KC, PAIR, P + 1])
        sx = sb("sx", [P, KC, PAIR, P])
        xmaa = sb("xmaa", [P, KC, PAIR, P])
        low, low_g = sb("low", [P, PT]), sb("low_g", [R, PT])
        mixed = sb("mixed", [P, F, KC, PT])
        td_low = sb("td_low", [RD, PT])
        kT, vT, rT = (sb(n, [P, 2, KC, PT]) for n in ("kT", "vT", "rT"))
        rate = sb("rate", [P, 2, KC, PT])
        g_tanh = sb("g_tanh", [P, PAIR, D])
        gate = sb("gate", [P, 2, PAIR, D])
        decay = sb("decay", [P, 2, J, P + 1])
        kv = sb("kv", [P, J, P + 1])
        states = sb("states", [P, J, P + 1])
        prod = sb("prod", [P, 2, J, P])
        og = sb("og", [P, UNITS, HT, J])
        sq = sb("sq", [P, UNITS, HT, J])
        msum, mean, vsum, gstd, grstd = (sb(n, [P, UNITS * HT]) for n in ("msum", "mean", "vsum", "gstd", "grstd"))
        zT = sb("zT", [P, KC, PT])
        std2, rstd2 = sb("std2", [P, PAIR]), sb("rstd2", [P, PAIR])
        xn2 = sb("xn2", [P, PAIR, D])
        xc = sb("xc", [P, KC, PAIR, P + 1])
        sx2 = sb("sx2", [P, KC, PAIR, P])
        xk2, xr2 = sb("xk2", [P, KC, PT]), sb("xr2", [P, KC, PT])
        relu, kkT = sb("relu", [P, KC, PT]), sb("kkT", [P, KC, PT])
        r_tanh = sb("r_tanh", [P, PAIR, D])
        gated = sb("gated", [P, PAIR, D])
        result = sb("result", [P, PAIR, D])
        bank = core.bank
        VB = core.banks[:, 0:2, :].rearrange("p n c -> p (n c)").rearrange("p (j t) -> p j t", j=J)
        OG = bank[2]

        gn_in = sem("gn_in")
        root, rstep, made = sem("root"), sem("rstep"), sem("made")
        TILES = ["xa", "low", "td", "k", "r", "v", "rate", "g", "z", "out", "xc", "kk", "rr", "ff"]
        ready = {n: sem(n + "_ready") for n in TILES}
        read = {n: sem(n + "_read") for n in TILES}
        f_ready, f_read = sem("f_ready"), sem("f_read")
        xn_ok, first_ok, xmaa_ok, mix_ok = sem("xn_ok"), sem("first_ok"), sem("xmaa_ok"), sem("mix_ok")
        mid_ok = sem("mid_ok")
        vb_ready, kv_ok, decay_ok, scan_ok, q_ok, prod_ok, sum_ready = (sem(n) for n in ("vb", "kv_ok", "decay_ok", "scan_ok", "q_ok", "prod_ok", "sum"))
        og_read, gn_step, vsum_ok, gstd_ok, z_ok = sem("og_read"), sem("gn_step"), sem("vsum_ok"), sem("gstd_ok"), sem("z_ok")
        st_ok, mv2_ok, std2_ok, c_step, xn2_ok, c_first = sem("st_ok"), sem("mv2_ok"), sem("std2_ok"), sem("c_step"), sem("xn2_ok"), sem("c_first")
        xk_step, xk_ok, relu_ok, ff_step, result_ok, stored = (sem(n) for n in ("xk_step", "xk_ok", "relu_ok", "ff_step", "result_ok", "stored"))
        g_tanh_ok = sem("g_tanh_ok")
        block = ctx.enter_context(nc.Block())
        ctx_rows = core.cT[:, :, :].rearrange("p k (b t) -> p k b t", b=NB)

        def static(p):
            return isinstance(p, int)

        def exists(p):
            return not static(p) or 0 <= p < NP

        def over_slots(eng, slot):
            over_steps(eng, slot)
            slot(NP, NP % 2)

        flat = lambda t: t.rearrange("p k b t -> p k (b t)")
        halves = lambda t, n=2: t[:, :].rearrange("p (k t) -> p k t", k=n)

        @block.sync
        def _(sp):
            core.load(sp, stage)
            for i, n in enumerate(("gn_w", "gn_b")):
                sp.dma_start(gn_rows[:, i, :], core.dram["row_" + n]).then_inc(gn_in, DMA)

            def slot(p, par):
                if exists(p - 1):
                    sp.wait_ge(result_ok, p)
                    sp.dma_start(core.out[bass.ds((p - 1) * PAIR, PAIR), :, :].rearrange("b t d -> t b d"), result[:, :, :]).then_inc(stored, DMA)
            over_slots(sp, slot)
            sp.wait_ge(stored, NP * DMA)

        @block.gpsimd
        def _(gp):
            gp.memset(pick[:, :, :], 0.0).then_inc(made, 1)
            gp.memset(head_sum[:, :], 1.0).then_inc(made, 1)
            gp.memset(decay[:, :, :, :], 0.0).then_inc(made, 1)
            gp.wait_ge(made, 3)
            gp.affine_select(out=pick[:, :, :].rearrange("p j (h i) -> p j h i", i=J), in_=pick[:, :, :].rearrange("p j (h i) -> p j h i", i=J),
                             compare_op=ALU.not_equal, fill=1.0, base=0, pattern=[[-1, J], [-J, HT], [0, J]], channel_multiplier=1).then_inc(made, 1)
            gp.affine_select(out=head_sum[:, :], in_=head_sum[:, :], compare_op=ALU.is_ge, fill=0.0,
                             base=0, pattern=[[-J, HT]], channel_multiplier=1).then_inc(made, 1)
            gp.wait_ge(made, 5)
            gp.affine_select(out=head_sum[:, :], in_=head_sum[:, :], compare_op=ALU.is_ge, fill=0.0,
                             base=J - 1, pattern=[[J, HT]], channel_multiplier=-1).then_inc(made, 1)

            def times_r(p, par, s):
                k, b = s // PAIR, s % PAIR
                gp.wait_ge(read["r"], p + 1)
                gp.wait_ge(q_ok, p * UNITS + (s + 1))
                gp.tensor_tensor(prod[:, s % 2, :, :], prod[:, s % 2, :, :],
                                 rT[:, par, k, b * P:(b + 1) * P][:, None, :].to_broadcast([P, J, P]), ALU.mult).then_inc(prod_ok, 1)

            def add_xa(a):
                for f in range(F):
                    gp.wait_ge(f_read, a * F + (f + 1))
                    gp.tensor_tensor(mixed[:, f, :, :].rearrange("p k (b t) -> p k b t", b=PAIR), mixed[:, f, :, :].rearrange("p k (b t) -> p k b t", b=PAIR),
                                     xa[:, :, :, 1:P + 1], ALU.add).then_inc(mix_ok, 1)

            def slot(p, par):
                for s in range(UNITS):
                    if exists(p):
                        if s == UNITS - 1 and exists(p + 1):
                            add_xa(p + 1)
                        times_r(p, par, s)
            add_xa(0)
            over_steps(gp, slot)

        @block.tensor
        def _(pe):
            def spread_v(p, par, s):
                k, b = s // PAIR, s % PAIR
                pe.wait_ge(read["v"], p + 1)
                if not (static(p) and p == 0 and s == 0):
                    pe.wait_ge(kv_ok, p * (2 * UNITS) + (2 * s - 1))
                for j in range(J):
                    mm = pe.matmul(VB[:, j, :], pick[:, j, :], vT[:, par, k, b * P:(b + 1) * P], start=True, stop=True)
                mm.then_inc(vb_ready, 1)

            def sum_heads(p, s):
                pe.wait_ge(prod_ok, p * UNITS + (s + 1))
                if s == 0:
                    wait(pe, og_read, p)
                b, k = s % PAIR, s // PAIR
                for j in range(J):
                    at = (b * KC + k) * P + j * HT
                    mm = pe.matmul(OG[:, at:at + HT], prod[:, s % 2, j, :], head_sum[:, :], start=True, stop=True)
                mm.then_inc(sum_ready, 1)

            def transposes(to, src):
                for k in range(KC):
                    for b in range(PAIR):
                        mm = pe.transpose(to[:, k * PT + b * P:k * PT + (b + 1) * P], src[:, b, k * P:(k + 1) * P], core.ident[:, :])
                return mm

            def feature_major(to, weight, moving):
                for t in range(KC):
                    for k in range(KC):
                        mm = pe.matmul(to[:, t * PT:(t + 1) * PT], weight[:, k, t * P:(t + 1) * P], moving[:, k, :], start=(k == 0), stop=(k == KC - 1))
                return mm

            def token_major(to, source, weight):
                for b in range(PAIR):
                    for k in range(KC):
                        mm = pe.matmul(to[:, b * D:(b + 1) * D], source[:, k, b * P:(b + 1) * P], weight[:, k, :], start=(k == 0), stop=(k == KC - 1))
                return mm

            def a_transpose(a):
                pe.wait_ge(xn_ok, a * PAIR + PAIR)
                wait(pe, read["v"], a)
                transposes(bank[3], xn).then_inc(ready["xa"], 1)

            def a_low(a):
                pe.wait_ge(xmaa_ok, a * KC + KC)
                pe.wait_ge(read["xa"], a + 1)
                for m0, m1 in ((0, P), (P, F * R)):
                    at = 0 if m0 == 0 else PT
                    for k in range(KC):
                        mm = pe.matmul(bank[3][0:m1 - m0, at:at + PT], maa_w1[:, k, m0:m1], flat(xmaa[:, :, :, :])[:, k, :], start=(k == 0), stop=(k == KC - 1))
                mm.then_inc(ready["low"], 1)

            def a_mix(a):
                pe.wait_ge(read["low"], a + 1)
                for f in range(F):
                    if f == 0:
                        wait(pe, read["g"], a)
                    elif f == 1:
                        wait(pe, read["rate"], a)
                    else:
                        pe.wait_ge(f_read, a * F + (f - 1))
                    r0 = R * f if f < FG else 0
                    src, rhs = (maa_w2, low) if f < FG else (maa_w2g, low_g)
                    for k in range(KC):
                        mm = pe.matmul(bank[4 + f % 2][:, k * PT:(k + 1) * PT], src[r0:r0 + R, k * P:(k + 1) * P], rhs[r0:r0 + R, :], start=True, stop=True)
                    mm.then_inc(f_ready, 1)

            def a_project(a):
                pe.wait_ge(mix_ok, a * F + FW + 1)
                for k in range(KC):
                    mm = pe.matmul(bank[3][0:RD, 0:PT], td_w1[:, k, :], mixed[:, FW, k, :], start=(k == 0), stop=(k == KC - 1))
                mm.then_inc(ready["td"], 1)
                pe.wait_ge(f_read, a * F + F)
                feature_major(bank[5], w["Wk"], mixed[:, FK, :, :]).then_inc(ready["k"], 1)
                pe.wait_ge(mix_ok, a * F + FR + 1)
                feature_major(bank[4], w["Wr"], mixed[:, FR, :, :]).then_inc(ready["r"], 1)
                pe.wait_ge(read["td"], a + 1)
                feature_major(bank[3], w["Wv"], mixed[:, FV, :, :]).then_inc(ready["v"], 1)
                pe.wait_ge(read["k"], a + 1)
                for t in range(KC):
                    mm = pe.matmul(bank[5][:, t * PT:(t + 1) * PT], td_w2[:, t * P:(t + 1) * P], td_low[:, :], start=True, stop=True)
                mm.then_inc(ready["rate"], 1)
                pe.wait_ge(read["r"], a + 1)
                pe.wait_ge(mix_ok, a * F + FG + 1)
                token_major(bank[4], mixed[:, FG, :, :], w["Wg"]).then_inc(ready["g"], 1)

            def slot(p, par):
                u, a, c = exists(p), exists(p + 1), exists(p - 1)
                if u:
                    spread_v(p, par, 0)
                if c:
                    pe.wait_ge(z_ok, p)
                    if not static(p) or p > 1:
                        pe.wait_ge(read["rr"], p - 1)
                    transposes(bank[6], og[:, :, :, :].rearrange("p (b k) h j -> p b (k h j)", b=PAIR)).then_inc(ready["z"], 1)
                    pe.wait_ge(read["z"], p)
                    if not static(p) or p > 1:
                        pe.wait_ge(read["ff"], p - 1)
                    token_major(bank[7], zT, w["Wo"]).then_inc(ready["out"], 1)
                if u:
                    spread_v(p, par, 1)
                if a:
                    a_transpose(p + 1)
                if u:
                    sum_heads(p, 0)
                    spread_v(p, par, 2)
                if a:
                    a_low(p + 1)
                if u:
                    sum_heads(p, 1)
                if c:
                    pe.wait_ge(xn2_ok, p * PAIR)
                    transposes(bank[6], xn2).then_inc(ready["xc"], 1)
                if u:
                    spread_v(p, par, 3)
                if a:
                    a_mix(p + 1)
                if u:
                    sum_heads(p, 2)
                if c:
                    pe.wait_ge(xk_ok, p * (2 * KC))
                    pe.wait_ge(read["out"], p)
                    feature_major(bank[7], w["Wfk"], xk2).then_inc(ready["kk"], 1)
                    pe.wait_ge(read["xc"], p)
                    token_major(bank[6], xr2, w["Wfr"]).then_inc(ready["rr"], 1)
                if a:
                    a_project(p + 1)
                if u:
                    sum_heads(p, 3)
                if c:
                    pe.wait_ge(read["kk"], p)
                    token_major(bank[7], kkT, w["Wfv"]).then_inc(ready["ff"], 1)

            core.wait_loaded(pe, stage, "maa_w1", "maa_w2", "maa_w2g")
            a_transpose(0)
            a_low(0)
            a_mix(0)
            core.wait_loaded(pe, stage, "td_w1", "td_w2", "Wk", "Wv", "Wr", "Wg")
            a_project(0)
            pe.wait_ge(made, 6)
            core.wait_loaded(pe, stage, "Wo", "Wfk", "Wfr", "Wfv")
            over_slots(pe, slot)

        @block.scalar
        def _(act):
            def copy_xa(a):
                act.wait_ge(ready["xa"], a + 1)
                wait(act, mix_ok, a * F)
                for k in range(KC):
                    done = act.activation(xa[:, k, :, 1:P + 1], halves(bank[3])[:, k, :].rearrange("p (b t) -> p b t", b=PAIR), ACT.Identity,
                                          scale=core.col(pre + "ln1_w", k), bias=core.col(pre + "ln1_b", k))
                done.then_inc(read["xa"], 1)

            def tanh_low(a):
                act.wait_ge(ready["low"], a + 1)
                act.activation(low[:, :], bank[3][:, 0:PT], ACT.Tanh)
                act.activation(low_g[:, :], bank[3][0:R, PT:2 * PT], ACT.Tanh).then_inc(read["low"], 1)

            def projections(a, par):
                act.wait_ge(ready["td"], a + 1)
                act.activation(td_low[:, :], bank[3][0:RD, 0:PT], ACT.Tanh).then_inc(read["td"], 1)
                act.wait_ge(ready["r"], a + 1)
                act.activation(rT[:, par, :, :], halves(bank[4]), ACT.Copy).then_inc(read["r"], 1)
                act.wait_ge(ready["rate"], a + 1)
                for t in range(KC):
                    done = act.activation(rate[:, par, t, :], bank[5][:, t * PT:(t + 1) * PT], ACT.Exp, bias=core.col(pre + "time_decay", t))
                done.then_inc(read["rate"], 1)
                act.wait_ge(ready["g"], a + 1)
                wait(act, read["g"], a)
                act.activation(g_tanh[:, :, :], halves(bank[4]), ACT.Tanh, scale=0.5).then_inc(g_tanh_ok, 1)

            def make_decay(p, par, s):
                k, b = s // PAIR, s % PAIR
                if not (static(p) and p == 0 and s < 2):
                    act.wait_ge(scan_ok, p * UNITS + (s - 1))
                if s == 0:
                    act.wait_ge(read["rate"], p + 1)
                act.activation(decay[:, s % 2, :, 1:P + 1], rate[:, par, k, b * P:(b + 1) * P][:, None, :].to_broadcast([P, J, P]),
                               ACT.Exp, scale=-1.0).then_inc(decay_ok, 1)

            def slot(p, par):
                u, a, c = exists(p), exists(p + 1), exists(p - 1)
                if c:
                    act.wait_ge(vsum_ok, p)
                    act.activation(gstd[:, :], vsum[:, :], ACT.Sqrt, scale=1.0 / J, bias=core.eps[:, 0:1]).then_inc(gstd_ok, 1)
                if u:
                    make_decay(p, par, 1)
                if c:
                    act.wait_ge(ready["z"], p)
                    act.activation(zT[:, :, :], halves(bank[6]), ACT.Copy, scale=0.5).then_inc(read["z"], 1)
                if a:
                    copy_xa(p + 1)
                if u:
                    make_decay(p, par, 2)
                if c:
                    act.wait_ge(mv2_ok, p * PAIR)
                    act.activation(std2[:, :], core.mv_new[:, :, 1], ACT.Sqrt, bias=core.eps[:, 0:1]).then_inc(std2_ok, 1)
                if a:
                    tanh_low(p + 1)
                if u:
                    make_decay(p, par, 3)
                if c:
                    act.wait_ge(ready["xc"], p)
                    for k in range(KC):
                        done = act.activation(xc[:, k, :, 1:P + 1], halves(bank[6])[:, k, :].rearrange("p (b t) -> p b t", b=PAIR), ACT.Identity,
                                              scale=core.col(pre + "ln2_w", k), bias=core.col(pre + "ln2_b", k))
                    done.then_inc(read["xc"], 1)
                    act.wait_ge(ready["kk"], p)
                    act.activation(relu[:, :, :], halves(bank[7]), ACT.Relu).then_inc(relu_ok, 1)
                    act.wait_ge(relu_ok, p)
                    act.activation(kkT[:, :, :], relu[:, :, :], ACT.Square).then_inc(read["kk"], 1)
                    act.wait_ge(ready["rr"], p)
                    act.activation(r_tanh[:, :, :], halves(bank[6]), ACT.Tanh, scale=0.5).then_inc(read["rr"], 1)
                if a:
                    projections(p + 1, 1 - par)
                    make_decay(p + 1, 1 - par, 0)

            rstd_scalar(core, act, root)
            copy_xa(0)
            tanh_low(0)
            projections(0, 0)
            act.wait_ge(made, 6)
            make_decay(0, 0, 0)
            over_slots(act, slot)

        @block.vector
        def _(dve):
            def normalise(a):
                wait(dve, ready["xa"], a)
                for b in range(PAIR):
                    i = a * PAIR + b
                    dve.tensor_scalar(xn[:, b, :], core.x[:, i, :], core.mv[:, i, 0:1], core.rstd[:, bass.ds(i, 1)],
                                      ALU.subtract, ALU.mult).then_inc(xn_ok, 1)
                wait(dve, mix_ok, a * F)
                dve.tensor_scalar(xa[:, :, :, 0:1], ctx_rows[:, :, bass.ds(a * PAIR, PAIR), 1:2], 1.0, None, ALU.mult).then_inc(first_ok, 1)

            def shift_a(a):
                dve.wait_ge(first_ok, a * 2 + 1)
                dve.wait_ge(read["xa"], a + 1)
                dve.tensor_tensor(sx[:, :, :, :].rearrange("p k b t -> p (k b) t"), xa[:, :, :, 0:P].rearrange("p k b t -> p (k b) t"),
                                  xa[:, :, :, 1:P + 1].rearrange("p k b t -> p (k b) t"), ALU.subtract).then_inc(first_ok, 1)
                dve.wait_ge(first_ok, a * 2 + 2)
                for k in range(KC):
                    dve.scalar_tensor_tensor(xmaa[:, k, :, :], sx[:, k, :, :], core.col(pre + "maa_x", k), xa[:, k, :, 1:P + 1],
                                             ALU.mult, ALU.add).then_inc(xmaa_ok, 1)

            def mix(a):
                for f in range(F):
                    dve.wait_ge(f_ready, a * F + (f + 1))
                    for k in range(KC):
                        done = dve.scalar_tensor_tensor(mixed[:, f, k, :], bank[4 + f % 2][:, k * PT:(k + 1) * PT],
                                                        core.col(pre + "maa_stack", f * KC + k), flat(sx[:, :, :, :])[:, k, :], ALU.add, ALU.mult)
                    done.then_inc(f_read, 1)

            def copy_kv(a, par):
                dve.wait_ge(ready["k"], a + 1)
                dve.tensor_copy(kT[:, par, :, :], halves(bank[5])).then_inc(read["k"], 1)
                dve.wait_ge(ready["v"], a + 1)
                dve.tensor_copy(vT[:, par, :, :], halves(bank[3])).then_inc(read["v"], 1)
                dve.wait_ge(g_tanh_ok, a + 1)
                dve.scalar_tensor_tensor(gate[:, par, :, :], g_tanh[:, :, :], 1.0, halves(bank[4]), ALU.add, ALU.mult).then_inc(read["g"], 1)

            def scan(p, par, s):
                k, b = s // PAIR, s % PAIR
                n = p * UNITS + s
                wait(dve, q_ok, n)
                dve.wait_ge(vb_ready, n + 1)
                dve.tensor_tensor(kv[:, :, 1:P + 1], VB, kT[:, par, k, b * P:(b + 1) * P][:, None, :].to_broadcast([P, J, P]), ALU.mult).then_inc(kv_ok, 1)
                dve.tensor_scalar(kv[:, :, 0:1], state0[:, k, bass.ds(p * PAIR + b, 1), :].rearrange("p b j -> p j b"), 1.0, None, ALU.mult).then_inc(kv_ok, 1)
                dve.wait_ge(kv_ok, n * 2 + 2)
                dve.wait_ge(decay_ok, n + 1)
                dve.tensor_tensor_scan(states[:, :, :].rearrange("p j t -> p (j t)"), decay[:, s % 2, :, :].rearrange("p j t -> p (j t)"),
                                       kv[:, :, :].rearrange("p j t -> p (j t)"), 0.0, ALU.mult, ALU.add).then_inc(scan_ok, 1)
                dve.wait_ge(scan_ok, n + 1)
                if not (static(p) and p == 0 and s < 2):
                    dve.wait_ge(sum_ready, p * UNITS + (s - 1))
                dve.scalar_tensor_tensor(prod[:, s % 2, :, :], kv[:, :, 1:P + 1], core.col(pre + "u", k), states[:, :, 0:P],
                                         ALU.mult, ALU.add).then_inc(q_ok, 1)

            def group_norm(c, par):
                dve.wait_ge(sum_ready, c * UNITS + UNITS)
                wait(dve, ready["z"], c)
                dve.tensor_copy(og[:, :, :, :], OG[:, :].rearrange("p (n j h) -> p n h j", j=J, h=HT)).then_inc(og_read, 1)
                heads = og[:, :, :, :].rearrange("p n h j -> p (n h) j")
                squares = sq[:, :, :, :].rearrange("p n h j -> p (n h) j")
                over_j = lambda t: t[:, :, None].to_broadcast([P, UNITS * HT, J])
                s0 = c * 8
                dve.wait_ge(og_read, c + 1)
                dve.tensor_reduce(msum[:, :], heads, AX_X, ALU.add).then_inc(gn_step, 1)
                dve.wait_ge(gn_step, s0 + 1)
                dve.tensor_scalar(mean[:, :], msum[:, :], 1.0 / J, None, ALU.mult).then_inc(gn_step, 1)
                dve.wait_ge(gn_step, s0 + 2)
                dve.tensor_tensor(heads, heads, over_j(mean), ALU.subtract).then_inc(gn_step, 1)
                dve.wait_ge(gn_step, s0 + 3)
                dve.tensor_tensor(squares, heads, heads, ALU.mult).then_inc(gn_step, 1)
                dve.wait_ge(gn_step, s0 + 4)
                dve.tensor_reduce(vsum[:, :], squares, AX_X, ALU.add).then_inc(vsum_ok, 1)
                dve.wait_ge(gstd_ok, c + 1)
                dve.reciprocal(grstd[:, :], gstd[:, :]).then_inc(gn_step, 1)
                dve.wait_ge(gn_step, s0 + 5)
                dve.tensor_tensor(heads, heads, over_j(grstd), ALU.mult).then_inc(gn_step, 1)
                per_token = og[:, :, :, :].rearrange("p (b k) h j -> p b (k h j)", b=PAIR)
                row = lambda i: gn_rows[:, i:i + 1, :].to_broadcast([P, PAIR, D])
                dve.wait_ge(gn_step, s0 + 6)
                dve.tensor_tensor(per_token, per_token, row(0), ALU.mult).then_inc(gn_step, 1)
                dve.wait_ge(gn_step, s0 + 7)
                dve.tensor_tensor(per_token, per_token, row(1), ALU.add).then_inc(gn_step, 1)
                dve.wait_ge(gn_step, s0 + 8)
                dve.wait_ge(read["g"], c + 1)
                dve.tensor_tensor(per_token, per_token, gate[:, par, :, :], ALU.mult).then_inc(z_ok, 1)

            def residual(c):
                dve.wait_ge(ready["out"], c + 1)
                dve.tensor_tensor(core.x_new[:, :, :], core.x[:, bass.ds(c * PAIR, PAIR), :], halves(bank[7]), ALU.add).then_inc(read["out"], 1)
                dve.wait_ge(read["out"], c + 1)
                for b in range(PAIR):
                    dve.bn_stats(core.stats[:, b, :], core.x_new[:, b, :]).then_inc(st_ok, 1)
                wait(dve, std2_ok, c)
                dve.wait_ge(st_ok, c * PAIR + PAIR)
                dve.tensor_scalar(xc[:, :, :, 0:1], ctx_rows[:, :, bass.ds(c * PAIR, PAIR), 0:1], 1.0, None, ALU.mult).then_inc(c_first, 1)
                for b in range(PAIR):
                    dve.bn_aggr(core.mv_new[:, b, :], core.stats[:, b, :]).then_inc(mv2_ok, 1)

            def normalise2(c):
                dve.wait_ge(std2_ok, c + 1)
                dve.wait_ge(mv2_ok, c * PAIR + PAIR)
                dve.reciprocal(rstd2[:, :], std2[:, :]).then_inc(c_step, 1)
                dve.wait_ge(c_step, c + 1)
                for b in range(PAIR):
                    dve.tensor_scalar(xn2[:, b, :], core.x_new[:, b, :], core.mv_new[:, b, 0:1], rstd2[:, b:b + 1],
                                      ALU.subtract, ALU.mult).then_inc(xn2_ok, 1)

            def shift_c(c):
                dve.wait_ge(read["xc"], c + 1)
                dve.wait_ge(c_first, c + 1)
                dve.tensor_tensor(sx2[:, :, :, :].rearrange("p k b t -> p (k b) t"), xc[:, :, :, 0:P].rearrange("p k b t -> p (k b) t"),
                                  xc[:, :, :, 1:P + 1].rearrange("p k b t -> p (k b) t"), ALU.subtract).then_inc(xk_step, 1)
                dve.wait_ge(xk_step, c + 1)
                for to, n in ((xk2, "ffn_maa_k"), (xr2, "ffn_maa_r")):
                    for k in range(KC):
                        dve.scalar_tensor_tensor(to[:, k, :].rearrange("p (b t) -> p b t", b=PAIR), sx2[:, k, :, :], core.col(pre + n, k),
                                                 xc[:, k, :, 1:P + 1], ALU.mult, ALU.add).then_inc(xk_ok, 1)

            def finish(c):
                dve.wait_ge(read["rr"], c + 1)
                dve.wait_ge(ready["ff"], c + 1)
                dve.scalar_tensor_tensor(gated[:, :, :], r_tanh[:, :, :], 1.0, halves(bank[7]), ALU.add, ALU.mult).then_inc(read["ff"], 1)
                wait(dve, stored, c * DMA)
                dve.wait_ge(read["ff"], c + 1)
                dve.scalar_tensor_tensor(result[:, :, :], gated[:, :, :], 0.5, core.x_new[:, :, :], ALU.mult, ALU.add).then_inc(result_ok, 1)

            def slot(p, par):
                u, a, c = exists(p), exists(p + 1), exists(p - 1)
                if c:
                    group_norm(p - 1, 1 - par)
                if u:
                    scan(p, par, 0)
                if a:
                    normalise(p + 1)
                if c:
                    residual(p - 1)
                if u:
                    scan(p, par, 1)
                if a:
                    shift_a(p + 1)
                if c:
                    normalise2(p - 1)
                if u:
                    scan(p, par, 2)
                if a:
                    mix(p + 1)
                if c:
                    shift_c(p - 1)
                if u:
                    scan(p, par, 3)
                if a:
                    copy_kv(p + 1, 1 - par)
                if c:
                    finish(p - 1)

            rstd_vector(core, dve, root, rstep)
            normalise(0)
            shift_a(0)
            mix(0)
            copy_kv(0, 0)
            core.wait_loaded(dve, stage, "state0")
            dve.wait_ge(gn_in, 2 * DMA)
            over_slots(dve, slot)


def store_stage(core):
    nc = core.nc
    with ExitStack() as ctx:
        stored = ctx.enter_context(nc.semaphore("stored"))
        block = ctx.enter_context(nc.Block())

        @block.sync
        def _(sp):
            sp.dma_start(core.out.rearrange("b t d -> t b d"), core.x[:, :, :]).then_inc(stored, DMA)
            sp.wait_ge(stored, DMA)


def build_program(nc, dram, out):
    with ExitStack() as ctx:
        core = Core(nc, ctx, dram, out)
        load_stage(core)
        for stage in STAGES:
            if stage == "l0_self":
                narrow_attention(core, stage, "self")
            elif stage == "l0_cross":
                narrow_attention(core, stage, "cross")
            elif stage == "l0_mlp":
                mlp(core, stage, "L0_xattn_ln3_s", "L0_xattn_ln3_b", "L0_xattn_b1", ACT.Gelu_apprx_tanh)
            elif stage == "l1_first":
                wide_attention(core, stage, 1)
            elif stage == "l1_second":
                wide_attention(core, stage, 2)
            elif stage == "l1_mlp":
                mlp(core, stage, "L1_xattn_ln_mlp_scale", "L1_xattn_ln_mlp_offset", "L1_xattn_b_fc1", ACT.Gelu)
            elif stage == "l2":
                single_attention(core, stage)
            elif stage == "l3":
                recurrence(core, stage)
        if STAGES[-1] != "l3":
            store_stage(core)


PLAIN = ["L0_xattn_w_qkv", "L0_xattn_w_ao", "L0_xattn_w_q", "L0_xattn_w_kv", "L0_xattn_w_co", "L0_xattn_w1", "L0_xattn_w2",
         "L1_xattn_wq1", "L1_xattn_wk1", "L1_xattn_wv1", "L1_xattn_wo1", "L1_xattn_wq2", "L1_xattn_wk2", "L1_xattn_wv2",
         "L1_xattn_wo2", "L1_xattn_w_fc1", "L1_xattn_w_fc2", "L3_xattn_maa_w1", "L3_xattn_td_w1", "L3_xattn_td_w2"]
TRANSPOSED = ["L2_xattn_w_q", "L2_xattn_w_k", "L2_xattn_w_v", "L2_xattn_w_o", "L3_xattn_Wr", "L3_xattn_Wk", "L3_xattn_Wv",
              "L3_xattn_Wg", "L3_xattn_Wo", "L3_xattn_Wfk", "L3_xattn_Wfr", "L3_xattn_Wfv"]


def kernel(**inputs):
    import concourse.bacc as bacc
    from concourse.bass_utils import run_bass_kernel_spmd

    a = {k: np.asarray(v) for k, v in inputs.items()}
    arrays = {
        "x": a["x"],
        "ctx_t": np.ascontiguousarray(a["ctx_2048"].reshape(TOK, D).T),
        "state0": np.ascontiguousarray(a["ctx_2048"][:, 2:10, :].reshape(NB, KC, P, 8).transpose(2, 1, 0, 3)).reshape(P, D),
        "mask_self": a["mask_1x1xSxS2_fc1"].reshape(P, P),
        "mask_cross": np.ascontiguousarray(a["mask_Bx1xSxS2_ff1"].reshape(NB, P, P)),
        "columns": np.ascontiguousarray(np.concatenate([a[n].reshape(-1, P) for n, _ in COLUMNS]).T),
        "maa_w2": np.ascontiguousarray(a["L3_xattn_maa_w2"].reshape(5 * 32, D)[:P]),
        "maa_w2g": np.ascontiguousarray(a["L3_xattn_maa_w2"].reshape(5 * 32, D)[P:]),
        "alpha": np.ascontiguousarray(np.broadcast_to(a["L2_xattn_alpha"].reshape(1, 1), (P, 1))),
    }
    for n, of in ROWS.items():
        arrays["row_" + n] = np.ascontiguousarray(np.broadcast_to(a[of], (P, D)))
    for n in PLAIN:
        arrays[n] = a[n]
    for n in TRANSPOSED:
        arrays[n] = np.ascontiguousarray(a[n].T)
    nc = bacc.Bacc("TRN2", target_bir_lowering=False, num_devices=1)
    dram = {n: nc.dram_tensor("in_" + n, v.shape, mybir.dt.from_np(v.dtype), kind="ExternalInput").ap()
            for n, v in arrays.items()}
    out = nc.dram_tensor("out", (NB, P, D), F32, kind="ExternalOutput").ap()
    build_program(nc, dram, out)
    r = run_bass_kernel_spmd(nc, [{"in_" + n: v for n, v in arrays.items()}], core_ids=[0])
    return r.results[0]["out"]
```

```python
from contextlib import ExitStack

import numpy as np

import concourse.bass as bass
from concourse import mybir

ALU = mybir.AluOpType
ACT = mybir.ActivationFunctionType
F32 = mybir.dt.float32
F32R = mybir.dt.float32r
AX_X = mybir.AxisListType.X

P = 128
NB = 16
D = 256
KC = D // P
PAIR = 2
NP = NB // PAIR
TOK = NB * P
PT = PAIR * P
EPS = 1e-5
HG = 4
NHG = 4
DMA = 16

COLUMNS = [
    ("L0_xattn_ln1_s", D), ("L0_xattn_ln1_b", D), ("L0_xattn_ln2_s", D), ("L0_xattn_ln2_b", D),
    ("L0_xattn_ln3_s", D), ("L0_xattn_ln3_b", D), ("L0_xattn_b_qkv", 3 * D), ("L0_xattn_b_q", D),
    ("L0_xattn_b_kv", 2 * D), ("L0_xattn_b1", 4 * D),
    ("L1_xattn_ln1_scale", D), ("L1_xattn_ln1_offset", D), ("L1_xattn_ln2_scale", D),
    ("L1_xattn_ln2_offset", D), ("L1_xattn_ln_mlp_scale", D), ("L1_xattn_ln_mlp_offset", D),
    ("L1_xattn_bq1", 2048), ("L1_xattn_bk1", 2048), ("L1_xattn_bv1", 2048),
    ("L1_xattn_bias_k1", 2048), ("L1_xattn_bias_v1", 2048),
    ("L1_xattn_bq2", 2048), ("L1_xattn_bk2", 2048), ("L1_xattn_bv2", 2048),
    ("L1_xattn_bias_k2", 2048), ("L1_xattn_bias_v2", 2048), ("L1_xattn_b_fc1", 4 * D),
    ("L3_xattn_ln1_w", D), ("L3_xattn_ln1_b", D), ("L3_xattn_ln2_w", D), ("L3_xattn_ln2_b", D),
    ("L3_xattn_maa_x", D), ("L3_xattn_maa_stack", 5 * D), ("L3_xattn_time_decay", D),
    ("L3_xattn_u", D), ("L3_xattn_ffn_maa_k", D), ("L3_xattn_ffn_maa_r", D),
]
ROWS = {"b_ao": "L0_xattn_b_ao", "b_co": "L0_xattn_b_co", "b2": "L0_xattn_b2", "bo1": "L1_xattn_bo1", "bo2": "L1_xattn_bo2",
        "b_fc2": "L1_xattn_b_fc2", "gn_w": "L3_xattn_gn_w", "gn_b": "L3_xattn_gn_b"}
COLUMN_AT, at = {}, 0
for name, size in COLUMNS:
    COLUMN_AT[name] = at
    at += size // P
N_COLUMNS = at

LATE, EARLY, WO, WORK, ARENA = 0, 12288, 24576, 28672, 42496
GROUP = 3 * KC * HG * P
FREE = {
    "l0_self": [(EARLY, ARENA)], "l0_cross": [(EARLY, ARENA)], "l0_mlp": [(WORK, ARENA)],
    "l1_first": [(WORK, ARENA)], "l1_second": [(WORK, ARENA)], "l1_mlp": [(WORK, ARENA)],
    "l2": [(WORK, ARENA)], "l3": [(LATE, EARLY), (WO, ARENA)],
}


def matrix(name, dram, at, rows, cols):
    return name, dram, at, rows, cols


WEIGHTS = {
    "l0_self": [matrix("w_qkv", "L0_xattn_w_qkv", LATE, D, 3 * D), matrix("w_out", "L0_xattn_w_ao", LATE + 1536, D, D),
                matrix("row", "row_b_ao", LATE + 8192, P, D)],
    "l0_cross": [matrix("w_q", "L0_xattn_w_q", LATE + 2048, D, D), matrix("w_kv", "L0_xattn_w_kv", LATE + 2560, D, 2 * D),
                 matrix("w_out", "L0_xattn_w_co", LATE + 3584, D, D), matrix("row", "row_b_co", LATE + 8448, P, D)],
    "l0_mlp": [matrix("w1", "L0_xattn_w1", LATE + 4096, D, 4 * D), matrix("w2", "L0_xattn_w2", LATE + 6144, 4 * D, D),
               matrix("row", "row_b2", LATE + 8704, P, D)],
    "l1_first": [matrix("wo", "L1_xattn_wo1", WO, 2048, D)],
    "l1_second": [matrix("wo", "L1_xattn_wo2", WO, 2048, D)],
    "l1_mlp": [matrix("w1", "L1_xattn_w_fc1", EARLY, D, 4 * D), matrix("row", "row_b_fc2", EARLY + 2048, P, D),
               matrix("w2", "L1_xattn_w_fc2", EARLY + GROUP, 4 * D, D)],
    "l2": [matrix(w, "L2_xattn_" + w, EARLY + 5120 + 512 * i, D, D) for i, w in enumerate(("w_q", "w_k", "w_v", "w_o"))]
          + [matrix("alpha", "alpha", EARLY + 2944, P, 1)],
    "l3": [matrix("maa_w1", "L3_xattn_maa_w1", EARLY + 7168, D, 160), matrix("maa_w2", "maa_w2", EARLY + 2304, P, D),
           matrix("maa_w2g", "maa_w2g", EARLY + 2560, 32, D), matrix("td_w1", "L3_xattn_td_w1", EARLY + 2816, D, 64),
           matrix("td_w2", "L3_xattn_td_w2", EARLY + 7488, 64, D), matrix("state0", "state0", EARLY + 7744, P, D)]
          + [matrix(w, "L3_xattn_" + w, EARLY + 8000 + 512 * i, D, D)
             for i, w in enumerate(("Wk", "Wv", "Wr", "Wg", "Wo", "Wfk", "Wfr", "Wfv"))],
}
LOADED_IN = {"load": ["l0_self", "l0_cross", "l0_mlp"], "l0_mlp": ["l1_first"]}
LOADED_AFTER_GROUP = {0: [("l1_mlp", "w1"), ("l1_mlp", "row")], 1: [("l1_mlp", "w2")], 3: [("l2", None), ("l3", None)]}

STAGES = ["l0_self", "l0_cross", "l0_mlp", "l1_first", "l1_second", "l1_mlp", "l2", "l3"]


def wait(eng, sem, value):
    if isinstance(value, int) and value <= 0:
        return
    eng.wait_ge(sem, value)


def over_pairs(eng, body):
    body(0)
    with eng.Fori(1, NP - 1) as p:
        body(p)
    body(NP - 1)


def split_product(pe, out, stationary, moving, start, stop):
    (s_hi, s_lo), (m_hi, m_lo) = stationary, moving
    pe.matmul(out, s_hi, m_lo, start=start, stop=False)
    pe.matmul(out, s_lo, m_hi, start=False, stop=False)
    return pe.matmul(out, s_hi, m_hi, start=False, stop=stop)


def over_steps(eng, body):
    def step(s):
        for par in range(2):
            body(s * 2 + par, par)
    step(0)
    with eng.Fori(1, NP // 2 - 1) as s:
        step(s)
    step(NP // 2 - 1)


GROUPS = {"l1_first": [f"group{g}" for g in range(NHG)], "l1_second": [f"group{g}" for g in range(NHG)]}


class Core:

    def __init__(self, nc, ctx, dram, out):
        self.nc, self.dram, self.out = nc, dram, out
        sb = lambda name, shape: ctx.enter_context(nc.sbuf_tensor(name, shape, F32))
        self.x = sb("x", [P, NB, D])
        self.cT = sb("ctx_t", [P, KC, TOK])
        self.ident = sb("ident", [P, P])
        self.cols = sb("cols", [P, N_COLUMNS])
        self.arena_at = nc.sbuf_base
        self.arena = sb("arena", [P, ARENA])
        self.loaded = {(stage, name): ctx.enter_context(nc.semaphore(f"loaded_{stage}_{name}"))
                       for stage in STAGES for name in [w[0] for w in WEIGHTS[stage]] + GROUPS.get(stage, [])}
        self.begun = set()
        self.ctx_in = ctx.enter_context(nc.semaphore("ctx_in"))
        self.mv = sb("mean_var", [P, NB, 2])
        self.rstd = sb("rstd", [P, NB])
        self.std = sb("std", [P, NB])
        self.newton = sb("newton", [P, NB])
        self.stats = sb("bn_stats", [P, PAIR, 6])
        self.mv_new = sb("mean_var_new", [P, PAIR, 2])
        self.x_new = sb("x_new", [P, PAIR, D])
        self.eps = sb("eps", [P, 1])
        self.unused = sb("unused", [P, 1])
        self.head_rows = sb("head_rows", [P, 8])
        self.banks = ctx.enter_context(nc.psum_tensor("banks", [P, 8, 512], F32))
        self.bank = [self.banks[:, i, :] for i in range(8)]

    def col(self, name, k=0, n=1):
        at = COLUMN_AT[name] + k
        return self.cols[:, at:at + n]

    def place(self, at, shape):
        size = int(np.prod(shape[1:]))
        flat = self.arena[0:shape[0], at:at + size]
        if len(shape) == 2:
            return flat
        names = "abcd"[:len(shape) - 1]
        return flat.rearrange(f"p ({' '.join(names)}) -> p {' '.join(names)}", **dict(zip(names, shape[1:])))

    def place_r(self, name, at, shape):
        return self.nc.alloc_sbuf_tensor_at(name, shape, F32R, offset=self.arena_at + 4 * at)

    def weight(self, stage, name):
        _, _, at, rows, cols = next(w for w in WEIGHTS[stage] if w[0] == name)
        return self.place(at, [rows, cols] if rows <= P else [P, rows // P, cols])

    def weight_at(self, stage, name):
        return next(w for w in WEIGHTS[stage] if w[0] == name)[2]

    def wait_loaded(self, eng, stage, *names, times=1):
        for name in names:
            eng.wait_ge(self.loaded[stage, name], DMA * times)

    def load_one(self, sp, stage, wanted=None):
        for name, dram, at, rows, cols in WEIGHTS.get(stage, []):
            if stage not in STAGES or (stage, name) in self.begun or wanted not in (None, name):
                continue
            self.begun.add((stage, name))
            source = self.dram[dram]
            if rows > P:
                source = source.rearrange("(k p) o -> p k o", p=P)
            sp.dma_start(self.weight(stage, name), source).then_inc(self.loaded[stage, name], DMA)

    def load_group(self, sp, stage, g):
        name = GROUPS[stage][g]
        if stage not in STAGES or (stage, name) in self.begun:
            return
        self.begun.add((stage, name))
        n = 1 + list(GROUPS).index(stage)
        for i, w in enumerate("qkv"):
            source = self.dram[f"L1_xattn_w{w}{n}"].rearrange("(k p) o -> p k o", p=P)[:, :, g * HG * P:(g + 1) * HG * P]
            sp.dma_start(self.group_weight(EARLY, i, g), source).then_inc(self.loaded[stage, name], DMA)

    def group_weight(self, region, i, g):
        return self.place(region + self.group_at(i, g), [P, KC, HG * P])

    def group_at(self, i, g):
        return g * GROUP + i * KC * HG * P

    def load(self, sp, stage):
        for of in [stage] + LOADED_IN.get(stage, []):
            for g in range(len(GROUPS.get(of, []))):
                self.load_group(sp, of, g)
            self.load_one(sp, of)


class Space:

    def __init__(self, core, stage):
        self.core, self.free = core, [list(r) for r in FREE[stage]]

    def __call__(self, name, shape):
        size = int(np.prod(shape[1:]))
        for r in self.free:
            if r[1] - r[0] >= size:
                at = r[0]
                r[0] += size
                return self.core.place(at, shape)
        raise AssertionError(f"no room for {name}: {size} of {self.free}")

    def split(self, name, shape):
        before = [r[0] for r in self.free]
        full = self(name, shape)
        at = next(b for b, r in zip(before, self.free) if r[0] != b)
        before = [r[0] for r in self.free]
        self(name + "_hi", shape)
        hi_at = next(b for b, r in zip(before, self.free) if r[0] != b)
        return full, (self.core.place_r(name + "_hi", hi_at, shape), self.core.place_r(name + "_lo", at, shape))


def zero_signals(core, signals):
    numbers = sorted(s.num for s in signals)
    starts = [n for n in numbers if n - 1 not in numbers]
    ends = [n + 1 for n in numbers if n + 1 not in numbers]
    with core.nc.Block() as block:
        @block.gpsimd
        def _(gp):
            for start, end in zip(starts, ends):
                gp.sem_clear(range(start, end))


class Signals:

    def __init__(self, core, ctx, prefix):
        self.core, self.nc, self.prefix, self.all = core, core.nc, prefix, []
        ctx.callback(self.close)
        self.holders = ExitStack()

    def __call__(self, name):
        self.all.append(self.holders.enter_context(self.nc.semaphore(self.prefix + name)))
        return self.all[-1]

    def close(self):
        zero_signals(self.core, self.all)
        self.holders.close()


def load_stage(core):
    nc = core.nc
    with ExitStack() as ctx:
        sem = Signals(core, ctx, "")
        PARTS = 4
        NX = NB // PARTS
        x_in = [sem(f"ld_x{i}") for i in range(PARTS)]
        consts_in, filled, stat = sem("ld_consts"), sem("ld_filled"), sem("ld_stat")
        stats = core.place(WORK, [P, NB, 6])
        block = ctx.enter_context(nc.Block())

        @block.sync
        def _(sp):
            for i in range(PARTS):
                part = slice(i * NX, (i + 1) * NX)
                sp.dma_start(core.x[:, part, :], core.dram["x"][part].rearrange("b t d -> t b d")).then_inc(x_in[i], DMA)
            sp.dma_start(core.cols[:, :], core.dram["columns"]).then_inc(consts_in, DMA)
            core.load(sp, "load")
            sp.dma_start(core.cT[:, :, :], core.dram["ctx_t"].rearrange("(k p) t -> p k t", p=P)).then_inc(core.ctx_in, DMA)
            sp.wait_ge(consts_in, DMA)
            if STAGES[0] != "l0_self":
                sp.wait_ge(core.ctx_in, DMA)

        @block.gpsimd
        def _(gp):
            gp.memset(core.eps[:, :], EPS).then_inc(filled, 1)
            gp.memset(core.ident[:, :], 0.0).then_inc(filled, 1)
            gp.wait_ge(filled, 2)
            gp.affine_select(out=core.ident[:, :], in_=core.ident[:, :], compare_op=ALU.not_equal, fill=1.0,
                             base=0, pattern=[[-1, P]], channel_multiplier=1).then_inc(filled, 1)
            gp.memset(core.head_rows[:, :], 1.0).then_inc(filled, 1)
            gp.wait_ge(filled, 4)
            gp.affine_select(out=core.head_rows[:, :], in_=core.head_rows[:, :], compare_op=ALU.is_ge, fill=0.0,
                             base=0, pattern=[[-16, 8]], channel_multiplier=1).then_inc(filled, 1)
            gp.wait_ge(filled, 5)
            gp.affine_select(out=core.head_rows[:, :], in_=core.head_rows[:, :], compare_op=ALU.is_ge, fill=0.0,
                             base=15, pattern=[[16, 8]], channel_multiplier=-1).then_inc(filled, 1)

        @block.scalar
        def _(act):
            act.wait_ge(filled, 1)
            load_sqrt_table(core, act)

        @block.vector
        def _(dve):
            for i in range(NB):
                if i % NX == 0:
                    dve.wait_ge(x_in[i // NX], DMA)
                dve.bn_stats(stats[:, i, :], core.x[:, i, :]).then_inc(stat, 1)
            dve.wait_ge(stat, NB)
            for i in range(NB):
                dve.bn_aggr(core.mv[:, i, :], stats[:, i, :])


def row_stats(core, dve, stat, p, before):
    for b in range(PAIR):
        dve.bn_stats(core.stats[:, b, :], core.x_new[:, b, :]).then_inc(stat, 1)
    dve.wait_ge(stat, before + PAIR)
    dve.tensor_scalar(core.x[:, bass.ds(p * PAIR, PAIR), :], core.x_new[:, :, :], 1.0, None, ALU.mult)
    for b in range(PAIR):
        dve.bn_aggr(core.mv_new[:, b, :], core.stats[:, b, :]).then_inc(stat, 1)
    dve.wait_ge(stat, before + 2 * PAIR)
    dve.tensor_scalar(core.mv[:, bass.ds(p * PAIR, PAIR), :], core.mv_new[:, :, :], 1.0, None, ALU.mult).then_inc(stat, 1)


def new_rows(core, dve, step, stat, p, update, update_ready, bias=None):
    steps = 1 if bias is None else 2
    dve.wait_ge(update_ready, p + 1)
    wait(dve, stat, p * (2 * PAIR + 1))
    dve.tensor_tensor(core.x_new[:, :, :], core.x[:, bass.ds(p * PAIR, PAIR), :], update, ALU.add).then_inc(step, 1)
    dve.wait_ge(step, p * steps + 1)
    if bias is not None:
        dve.tensor_tensor(core.x_new[:, :, :], core.x_new[:, :, :], bias[:, None, :].to_broadcast([P, PAIR, D]), ALU.add).then_inc(step, 1)
        dve.wait_ge(step, p * steps + 2)
    row_stats(core, dve, stat, p, p * (2 * PAIR + 1))


def load_sqrt_table(core, act):
    act.activation(core.unused[:, :], core.eps[:, :], ACT.Sqrt)


def rstd_scalar(core, act, root):
    act.activation(core.std[:, :], core.mv[:, :, 1], ACT.Sqrt, bias=core.eps[:, 0:1]).then_inc(root, 1)


def rstd_vector(core, dve, root, step):
    dve.wait_ge(root, 1)
    dve.reciprocal(core.rstd[:, :], core.std[:, :]).then_inc(step, 1)
    dve.wait_ge(step, 1)
    dve.tensor_tensor(core.newton[:, :], core.rstd[:, :], core.rstd[:, :], ALU.mult).then_inc(step, 1)
    dve.tensor_scalar(core.std[:, :], core.mv[:, :, 1], EPS, -0.5, ALU.add, ALU.mult).then_inc(step, 1)
    dve.wait_ge(step, 3)
    dve.tensor_tensor(core.newton[:, :], core.newton[:, :], core.std[:, :], ALU.mult).then_inc(step, 1)
    dve.wait_ge(step, 4)
    dve.scalar_tensor_tensor(core.rstd[:, :], core.newton[:, :], 1.5, core.rstd[:, :],
                             ALU.add, ALU.mult).then_inc(step, 1)
    dve.wait_ge(step, 5)


def wide_attention(core, stage, n):
    nc = core.nc
    H, HD = 16, P
    NK = P + 1
    SCALE = float(HD) ** -0.5
    pre = "L1_xattn_"
    ln_s, ln_b = pre + f"ln{n}_scale", pre + f"ln{n}_offset"
    bq, bk, bv = pre + f"bq{n}", pre + f"bk{n}", pre + f"bv{n}"
    bias_k, bias_v = pre + f"bias_k{n}", pre + f"bias_v{n}"
    with ExitStack() as ctx:
        sb = Space(core, stage)
        sem = Signals(core, ctx, f"w{n}_")
        wo = core.weight(stage, "wo")
        w_full = [[core.group_weight(EARLY, i, g) for i in range(3)] for g in range(NHG)]
        w_hi, w_lo = ([[core.place_r(f"w{n}_{part}_{g}_{i}", region + core.group_at(i, g), [P, KC, HG * HD]) for i in range(3)]
                       for g in range(NHG)] for part, region in (("hi", LATE), ("lo", EARLY)))
        xn = sb("xn", [P, PAIR, D])
        hT, (hT_hi, hT_lo) = sb.split(f"w{n}_hT", [P, KC, PT])
        kv_in, (kv_hi, kv_lo) = sb.split(f"w{n}_kv", [P, KC, PT])
        qT = sb("qT", [P, HG, PT])
        kT = sb("kT", [P, HG, PAIR, NK])
        v = sb("v", [P, 2, PAIR, HG * HD])
        prob = sb("prob", [P, PAIR, HG, NK])
        probT = sb("probT", [P, PAIR, HG, P])
        headT = sb("headT", [P, H, PT])
        top = sb("top", [P, PAIR, HG])
        shift = sb("shift", [P, PAIR, HG])
        total = sb("total", [P, PAIR, HG])
        inv = sb("inv", [P, PAIR, HG])
        own_p = sb("own_p", [P, PAIR, H])
        early = sb("early", [P, H * H])
        dvz = early.rearrange("p (a b) -> p a b", a=H)
        own_pT = early[0:H, 0:PT]
        bvo = sb("bvo", [H, D])
        obias = sb("obias", [P, D])
        bank = core.bank
        LN = bank[7]
        CHUNKS = [(2, [(0, 3), (1, 3)], (slice(0, PAIR), 3)), (3, [(0, i) for i in range(3)], (0, slice(0, 3))),
                  (4, [(1, i) for i in range(3)], (1, slice(0, 3)))]
        NCH = len(CHUNKS)

        def score_tile(c, j):
            return bank[CHUNKS[c][0]][:, j * NK:(j + 1) * NK]

        def of_chunk(t, c):
            b, h = CHUNKS[c][2]
            return t[:, b, h]

        row_in = sem("row_in")
        root, rstep = sem("root"), sem("rstep")
        hn_ok, lt_ok, hT_ok = sem("hn_ok"), sem("lt_ok"), sem("hT_ok")
        kv_in_ok, kv_hi_ok, kv_ok = sem("kv_in_ok"), sem("kv_hi_ok"), sem("kv_ok")
        hT_raw, hT_hi_ok, w_hi_ok = sem("hT_raw"), sem("hT_hi_ok"), sem("w_hi_ok")
        w_ok = [sem(f"w_ok{g}") for g in range(NHG)]
        proj_ok, qk_ok, v_ok = sem("proj_ok"), sem("qk_ok"), sem("v_ok")
        own_ok = sem("own_ok")
        score_ok, top_step, shift_ok, exp_ok = sem("score_ok"), sem("top_step"), sem("shift_ok"), sem("exp_ok")
        norm_step, prob_ok = sem("norm_step"), sem("prob_ok")
        pt_ok, probT_ok, pv_ok, head_ok = sem("pt_ok"), sem("probT_ok"), sem("pv_ok"), sem("head_ok")
        ot_ok, own_pT_ok, out_ok = sem("ot_ok"), sem("own_pT_ok"), sem("out_ok")
        dv_step, const_ok, const_copied = sem("dv_step"), sem("const_ok"), sem("const_copied")
        res_ok, stat = sem("res_ok"), sem("stat")
        block = ctx.enter_context(nc.Block())

        @block.sync
        def _(sp):
            def body(p):
                wait(sp, proj_ok, p * (6 * NHG))
                sp.dma_start(kv_in[:, :, :], core.cT[:, :, bass.ts(p, PT)]).then_inc(kv_in_ok, DMA)
            body(0)
            core.load(sp, stage)
            sp.dma_start(obias, core.dram[f"row_bo{n}"]).then_inc(row_in, DMA)
            with sp.Fori(1, NP - 1) as p:
                body(p)
            body(NP - 1)
            for g in range(NHG):
                sp.wait_ge(proj_ok, ((NP - 1) * NHG + g + 1) * 6)
                if n == 1:
                    core.load_group(sp, "l1_second", g)
                else:
                    for of, name in LOADED_AFTER_GROUP.get(g, []):
                        core.load_one(sp, of, name)

        @block.gpsimd
        def _(gp):
            def weight_lo(g):
                for i in range(3):
                    gp.wait_ge(w_hi_ok, g * 3 + i + 1)
                    gp.tensor_tensor(w_lo[g][i][:, :, :], w_full[g][i], w_hi[g][i][:, :, :], ALU.subtract).then_inc(w_ok[g], 1)

            def context_lo(p):
                gp.wait_ge(kv_hi_ok, p + 1)
                gp.tensor_tensor(kv_lo[:, :, :], kv_in, kv_hi[:, :, :], ALU.subtract).then_inc(kv_ok, 1)

            def rows_lo(p):
                gp.wait_ge(hT_hi_ok, p + 1)
                gp.tensor_tensor(hT_lo[:, :, :], hT, hT_hi[:, :, :], ALU.subtract).then_inc(hT_ok, 1)

            def body(p):
                if isinstance(p, int) and p == NP - 1:
                    return
                if isinstance(p, int) and p == 0:
                    weight_lo(2)
                    weight_lo(3)
                rows_lo(p + 1)
                context_lo(p + 1)

            rows_lo(0)
            context_lo(0)
            weight_lo(1)
            over_pairs(gp, body)

        @block.tensor
        def _(pe):
            def ln_transpose(p):
                if not isinstance(p, int) or p > 1:
                    wait(pe, res_ok, (p - 1) * 2 - 1)
                pe.wait_ge(hn_ok, p * PAIR + PAIR)
                for k in range(KC):
                    for b in range(PAIR):
                        mm = pe.transpose(LN[:, k * PT + b * P:k * PT + (b + 1) * P], xn[:, b, k * P:(k + 1) * P], core.ident[:, :])
                mm.then_inc(lt_ok, 1)

            def project_qk(p, g, u):
                if g == 0:
                    pe.wait_ge(hT_ok, p + 1)
                for use in range(4):
                    i_w, hi, lo = (0, hT_hi, hT_lo) if use < 2 else (1, kv_hi, kv_lo)
                    if use == 2 and g == 0:
                        pe.wait_ge(kv_ok, p + 1)
                    if isinstance(p, int) and p == 0 and use % 2 == 0:
                        pe.wait_ge(w_ok[g], i_w + 1)
                    if use < 2:
                        wait(pe, v_ok, u * 2 - 1 + use)
                    else:
                        pe.wait_ge(qk_ok, u * 4 + use - 1)
                    for i in range(2):
                        h = (use % 2) * 2 + i
                        for k in range(KC):
                            mm = split_product(pe, bank[use % 2][:, i * PT:(i + 1) * PT],
                                               [w[g][i_w][:, k, h * HD:(h + 1) * HD] for w in (w_hi, w_lo)],
                                               [m[:, k, :] for m in (hi, lo)], k == 0, k == KC - 1)
                    mm.then_inc(proj_ok, 1)

            def project_v(p, g, u):
                if isinstance(p, int) and p == 0:
                    pe.wait_ge(w_ok[g], 3)
                for b in range(PAIR):
                    pe.wait_ge(qk_ok, u * 4 + 3 + b)
                    for k in range(KC):
                        mm = split_product(pe, bank[b][:, :], [m[:, k, b * P:(b + 1) * P] for m in (kv_hi, kv_lo)],
                                           [w[g][2][:, k, :] for w in (w_hi, w_lo)], k == 0, k == KC - 1)
                    mm.then_inc(proj_ok, 1)

            def scores(u, g):
                pe.wait_ge(qk_ok, u * 4 + 4)
                for c, (_, tiles, _) in enumerate(CHUNKS):
                    wait(pe, exp_ok, (u - 1) * NCH + c + 1)
                    for j, (b, i) in enumerate(tiles):
                        mm = pe.matmul(score_tile(c, j), qT[:, i, b * P:(b + 1) * P], kT[:, i, b, :], start=True, stop=True)
                    mm.then_inc(score_ok, 1)

            def prob_transpose(u):
                for b in range(PAIR):
                    pe.wait_ge(prob_ok, u * NCH + 2 + b)
                    wait(pe, head_ok, u * 2 - 1 + b)
                    for i in range(HG):
                        mm = pe.transpose(bank[5 + b][:, i * P:(i + 1) * P], prob[:, b, i, 0:P], core.ident[:, :])
                    mm.then_inc(pt_ok, 1)

            def weigh_values(u, par):
                pe.wait_ge(probT_ok, u * 2 + 2)
                pe.wait_ge(v_ok, u * 2 + 2)
                for half in range(2):
                    for i in (half * 2, half * 2 + 1):
                        for b in range(PAIR):
                            at = (i % 2) * PT + b * P
                            mm = pe.matmul(bank[5 + half][:, at:at + P], v[:, par, b, i * HD:(i + 1) * HD], probT[:, b, i, :],
                                           start=True, stop=True)
                    mm.then_inc(pv_ok, 1)

            def own_transpose(p):
                pe.wait_ge(own_ok, (p + 1) * NHG)
                if isinstance(p, int) and p == NP - 1:
                    pe.wait_ge(hT_raw, NP)
                else:
                    pe.wait_ge(hT_raw, p + 2)
                for b in range(PAIR):
                    mm = pe.transpose(LN[0:H, b * P:(b + 1) * P], own_p[:, b, :], core.ident[:, :])
                mm.then_inc(ot_ok, 1)

            def project_out(p):
                pe.wait_ge(own_pT_ok, p + 1)
                pe.wait_ge(head_ok, (p + 1) * (2 * NHG))
                for b in range(PAIR):
                    at = LN[:, b * D:(b + 1) * D]
                    pe.matmul(at, own_pT[:, b * P:(b + 1) * P], bvo[:, :], start=True, stop=False)
                    for h in range(H):
                        mm = pe.matmul(at, headT[:, h, b * P:(b + 1) * P], wo[:, h, :], start=False, stop=(h == H - 1))
                mm.then_inc(out_ok, 1)

            def constants():
                pe.wait_ge(head_ok, 2 * (NHG - 1))
                core.wait_loaded(pe, stage, "wo")
                pe.wait_ge(dv_step, 3)
                for h in range(H):
                    mm = pe.matmul(bank[5][0:H, 0:D], dvz[:, h, :], wo[:, h, :], start=(h == 0), stop=(h == H - 1))
                mm.then_inc(const_ok, 1)
                for h in range(H):
                    mm = pe.matmul(bank[6][:, 0:D], core.col(bv, h).to_broadcast([P, P]), wo[:, h, :],
                                   start=(h == 0), stop=(h == H - 1))
                mm.then_inc(const_ok, 1)

            def body(p):
                last = isinstance(p, int) and p == NP - 1
                for g in range(NHG):
                    u = p * NHG + g
                    p1, g1 = (p, g + 1) if g < NHG - 1 else (p + 1, 0)
                    if g == 0 and not (isinstance(p, int) and p == 0):
                        own_transpose(p - 1)
                    scores(u, g)
                    more = not (last and g == NHG - 1)
                    if more:
                        project_qk(p1, g1, u + 1)
                    if g == 0 and not (isinstance(p, int) and p == 0):
                        project_out(p - 1)
                    if g == NHG - 2 and not last:
                        ln_transpose(p + 1)
                    if isinstance(u, int) and u == NHG - 1:
                        constants()
                        pe.wait_ge(const_copied, 2)
                    prob_transpose(u)
                    if more:
                        project_v(p1, g1, u + 1)
                    weigh_values(u, g % 2)

            ln_transpose(0)
            project_qk(0, 0, 0)
            project_v(0, 0, 0)
            over_pairs(pe, body)
            own_transpose(NP - 1)
            project_out(NP - 1)

        @block.scalar
        def _(act):
            def layer_norm(p):
                act.wait_ge(lt_ok, p + 1)
                for k in range(KC):
                    done = act.activation(hT[:, k, :], LN[:, k * PT:(k + 1) * PT], ACT.Identity,
                                          scale=core.col(ln_s, k), bias=core.col(ln_b, k))
                done.then_inc(hT_raw, 1)
                act.wait_ge(hT_raw, p + 1)
                act.activation(hT_hi[:, :, :], hT, ACT.Copy).then_inc(hT_hi_ok, 1)

            def context_hi(p):
                act.wait_ge(kv_in_ok, p * DMA + DMA)
                act.activation(kv_hi[:, :, :], kv_in, ACT.Copy).then_inc(kv_hi_ok, 1)

            def weight_hi(g):
                core.wait_loaded(act, stage, GROUPS[stage][g], times=3)
                for i in range(3):
                    act.activation(w_hi[g][i][:, :, :], w_full[g][i], ACT.Copy).then_inc(w_hi_ok, 1)

            def copy_v(u, par):
                for b in range(PAIR):
                    act.wait_ge(proj_ok, u * 6 + 5 + b)
                    act.activation(v[:, par, b, :], bank[b][:, :], ACT.Copy).then_inc(v_ok, 1)

            def body(p):
                last = isinstance(p, int) and p == NP - 1
                for g in range(NHG):
                    u = p * NHG + g
                    if g == NHG - 1 and not last:
                        context_hi(p + 1)
                    for c, (_, tiles, _) in enumerate(CHUNKS):
                        act.wait_ge(shift_ok, u * NCH + c + 1)
                        for j, (b, i) in enumerate(tiles):
                            done = act.activation(prob[:, b, i, :], score_tile(c, j), ACT.Exp, scale=SCALE,
                                                  bias=shift[:, b, i:i + 1], accum_out=total[:, b, i:i + 1])
                        done.then_inc(exp_ok, 1)
                    if g == NHG - 2 and not last:
                        layer_norm(p + 1)
                    for b in range(PAIR):
                        act.wait_ge(pt_ok, u * 2 + 1 + b)
                        act.activation(probT[:, b, :, :], bank[5 + b][:, :].rearrange("p (h q) -> p h q", h=HG),
                                       ACT.Copy).then_inc(probT_ok, 1)
                    if isinstance(u, int) and u < 2:
                        weight_hi(u + 2)
                    if not (last and g == NHG - 1):
                        copy_v(u + 1, (g + 1) % 2)

            rstd_scalar(core, act, root)
            weight_hi(0)
            layer_norm(0)
            context_hi(0)
            weight_hi(1)
            copy_v(0, 0)
            over_pairs(act, body)
            load_sqrt_table(core, act)

        @block.vector
        def _(dve):
            def normalise(p):
                wait(dve, lt_ok, p)
                for b in range(PAIR):
                    i = p * PAIR + b
                    dve.tensor_scalar(xn[:, b, :], core.x[:, i, :], core.mv[:, i, 0:1], core.rstd[:, bass.ds(i, 1)],
                                      ALU.subtract, ALU.mult).then_inc(hn_ok, 1)

            def copy_qk(g, u, use):
                dve.wait_ge(proj_ok, u * 6 + 1 + use)
                h, bias = (use % 2) * 2, (bq, bk)[use // 2]
                if use < 2:
                    dve.tensor_tensor(qT[:, h:h + 2, :], bank[use % 2][:, :].rearrange("p (h t) -> p h t", h=2),
                                      core.col(bias, g * HG + h, 2)[:, :, None].to_broadcast([P, 2, PT]), ALU.add).then_inc(qk_ok, 1)
                else:
                    dve.tensor_copy(kT[:, h:h + 2, :, P], core.col(bias_k, g * HG + h, 2)[:, :, None].to_broadcast([P, 2, PAIR]))
                    dve.tensor_tensor(kT[:, h:h + 2, :, 0:P], bank[use % 2][:, :].rearrange("p (h b t) -> p h b t", h=2, b=PAIR),
                                      core.col(bias, g * HG + h, 2)[:, :, None, None].to_broadcast([P, 2, PAIR, P]), ALU.add).then_inc(qk_ok, 1)

            def row_max(u):
                wait(dve, own_ok, u)
                for c, (_, tiles, _) in enumerate(CHUNKS):
                    dve.wait_ge(score_ok, u * NCH + c + 1)
                    dve.tensor_reduce(of_chunk(top, c), bank[CHUNKS[c][0]][:, 0:len(tiles) * NK].rearrange("p (j k) -> p j k", k=NK), AX_X,
                                      ALU.max).then_inc(top_step, 1)
                    dve.wait_ge(top_step, u * NCH + c + 1)
                    dve.tensor_scalar(of_chunk(shift, c), of_chunk(top, c), -SCALE, None, ALU.mult).then_inc(shift_ok, 1)

            def scale_probs(u, c):
                n = len(CHUNKS[c][1])
                dve.wait_ge(exp_ok, u * NCH + c + 1)
                dve.reciprocal(of_chunk(inv, c), of_chunk(total, c)).then_inc(norm_step, 1)
                dve.wait_ge(norm_step, u * NCH + c + 1)
                dve.tensor_tensor(of_chunk(prob, c), of_chunk(prob, c), of_chunk(inv, c)[:, :, None].to_broadcast([P, n, NK]),
                                  ALU.mult).then_inc(prob_ok, 1)

            def keep_own(g, u):
                dve.wait_ge(prob_ok, (u + 1) * NCH)
                dve.tensor_scalar(own_p[:, :, g * HG:(g + 1) * HG], prob[:, :, :, P], 1.0, None, ALU.mult).then_inc(own_ok, 1)

            def copy_heads(g, u):
                for half in range(2):
                    dve.wait_ge(pv_ok, u * 2 + 1 + half)
                    h = g * HG + half * 2
                    dve.tensor_copy(headT[:, h:h + 2, :], bank[5 + half][:, :].rearrange("p (h t) -> p h t", h=2)).then_inc(head_ok, 1)

            def copy_own(p):
                dve.wait_ge(ot_ok, p + 1)
                dve.tensor_copy(own_pT[:, :], LN[0:H, 0:PT]).then_inc(own_pT_ok, 1)

            def residual(p):
                new_rows(core, dve, res_ok, stat, p, LN[:, :].rearrange("p (b d) -> p b d", b=PAIR), out_ok, obias)

            def body(p):
                first = isinstance(p, int) and p == 0
                last = isinstance(p, int) and p == NP - 1
                for g in range(NHG):
                    u = p * NHG + g
                    g1 = (g + 1) % NHG
                    more = not (last and g == NHG - 1)
                    if g == 0 and not first:
                        copy_own(p - 1)
                    row_max(u)
                    if more:
                        copy_qk(g1, u + 1, 0)
                        copy_qk(g1, u + 1, 1)
                    scale_probs(u, 0)
                    scale_probs(u, 1)
                    if more:
                        copy_qk(g1, u + 1, 2)
                    scale_probs(u, 2)
                    if more:
                        copy_qk(g1, u + 1, 3)
                    keep_own(g, u)
                    if g == 0 and not first:
                        residual(p - 1)
                    if g == 1 and not last:
                        normalise(p + 1)
                    if isinstance(u, int) and u == NHG - 1:
                        dve.wait_ge(const_ok, 2)
                        dve.tensor_copy(bvo[:, :], bank[5][0:H, 0:D]).then_inc(const_copied, 1)
                        dve.wait_ge(row_in, DMA)
                        dve.tensor_tensor(obias[:, :], bank[6][:, 0:D], obias[:, :], ALU.add).then_inc(const_copied, 1)
                    copy_heads(g, u)

            rstd_vector(core, dve, root, rstep)
            normalise(0)
            for i in range(3):
                dve.wait_ge(w_hi_ok, i + 1)
                dve.tensor_tensor(w_lo[0][i][:, :, :], w_full[0][i], w_hi[0][i][:, :, :], ALU.subtract).then_inc(w_ok[0], 1)
            dve.memset(dvz[:, :, :], 0.0).then_inc(dv_step, 1)
            dve.tensor_tensor(own_p[:, 0, :], core.col(bias_v, 0, H), core.col(bv, 0, H), ALU.subtract).then_inc(dv_step, 1)
            dve.wait_ge(dv_step, 2)
            dve.tensor_copy(dvz[:, :, :].rearrange("p a b -> p (a b)")[:, 0:H * H:H + 1], own_p[:, 0, :]).then_inc(dv_step, 1)
            dve.wait_ge(dv_step, 3)
            for use in range(4):
                copy_qk(0, 0, use)
            over_pairs(dve, body)
            copy_own(NP - 1)
            residual(NP - 1)


def narrow_attention(core, stage, kind):
    nc = core.nc
    H, HD = 16, 16
    NHG = H // HG
    TILE_HEADS = P // HD
    SCALE = 0.25
    MASKED = 10000.0 / SCALE
    pre = "L0_xattn_"
    self_attn = kind == "self"
    nln = 1 if self_attn else 2
    ln_s, ln_b = pre + f"ln{nln}_s", pre + f"ln{nln}_b"
    n_mask = 1 if self_attn else NB
    AHEAD = 2
    with ExitStack() as ctx:
        sb = Space(core, stage)
        sem = Signals(core, ctx, f"n{kind}_")
        if self_attn:
            wqkv = core.weight(stage, "w_qkv")
            parts = [wqkv[:, :, i * D:(i + 1) * D] for i in range(3)]
        else:
            wkv = core.weight(stage, "w_kv")
            parts = [core.weight(stage, "w_q"), wkv[:, :, 0:D], wkv[:, :, D:2 * D]]
        wo, out_row = core.weight(stage, "w_out"), core.weight(stage, "row")
        mask = sb("mask", [P, n_mask, P])
        less = sb("less", [P, n_mask, P])
        less_pair = None if self_attn else sb("less_pair", [P, 2, PAIR, P])
        xn = sb("xn", [P, PAIR, D])
        hT = sb("hT", [P, KC, PT])
        kv_in = hT if self_attn else sb("kv_in", [P, KC, PT])
        q_tile = sb("q_tile", [P, KC, PT])
        qT = sb("qT", [P, 2, H, PT])
        kT = sb("kT", [P, 2, KC, PT])
        v = sb("v", [P, 2, PAIR, D])
        prob = sb("prob", [P, NHG, PAIR, HG, P])
        probT = sb("probT", [P, PAIR, HG, P])
        top = sb("top", [P, PAIR, HG])
        shift = sb("shift", [P, 2, PAIR, HG])
        total = sb("total", [P, PAIR, H])
        inv = sb("inv", [P, PAIR, H])
        head = sb("head", [P, PAIR, D])
        headT = sb("headT", [P, KC, PT])
        bank = core.bank
        CTX, OUT = bank[6], bank[7]

        if self_attn:
            bias_q, bias_k, bias_v = [(pre + "b_qkv", i * KC) for i in range(3)]
        else:
            bias_q, bias_k, bias_v = (pre + "b_q", 0), (pre + "b_kv", 0), (pre + "b_kv", KC)

        mask_in = sem("mask_in")
        root, rstep, less_ok = sem("root"), sem("rstep"), sem("less_ok")
        pair_ok = [sem(f"pair_ok{par}") for par in range(2)]
        hn_ok, lt_ok, hT_ok, kv_ok = sem("hn_ok"), sem("lt_ok"), sem("hT_ok"), sem("kv_ok")
        proj_ok = sem("proj_ok")
        q_copied, q_ok, k_ok, v_ok = sem("q_copied"), sem("q_ok"), sem("k_ok"), sem("v_ok")
        score_ok, kept_ok, masked_ok, top_ok, shift_ok = (sem(s) for s in ("score", "kept", "masked", "top", "shift_ok"))
        exp_ok, inv_ok = sem("exp_ok"), sem("inv_ok")
        pt_ok, probT_ok, pv_ok, head_ok = sem("pt_ok"), sem("probT_ok"), sem("pv_ok"), sem("head_ok")
        ht_ok, headT_ok, out_ok, res_ok, stat = sem("ht_ok"), sem("headT_ok"), sem("out_ok"), sem("res_ok"), sem("stat")
        block = ctx.enter_context(nc.Block())

        @block.sync
        def _(sp):
            if not self_attn:
                sp.dma_start(kv_in[:, :, :], core.cT[:, :, 0:PT]).then_inc(kv_ok, DMA)
            if self_attn:
                sp.dma_start(mask[:, 0, :], core.dram["mask_self"]).then_inc(mask_in, DMA)
            else:
                sp.dma_start(mask[:, :, :], core.dram["mask_cross"].rearrange("b q k -> q b k")).then_inc(mask_in, DMA)
            core.load(sp, stage)
            if self_attn:
                sp.wait_ge(core.ctx_in, DMA)
            else:
                def part_of_less(p, par):
                    if not isinstance(p, int) or p > 1:
                        sp.wait_ge(masked_ok, (p - 1) * (2 * NHG))
                    sp.dma_start(less_pair[:, par, :, :], less[:, bass.ds(p * PAIR, PAIR), :]).then_inc(pair_ok[par], DMA)

                def body(p, par):
                    if not (isinstance(p, int) and p == NP - 1):
                        sp.wait_ge(proj_ok, p * 4 + 4)
                        sp.dma_start(kv_in[:, :, :], core.cT[:, :, bass.ts(p + 1, PT)]).then_inc(kv_ok, DMA)
                        part_of_less(p + 1, 1 - par)
                sp.wait_ge(less_ok, 1)
                part_of_less(0, 0)
                over_steps(sp, body)

        @block.gpsimd
        def _(gp):
            gp.wait_ge(mask_in, DMA)
            gp.tensor_scalar(less[:, :, :], mask[:, :, :], MASKED, -MASKED, ALU.mult, ALU.add).then_inc(less_ok, 1)
            gp.wait_ge(less_ok, 1)

            def spread_q(p, par, t):
                n = p * KC + (t + 1)
                gp.wait_ge(q_copied, n)
                gp.tensor_tensor(qT[:, par, t * TILE_HEADS:(t + 1) * TILE_HEADS, :],
                                 q_tile[:, t, None, :].to_broadcast([P, TILE_HEADS, PT]),
                                 core.head_rows[:, :, None].to_broadcast([P, TILE_HEADS, PT]), ALU.mult).then_inc(q_ok, 1)

            def add_mask(p, par, g):
                for b in range(PAIR):
                    gp.wait_ge(kept_ok, p * (NHG * 2) + (g * 2 + 1 + b))
                    m = less[:, 0:1, :] if self_attn else less_pair[:, par, b:b + 1, :]
                    gp.tensor_tensor(prob[:, g, b, :, :], prob[:, g, b, :, :], m.to_broadcast([P, HG, P]),
                                     ALU.add).then_inc(masked_ok, 1)

            def body(p, par):
                last = isinstance(p, int) and p == NP - 1
                for g in range(NHG):
                    if g < NHG - AHEAD:
                        add_mask(p, par, g + AHEAD)
                    elif not last:
                        if not self_attn and g == NHG - AHEAD:
                            gp.wait_ge(pair_ok[1 - par], (p + 1 - (1 - par)) * (DMA // 2) + DMA)
                        add_mask(p + 1, 1 - par, g + AHEAD - NHG)
                    if not last and g in (0, 1):
                        spread_q(p + 1, 1 - par, g)

            spread_q(0, 0, 0)
            spread_q(0, 0, 1)
            if not self_attn:
                gp.wait_ge(pair_ok[0], DMA)
            for g in range(AHEAD):
                add_mask(0, 0, g)
            over_steps(gp, body)

        @block.tensor
        def _(pe):
            def ln_transpose(p):
                pe.wait_ge(hn_ok, p * PAIR + PAIR)
                wait(pe, v_ok, p)
                for k in range(KC):
                    for b in range(PAIR):
                        mm = pe.transpose(bank[1][:, k * PT + b * P:k * PT + (b + 1) * P], xn[:, b, k * P:(k + 1) * P], core.ident[:, :])
                mm.then_inc(lt_ok, 1)

            def project_tile(to, part, tile, moving):
                for k in range(KC):
                    mm = pe.matmul(to, parts[part][:, k, tile * P:(tile + 1) * P], moving(k), start=(k == 0), stop=(k == KC - 1))
                return mm

            def project_q(p):
                pe.wait_ge(hT_ok, p + 1)
                wait(pe, k_ok, p)
                for t in range(KC):
                    mm = project_tile(bank[0][:, t * PT:(t + 1) * PT], 0, t, lambda k: hT[:, k, :])
                mm.then_inc(proj_ok, 1)

            def project_k(p):
                pe.wait_ge(q_copied, p * KC + KC)
                k_in = (lambda k: hT[:, k, :]) if self_attn else (lambda k: core.cT[:, k, bass.ts(p, PT)])
                for t in range(KC):
                    mm = project_tile(bank[0][:, t * PT:(t + 1) * PT], 1, t, k_in)
                mm.then_inc(proj_ok, 1)

            def project_v(p):
                if not self_attn:
                    pe.wait_ge(kv_ok, p * DMA + DMA)
                for b in range(PAIR):
                    for k in range(KC):
                        mm = pe.matmul(bank[1][:, b * D:(b + 1) * D], kv_in[:, k, b * P:(b + 1) * P], parts[2][:, k, :],
                                       start=(k == 0), stop=(k == KC - 1))
                mm.then_inc(proj_ok, 2)

            def scores(p, par, g):
                u = p * NHG + g
                if g == 0:
                    pe.wait_ge(k_ok, p + 1)
                if g % (NHG // KC) == 0:
                    pe.wait_ge(q_ok, p * KC + (g // (NHG // KC) + 1))
                for b in range(PAIR):
                    wait(pe, kept_ok, u * 2 - 1 + b)
                    for i in range(HG):
                        h = g * HG + i
                        mm = pe.matmul(bank[2 + b][:, i * P:(i + 1) * P], qT[:, par, h, b * P:(b + 1) * P],
                                       kT[:, par, h // TILE_HEADS, b * P:(b + 1) * P], start=True, stop=True)
                    mm.then_inc(score_ok, 1)

            def scores_ahead(p, par, g):
                if g < NHG - AHEAD:
                    scores(p, par, g + AHEAD)
                elif not (isinstance(p, int) and p == NP - 1):
                    scores(p + 1, 1 - par, g + AHEAD - NHG)

            def prob_transpose(u, g):
                for b in range(PAIR):
                    pe.wait_ge(exp_ok, u * 2 + 1 + b)
                    wait(pe, probT_ok, u * 2 - 1 + b)
                    for i in range(HG):
                        mm = pe.transpose(bank[4 + b][:, i * P:(i + 1) * P], prob[:, g, b, i, :], core.ident[:, :])
                    mm.then_inc(pt_ok, 1)

            def weigh_values(p, par, g):
                u = p * NHG + g
                if g == 0:
                    pe.wait_ge(v_ok, p + 1)
                    wait(pe, head_ok, p)
                for b in range(PAIR):
                    pe.wait_ge(probT_ok, u * 2 + 1 + b)
                    for i in range(HG):
                        h = g * HG + i
                        mm = pe.matmul(CTX[:, b * D + h * HD:b * D + (h + 1) * HD], probT[:, b, i, :], v[:, par, b, h * HD:(h + 1) * HD],
                                       start=True, stop=True)
                mm.then_inc(pv_ok, 1)

            def head_transpose(p):
                pe.wait_ge(head_ok, p + 1)
                wait(pe, res_ok, p * 2 - 1)
                for k in range(KC):
                    for b in range(PAIR):
                        mm = pe.transpose(OUT[:, k * PT + b * P:k * PT + (b + 1) * P], head[:, b, k * P:(k + 1) * P], core.ident[:, :])
                mm.then_inc(ht_ok, 1)

            def project_out(p):
                pe.wait_ge(headT_ok, p + 1)
                for b in range(PAIR):
                    for k in range(KC):
                        mm = pe.matmul(OUT[:, b * D:(b + 1) * D], headT[:, k, b * P:(b + 1) * P], wo[:, k, :], start=(k == 0), stop=(k == KC - 1))
                mm.then_inc(out_ok, 1)

            def body(p, par):
                first = isinstance(p, int) and p == 0
                last = isinstance(p, int) and p == NP - 1
                for g in range(NHG):
                    scores_ahead(p, par, g)
                    if g > 0:
                        weigh_values(p, par, g - 1)
                    elif not first:
                        weigh_values(p - 1, 1 - par, NHG - 1)
                    if g == 0 and not last:
                        project_q(p + 1)
                        project_v(p + 1)
                    if g == 1:
                        if not last:
                            project_k(p + 1)
                        if not first:
                            head_transpose(p - 1)
                    if g == 2 and not first:
                        project_out(p - 1)
                    if g == NHG - 1:
                        if not (isinstance(p, int) and p >= NP - 2):
                            ln_transpose(p + 2)
                    prob_transpose(p * NHG + g, g)

            core.wait_loaded(pe, stage, *(["w_qkv"] if self_attn else ["w_q", "w_kv"]))
            ln_transpose(0)
            project_q(0)
            project_v(0)
            project_k(0)
            ln_transpose(1)
            for g in range(AHEAD):
                scores(0, 0, g)
            core.wait_loaded(pe, stage, "w_out")
            over_steps(pe, body)
            weigh_values(NP - 1, 1, NHG - 1)
            head_transpose(NP - 1)
            project_out(NP - 1)

        @block.scalar
        def _(act):
            def layer_norm(p):
                act.wait_ge(lt_ok, p + 1)
                for k in range(KC):
                    done = act.activation(hT[:, k, :], bank[1][:, k * PT:(k + 1) * PT], ACT.Identity,
                                          scale=core.col(ln_s, k), bias=core.col(ln_b, k))
                done.then_inc(hT_ok, 1)

            def copy_q(p):
                act.wait_ge(proj_ok, p * 4 + 1)
                wait(act, q_ok, p * KC)
                for t in range(KC):
                    act.activation(q_tile[:, t, :], bank[0][:, t * PT:(t + 1) * PT], ACT.Identity,
                                   bias=core.col(bias_q[0], bias_q[1] + t)).then_inc(q_copied, 1)

            def copy_v(p, par):
                act.wait_ge(proj_ok, p * 4 + 3)
                act.activation(v[:, par, :, :], bank[1][:, :].rearrange("p (b d) -> p b d", b=PAIR), ACT.Copy).then_inc(v_ok, 1)

            def copy_head(p):
                act.wait_ge(ht_ok, p + 1)
                for k in range(KC):
                    done = act.activation(headT[:, k, :], OUT[:, k * PT:(k + 1) * PT], ACT.Identity, bias=core.col(bias_v[0], bias_v[1] + k))
                done.then_inc(headT_ok, 1)

            def copy_probs(u):
                for b in range(PAIR):
                    act.wait_ge(pt_ok, u * 2 + 1 + b)
                    wait(act, pv_ok, u)
                    act.activation(probT[:, b, :, :], bank[4 + b][:, :].rearrange("p (h q) -> p h q", h=HG), ACT.Copy).then_inc(probT_ok, 1)

            def body(p, par):
                first = isinstance(p, int) and p == 0
                last = isinstance(p, int) and p == NP - 1
                for g in range(NHG):
                    u = p * NHG + g
                    if not (first and g == 0):
                        copy_probs(u - 1)
                    act.wait_ge(shift_ok, u + 1)
                    for b in range(PAIR):
                        for i in range(HG):
                            done = act.activation(prob[:, g, b, i, :], prob[:, g, b, i, :], ACT.Exp, scale=SCALE,
                                                  bias=shift[:, g % 2, b, i:i + 1], accum_out=total[:, b, g * HG + i:g * HG + i + 1])
                        done.then_inc(exp_ok, 1)
                    if g == 0 and not last:
                        copy_q(p + 1)
                    if g == 1:
                        if not last:
                            copy_v(p + 1, 1 - par)
                        if not first:
                            copy_head(p - 1)
                    if g == NHG - 1 and not (isinstance(p, int) and p >= NP - 2):
                        layer_norm(p + 2)

            rstd_scalar(core, act, root)
            layer_norm(0)
            copy_q(0)
            copy_v(0, 0)
            layer_norm(1)
            over_steps(act, body)
            copy_probs(NP * NHG - 1)
            copy_head(NP - 1)
            load_sqrt_table(core, act)

        @block.vector
        def _(dve):
            def normalise(p):
                wait(dve, lt_ok, p)
                for b in range(PAIR):
                    i = p * PAIR + b
                    dve.tensor_scalar(xn[:, b, :], core.x[:, i, :], core.mv[:, i, 0:1], core.rstd[:, bass.ds(i, 1)],
                                      ALU.subtract, ALU.mult).then_inc(hn_ok, 1)

            def keep_scores(p, par, g):
                u = p * NHG + g
                if not (isinstance(p, int) and p == 0):
                    dve.wait_ge(pt_ok, u * 2 - 2 * NHG + 2)
                for b in range(PAIR):
                    dve.wait_ge(score_ok, u * 2 + 1 + b)
                    m = mask[:, 0:1, :] if self_attn else mask[:, bass.ds(p * PAIR + b, 1), :]
                    dve.tensor_tensor(prob[:, g, b, :, :], bank[2 + b][:, :].rearrange("p (h k) -> p h k", h=HG),
                                      m.to_broadcast([P, HG, P]), ALU.mult).then_inc(kept_ok, 1)

            def row_max(u, g):
                for b in range(PAIR):
                    dve.wait_ge(masked_ok, u * 2 + 1 + b)
                    wait(dve, shift_ok, u)
                    dve.tensor_reduce(top[:, b, :], prob[:, g, b, :, :], AX_X, ALU.max).then_inc(top_ok, 1)
                dve.wait_ge(top_ok, u * 2 + 2)
                wait(dve, exp_ok, u * 2 - 2)
                dve.tensor_scalar(shift[:, g % 2, :, :], top[:, :, :], -SCALE, None, ALU.mult).then_inc(shift_ok, 1)

            def invert(u, g):
                dve.wait_ge(exp_ok, u * 2 + 2)
                dve.reciprocal(inv[:, :, g * HG:(g + 1) * HG], total[:, :, g * HG:(g + 1) * HG]).then_inc(inv_ok, 1)

            def copy_k(p, par):
                dve.wait_ge(proj_ok, p * 4 + 4)
                dve.tensor_tensor(kT[:, par, :, :], bank[0][:, :].rearrange("p (k t) -> p k t", k=KC),
                                  core.col(bias_k[0], bias_k[1], KC)[:, :, None].to_broadcast([P, KC, PT]), ALU.add).then_inc(k_ok, 1)

            def divide(p):
                dve.wait_ge(pv_ok, p * NHG + NHG)
                dve.wait_ge(inv_ok, p * NHG + NHG)
                wait(dve, ht_ok, p)
                dve.tensor_tensor(head[:, :, :].rearrange("p b (h d) -> p (b h) d", d=HD),
                                  CTX[:, :].rearrange("p (n d) -> p n d", d=HD),
                                  inv[:, :, :].rearrange("p b h -> p (b h)")[:, :, None].to_broadcast([P, PAIR * H, HD]), ALU.mult).then_inc(head_ok, 1)

            def body(p, par):
                first = isinstance(p, int) and p == 0
                last = isinstance(p, int) and p == NP - 1
                for g in range(NHG):
                    u = p * NHG + g
                    if g < NHG - AHEAD:
                        keep_scores(p, par, g + AHEAD)
                    elif not last:
                        keep_scores(p + 1, 1 - par, g + AHEAD - NHG)
                    if not (last and g == NHG - 1):
                        row_max(u + 1, (g + 1) % NHG)
                    if g == 1 and not last:
                        copy_k(p + 1, 1 - par)
                    if g > 0:
                        invert(u - 1, g - 1)
                    elif not first:
                        invert(u - 1, NHG - 1)
                        divide(p - 1)
                    if g == 2 and not (isinstance(p, int) and p >= NP - 2):
                        normalise(p + 2)
                    if g == NHG - 1 and not first:
                        new_rows(core, dve, res_ok, stat, p - 1, OUT[:, :].rearrange("p (b d) -> p b d", b=PAIR), out_ok, out_row)

            rstd_vector(core, dve, root, rstep)
            normalise(0)
            dve.wait_ge(mask_in, DMA)
            core.wait_loaded(dve, stage, "row")
            normalise(1)
            copy_k(0, 0)
            for g in range(AHEAD):
                keep_scores(0, 0, g)
            row_max(0, 0)
            over_steps(dve, body)
            invert(NP * NHG - 1, NHG - 1)
            divide(NP - 1)
            new_rows(core, dve, res_ok, stat, NP - 1, OUT[:, :].rearrange("p (b d) -> p b d", b=PAIR), out_ok, out_row)


def mlp(core, stage, ln_s, ln_b, b1, gelu):
    nc = core.nc
    NF = 4 * D // P
    with ExitStack() as ctx:
        sb = Space(core, stage)
        sem = Signals(core, ctx, f"m{stage}_")
        w1, w2, out_row = (core.weight(stage, w) for w in ("w1", "w2", "row"))
        (w1_hi, w1_lo), (w2_hi, w2_lo) = (
            (core.place_r(f"m{stage}_{w}_hi", hi_at, shape), core.place_r(f"m{stage}_{w}_lo", core.weight_at(stage, w), shape))
            for w, hi_at, shape in (("w1", LATE, [P, KC, 4 * D]), ("w2", LATE + KC * 4 * D, [P, NF, D])))
        xn = sb("xn", [P, PAIR, D])
        hT, (hT_hi, hT_lo) = sb.split(f"m{stage}_hT", [P, KC, PT])
        gT, (gT_hi, gT_lo) = sb.split(f"m{stage}_gT", [P, 2, NF, PT])
        w1_halves = [slice(h * (2 * D), (h + 1) * (2 * D)) for h in range(2)]
        bank = core.bank
        root, rstep = sem("root"), sem("rstep")
        hn_ok, lt_ok, hT_ok = sem("hn_ok"), sem("lt_ok"), sem("hT_ok")
        up_ok, gelu_ok, out_ok, res_ok, stat = sem("up_ok"), sem("gelu_ok"), sem("out_ok"), sem("res_ok"), sem("stat")
        w_hi_ok, w1_ok, w2_ok = sem("w_hi_ok"), sem("w1_ok"), sem("w2_ok")
        hT_raw, hT_hi_ok, g_hi_ok, g_ok = sem("hT_raw"), sem("hT_hi_ok"), sem("g_hi_ok"), sem("g_ok")
        block = ctx.enter_context(nc.Block())

        def within(p, ahead):
            return not isinstance(p, int) or p + ahead < NP

        @block.sync
        def _(sp):
            core.load(sp, stage)

        @block.gpsimd
        def _(gp):
            def rows_lo(p):
                gp.wait_ge(hT_hi_ok, p + 1)
                gp.tensor_tensor(hT_lo[:, :, :], hT, hT_hi[:, :, :], ALU.subtract).then_inc(hT_ok, 1)

            def hidden_lo(p, par):
                for c in range(NF // 2):
                    two = slice(2 * c, 2 * c + 2)
                    gp.wait_ge(g_hi_ok, p * (NF // 2) + c + 1)
                    gp.tensor_tensor(gT_lo[:, par, two, :], gT[:, par, two, :], gT_hi[:, par, two, :], ALU.subtract).then_inc(g_ok, 1)

            def body(p, par):
                if within(p, 2):
                    rows_lo(p + 2)
                if within(p, 1):
                    hidden_lo(p + 1, 1 - par)

            rows_lo(0)
            gp.wait_ge(w_hi_ok, 3)
            gp.tensor_tensor(w2_lo[:, :, :], w2, w2_hi[:, :, :], ALU.subtract).then_inc(w2_ok, 1)
            rows_lo(1)
            hidden_lo(0, 0)
            over_steps(gp, body)

        @block.tensor
        def _(pe):
            def ln_transpose(p):
                pe.wait_ge(hn_ok, p * PAIR + PAIR)
                wait(pe, hT_raw, p)
                for k in range(KC):
                    for b in range(PAIR):
                        mm = pe.transpose(bank[6][:, k * PT + b * P:k * PT + (b + 1) * P], xn[:, b, k * P:(k + 1) * P], core.ident[:, :])
                mm.then_inc(lt_ok, 1)

            def up(p):
                pe.wait_ge(hT_ok, p + 1)
                for f in range(NF):
                    if isinstance(p, int) and p == 0 and f % (NF // 2) == 0:
                        pe.wait_ge(w1_ok, f // (NF // 2) + 1)
                    if f % 2 == 0:
                        wait(pe, gelu_ok, (p - 1) * NF + f + 2)
                    at = bank[f // 2][:, (f % 2) * PT:(f % 2 + 1) * PT]
                    for k in range(KC):
                        mm = split_product(pe, at, [w[:, k, f * P:(f + 1) * P] for w in (w1_hi, w1_lo)],
                                           [h[:, k, :] for h in (hT_hi, hT_lo)], k == 0, k == KC - 1)
                    if f % 2:
                        mm.then_inc(up_ok, 1)

            def down(p, par):
                pe.wait_ge(g_ok, (p + 1) * (NF // 2))
                wait(pe, res_ok, p * 2 - 3)
                for b in range(PAIR):
                    for f in range(NF):
                        mm = split_product(pe, bank[4 + par][:, b * D:(b + 1) * D], [g[:, par, f, b * P:(b + 1) * P] for g in (gT_hi, gT_lo)],
                                           [w[:, f, :] for w in (w2_hi, w2_lo)], f == 0, f == NF - 1)
                mm.then_inc(out_ok, 1)

            def body(p, par):
                if within(p, 1):
                    up(p + 1)
                if within(p, 2):
                    ln_transpose(p + 2)
                if isinstance(p, int) and p == 0:
                    pe.wait_ge(w2_ok, 1)
                down(p, par)

            ln_transpose(0)
            up(0)
            ln_transpose(1)
            over_steps(pe, body)

        @block.scalar
        def _(act):
            def layer_norm(p):
                act.wait_ge(lt_ok, p + 1)
                for k in range(KC):
                    done = act.activation(hT[:, k, :], bank[6][:, k * PT:(k + 1) * PT], ACT.Identity,
                                          scale=core.col(ln_s, k), bias=core.col(ln_b, k))
                done.then_inc(hT_raw, 1)
                act.wait_ge(hT_raw, p + 1)
                act.activation(hT_hi[:, :, :], hT, ACT.Copy).then_inc(hT_hi_ok, 1)

            def activate(p, par):
                for f in range(NF):
                    if f % 2 == 0:
                        act.wait_ge(up_ok, p * (NF // 2) + f // 2 + 1)
                    act.activation(gT[:, par, f, :], bank[f // 2][:, (f % 2) * PT:(f % 2 + 1) * PT], gelu,
                                   bias=core.col(b1, f)).then_inc(gelu_ok, 1)

            def hidden_hi(p, par):
                for c in range(NF // 2):
                    two = slice(2 * c, 2 * c + 2)
                    act.wait_ge(gelu_ok, p * NF + 2 * c + 2)
                    act.activation(gT_hi[:, par, two, :], gT[:, par, two, :], ACT.Copy).then_inc(g_hi_ok, 1)

            def body(p, par):
                if within(p, 1):
                    activate(p + 1, 1 - par)
                if within(p, 2):
                    layer_norm(p + 2)
                if within(p, 1):
                    hidden_hi(p + 1, 1 - par)

            rstd_scalar(core, act, root)
            core.wait_loaded(act, stage, "w1")
            for part in w1_halves:
                act.activation(w1_hi[:, :, part], w1[:, :, part], ACT.Copy).then_inc(w_hi_ok, 1)
            layer_norm(0)
            core.wait_loaded(act, stage, "w2")
            act.activation(w2_hi[:, :, :], w2, ACT.Copy).then_inc(w_hi_ok, 1)
            activate(0, 0)
            layer_norm(1)
            hidden_hi(0, 0)
            over_steps(act, body)
            load_sqrt_table(core, act)

        @block.vector
        def _(dve):
            def normalise(p):
                wait(dve, lt_ok, p)
                for b in range(PAIR):
                    i = p * PAIR + b
                    dve.tensor_scalar(xn[:, b, :], core.x[:, i, :], core.mv[:, i, 0:1], core.rstd[:, bass.ds(i, 1)],
                                      ALU.subtract, ALU.mult).then_inc(hn_ok, 1)

            def body(p, par):
                if within(p, 2):
                    normalise(p + 2)
                new_rows(core, dve, res_ok, stat, p, bank[4 + par][:, :].rearrange("p (b d) -> p b d", b=PAIR), out_ok, out_row)

            rstd_vector(core, dve, root, rstep)
            normalise(0)
            for i, part in enumerate(w1_halves):
                dve.wait_ge(w_hi_ok, i + 1)
                dve.tensor_tensor(w1_lo[:, :, part], w1[:, :, part], w1_hi[:, :, part], ALU.subtract).then_inc(w1_ok, 1)
            normalise(1)
            core.wait_loaded(dve, stage, "row")
            over_steps(dve, body)


def single_attention(core, stage):
    nc = core.nc
    SCALE = float(D) ** -0.5
    pre = "L2_xattn_"
    with ExitStack() as ctx:
        sb = Space(core, stage)
        sem = Signals(core, ctx, f"s_")
        wo, alpha = core.weight(stage, "w_o"), core.weight(stage, "alpha")
        wq, wk, wv = ((core.weight(stage, w), core.place_r(f"s_{w}_hi", LATE + i * KC * D, [P, KC, D]),
                       core.place_r(f"s_{w}_lo", core.weight_at(stage, w), [P, KC, D])) for i, w in enumerate(("w_q", "w_k", "w_v")))
        x_in = sb("x_in", [P, PAIR, D])
        xT, xT_r = sb.split("s_xT", [P, KC, PT])
        kv_in, kv_r = sb.split("s_kv", [P, KC, PT])
        qT, kT = (sb(t, [P, KC, PT]) for t in ("qT", "kT"))
        v = sb("v", [P, PAIR, D])
        prob, probT = sb("prob", [P, PAIR, P]), sb("probT", [P, PAIR, P])
        headT = sb("headT", [P, KC, PT])
        scaled = sb("scaled", [P, PAIR, D])
        top, shift, total, inv = (sb(t, [P, PAIR]) for t in ("top", "shift", "total", "inv"))
        bank = core.bank
        xi_ok, xt_ok, xT_ok, kv_ok = sem("xi_ok"), sem("xt_ok"), sem("xT_ok"), sem("kv_ok")
        q_ready, k_ready, v_ready = sem("q_ready"), sem("k_ready"), sem("v_ready")
        q_ok, k_ok, v_ok = sem("q_ok"), sem("k_ok"), sem("v_ok")
        score_ok, top_ok, shift_ok, exp_ok, inv_ok, prob_ok = (sem(s) for s in ("score", "top_ok", "shift_ok", "exp", "inv_ok", "prob_ok"))
        pt_ok, probT_ok, pv_ok, headT_ok, out_ok = (sem(s) for s in ("pt", "probT_ok", "pv", "headT_ok", "out"))
        scaled_ok, res_ok, stat = sem("scaled_ok"), sem("res_ok"), sem("stat")
        w_hi_ok, w_ok, xT_raw, xT_hi_ok = sem("w_hi_ok"), sem("w_ok"), sem("xT_raw"), sem("xT_hi_ok")
        kv_in_ok, kv_hi_ok = sem("kv_in_ok"), sem("kv_hi_ok")
        block = ctx.enter_context(nc.Block())

        def within(p, ahead):
            return not isinstance(p, int) or p + ahead < NP

        halves = lambda t, n: t[:, :].rearrange("p (k t) -> p k t", k=n)

        @block.sync
        def _(sp):
            def body(p):
                wait(sp, v_ready, p)
                sp.dma_start(kv_in[:, :, :], core.cT[:, :, bass.ts(p, PT)]).then_inc(kv_in_ok, DMA)
            core.load(sp, stage)
            over_pairs(sp, body)

        @block.gpsimd
        def _(gp):
            def rows_lo(p):
                gp.wait_ge(xT_hi_ok, p + 1)
                gp.tensor_tensor(xT_r[1][:, :, :], xT, xT_r[0][:, :, :], ALU.subtract).then_inc(xT_ok, 1)

            def context_lo(p):
                gp.wait_ge(kv_hi_ok, p + 1)
                gp.tensor_tensor(kv_r[1][:, :, :], kv_in, kv_r[0][:, :, :], ALU.subtract).then_inc(kv_ok, 1)

            def body(p, par):
                if within(p, 1):
                    context_lo(p + 1)
                if within(p, 2):
                    rows_lo(p + 2)

            rows_lo(0)
            context_lo(0)
            rows_lo(1)
            over_steps(gp, body)

        @block.tensor
        def _(pe):
            def x_transpose(p):
                pe.wait_ge(xi_ok, p + 1)
                wait(pe, xT_raw, p)
                for k in range(KC):
                    for b in range(PAIR):
                        mm = pe.transpose(bank[0][:, k * PT + b * P:k * PT + (b + 1) * P], x_in[:, b, k * P:(k + 1) * P], core.ident[:, :])
                mm.then_inc(xt_ok, 1)

            def project(p, to, w, moving, ready):
                for t in range(KC):
                    for k in range(KC):
                        mm = split_product(pe, to[:, t * PT:(t + 1) * PT], [part[:, k, t * P:(t + 1) * P] for part in w[1:]],
                                           [part[:, k, :] for part in moving], k == 0, k == KC - 1)
                mm.then_inc(ready, 1)

            def project_qk(p):
                pe.wait_ge(xT_ok, p + 1)
                wait(pe, q_ok, p)
                project(p, bank[1], wq, xT_r, q_ready)
                wait(pe, k_ok, p)
                pe.wait_ge(kv_ok, p + 1)
                project(p, bank[2], wk, kv_r, k_ready)

            def project_v(p):
                pe.wait_ge(kv_ok, p + 1)
                wait(pe, v_ok, p)
                for b in range(PAIR):
                    for k in range(KC):
                        mm = split_product(pe, bank[3][:, b * D:(b + 1) * D], [part[:, k, b * P:(b + 1) * P] for part in kv_r],
                                           [part[:, k, :] for part in wv[1:]], k == 0, k == KC - 1)
                mm.then_inc(v_ready, 1)

            def scores(p):
                pe.wait_ge(q_ok, p + 1)
                pe.wait_ge(k_ok, p + 1)
                wait(pe, exp_ok, p)
                for b in range(PAIR):
                    for k in range(KC):
                        mm = pe.matmul(bank[4][:, b * P:(b + 1) * P], qT[:, k, b * P:(b + 1) * P], kT[:, k, b * P:(b + 1) * P],
                                       start=(k == 0), stop=(k == KC - 1))
                mm.then_inc(score_ok, 1)

            def prob_transpose(p):
                pe.wait_ge(prob_ok, p + 1)
                for b in range(PAIR):
                    mm = pe.transpose(bank[5][:, b * P:(b + 1) * P], prob[:, b, :], core.ident[:, :])
                mm.then_inc(pt_ok, 1)

            def weigh_values(p):
                pe.wait_ge(probT_ok, p + 1)
                pe.wait_ge(v_ok, p + 1)
                wait(pe, headT_ok, p)
                for k in range(KC):
                    for b in range(PAIR):
                        mm = pe.matmul(bank[6][:, k * PT + b * P:k * PT + (b + 1) * P], v[:, b, k * P:(k + 1) * P], probT[:, b, :], start=True, stop=True)
                mm.then_inc(pv_ok, 1)

            def project_out(p):
                pe.wait_ge(headT_ok, p + 1)
                wait(pe, scaled_ok, p)
                for b in range(PAIR):
                    for k in range(KC):
                        mm = pe.matmul(bank[7][:, b * D:(b + 1) * D], headT[:, k, b * P:(b + 1) * P], wo[:, k, :], start=(k == 0), stop=(k == KC - 1))
                mm.then_inc(out_ok, 1)

            def body(p, par):
                scores(p)
                if within(p, 1):
                    project_qk(p + 1)
                prob_transpose(p)
                if within(p, 1):
                    project_v(p + 1)
                weigh_values(p)
                if within(p, 2):
                    x_transpose(p + 2)
                project_out(p)

            x_transpose(0)
            pe.wait_ge(w_ok, 3)
            core.wait_loaded(pe, stage, "w_o")
            project_qk(0)
            project_v(0)
            x_transpose(1)
            over_steps(pe, body)

        @block.scalar
        def _(act):
            def copy_x(p):
                act.wait_ge(xt_ok, p + 1)
                act.activation(xT[:, :, :], halves(bank[0], KC), ACT.Copy).then_inc(xT_raw, 1)
                act.wait_ge(xT_raw, p + 1)
                act.activation(xT_r[0][:, :, :], xT, ACT.Copy).then_inc(xT_hi_ok, 1)

            def context_hi(p):
                act.wait_ge(kv_in_ok, p * DMA + DMA)
                act.activation(kv_r[0][:, :, :], kv_in, ACT.Copy).then_inc(kv_hi_ok, 1)

            def copy_v(p):
                act.wait_ge(v_ready, p + 1)
                wait(act, pv_ok, p)
                act.activation(v[:, :, :], halves(bank[3], PAIR), ACT.Copy).then_inc(v_ok, 1)

            def body(p, par):
                if within(p, 1):
                    context_hi(p + 1)
                act.wait_ge(shift_ok, p + 1)
                for b in range(PAIR):
                    done = act.activation(prob[:, b, :], bank[4][:, b * P:(b + 1) * P], ACT.Exp, scale=SCALE, bias=shift[:, b:b + 1],
                                          accum_out=total[:, b:b + 1])
                done.then_inc(exp_ok, 1)
                act.wait_ge(pt_ok, p + 1)
                act.activation(probT[:, :, :], bank[5][:, 0:PT].rearrange("p (b t) -> p b t", b=PAIR), ACT.Copy).then_inc(probT_ok, 1)
                if within(p, 1):
                    copy_v(p + 1)
                if within(p, 2):
                    copy_x(p + 2)

            core.wait_loaded(act, stage, "w_q", "w_k", "w_v")
            for full, hi, _ in (wq, wk, wv):
                act.activation(hi[:, :, :], full, ACT.Copy).then_inc(w_hi_ok, 1)
            copy_x(0)
            context_hi(0)
            copy_v(0)
            copy_x(1)
            over_steps(act, body)
            load_sqrt_table(core, act)

        @block.vector
        def _(dve):
            def fetch(p):
                wait(dve, xt_ok, p)
                dve.tensor_scalar(x_in[:, :, :], core.x[:, bass.ds(p * PAIR, PAIR), :], 1.0, None, ALU.mult).then_inc(xi_ok, 1)

            def copy_q(p):
                dve.wait_ge(q_ready, p + 1)
                dve.tensor_copy(qT[:, :, :], halves(bank[1], KC)).then_inc(q_ok, 1)

            def copy_k(p):
                dve.wait_ge(k_ready, p + 1)
                dve.tensor_copy(kT[:, :, :], halves(bank[2], KC)).then_inc(k_ok, 1)

            def scale_update(p):
                dve.wait_ge(out_ok, p + 1)
                wait(dve, res_ok, p)
                dve.tensor_scalar(scaled[:, :, :], halves(bank[7], PAIR), alpha[:, 0:1], None, ALU.mult).then_inc(scaled_ok, 1)

            def body(p, par):
                first = isinstance(p, int) and p == 0
                dve.wait_ge(score_ok, p + 1)
                dve.tensor_reduce(top[:, :], bank[4][:, 0:PT].rearrange("p (b t) -> p b t", b=PAIR), AX_X, ALU.max).then_inc(top_ok, 1)
                dve.wait_ge(top_ok, p + 1)
                dve.tensor_scalar(shift[:, :], top[:, :], -SCALE, None, ALU.mult).then_inc(shift_ok, 1)
                if within(p, 1):
                    copy_q(p + 1)
                dve.wait_ge(exp_ok, p + 1)
                dve.reciprocal(inv[:, :], total[:, :]).then_inc(inv_ok, 1)
                dve.wait_ge(inv_ok, p + 1)
                dve.tensor_tensor(prob[:, :, :], prob[:, :, :], inv[:, :, None].to_broadcast([P, PAIR, P]), ALU.mult).then_inc(prob_ok, 1)
                if within(p, 1):
                    copy_k(p + 1)
                if within(p, 2):
                    fetch(p + 2)
                if not first:
                    scale_update(p - 1)
                dve.wait_ge(pv_ok, p + 1)
                dve.tensor_copy(headT[:, :, :], halves(bank[6], KC)).then_inc(headT_ok, 1)
                if not first:
                    new_rows(core, dve, res_ok, stat, p - 1, scaled[:, :, :], scaled_ok)

            fetch(0)
            for i, (full, hi, lo) in enumerate((wq, wk, wv)):
                dve.wait_ge(w_hi_ok, i + 1)
                dve.tensor_tensor(lo[:, :, :], full, hi[:, :, :], ALU.subtract).then_inc(w_ok, 1)
            fetch(1)
            core.wait_loaded(dve, stage, "alpha")
            copy_q(0)
            copy_k(0)
            over_steps(dve, body)
            scale_update(NP - 1)
            new_rows(core, dve, res_ok, stat, NP - 1, scaled[:, :, :], scaled_ok)


def recurrence(core, stage):
    nc = core.nc
    J = 8
    HT = P // J
    F = 5
    FK, FW, FV, FR, FG = range(F)
    R = 32
    RD = 64
    UNITS = KC * PAIR
    pre = "L3_xattn_"
    with ExitStack() as ctx:
        sb = Space(core, stage)
        sem = Signals(core, ctx, f"r_")
        maa_w1, maa_w2, maa_w2g, td_w1, td_w2 = (core.weight(stage, n) for n in ("maa_w1", "maa_w2", "maa_w2g", "td_w1", "td_w2"))
        w = {n: core.weight(stage, n) for n in ("Wk", "Wv", "Wr", "Wg", "Wo", "Wfk", "Wfr", "Wfv")}
        state0 = core.weight(stage, "state0").rearrange("p (k b j) -> p k b j", k=KC, b=NB)
        gn_rows = sb("gn_rows", [P, 2, D])
        pick = sb("pick", [P, J, P])
        head_sum = sb("head_sum", [P, HT])
        xn = sb("xn", [P, PAIR, D])
        xa = sb("xa", [P, KC, PAIR, P + 1])
        sx = sb("sx", [P, KC, PAIR, P])
        xmaa = sb("xmaa", [P, KC, PAIR, P])
        low, low_g = sb("low", [P, PT]), sb("low_g", [R, PT])
        mixed = sb("mixed", [P, F, KC, PT])
        td_low = sb("td_low", [RD, PT])
        kT, vT, rT = (sb(n, [P, 2, KC, PT]) for n in ("kT", "vT", "rT"))
        rate = sb("rate", [P, 2, KC, PT])
        g_tanh = sb("g_tanh", [P, PAIR, D])
        gate = sb("gate", [P, 2, PAIR, D])
        decay = sb("decay", [P, 2, J, P + 1])
        kv = sb("kv", [P, J, P + 1])
        states = sb("states", [P, J, P + 1])
        prod = sb("prod", [P, 2, J, P])
        og = sb("og", [P, UNITS, HT, J])
        sq = sb("sq", [P, UNITS, HT, J])
        msum, mean, vsum, gstd, grstd = (sb(n, [P, UNITS * HT]) for n in ("msum", "mean", "vsum", "gstd", "grstd"))
        zT = sb("zT", [P, KC, PT])
        std2, rstd2 = sb("std2", [P, PAIR]), sb("rstd2", [P, PAIR])
        xn2 = sb("xn2", [P, PAIR, D])
        xc = sb("xc", [P, KC, PAIR, P + 1])
        sx2 = sb("sx2", [P, KC, PAIR, P])
        xk2, xr2 = sb("xk2", [P, KC, PT]), sb("xr2", [P, KC, PT])
        relu, kkT = sb("relu", [P, KC, PT]), sb("kkT", [P, KC, PT])
        r_tanh = sb("r_tanh", [P, PAIR, D])
        gated = sb("gated", [P, PAIR, D])
        result = sb("result", [P, PAIR, D])
        bank = core.bank
        VB = core.banks[:, 0:2, :].rearrange("p n c -> p (n c)").rearrange("p (j t) -> p j t", j=J)
        OG = bank[2]
        MIX = [bank[i] for i in (4, 5, 3, 4, 5)]

        gn_in = sem("gn_in")
        root, rstep, made = sem("root"), sem("rstep"), sem("made")
        TILES = ["xa", "low", "td", "k", "r", "v", "rate", "g", "z", "out", "xc", "kk", "rr", "ff"]
        ready = {n: sem(n + "_ready") for n in TILES}
        read = {n: sem(n + "_read") for n in TILES}
        f_ready, f_read = sem("f_ready"), sem("f_read")
        xn_ok, first_ok, xmaa_ok, mix_ok = sem("xn_ok"), sem("first_ok"), sem("xmaa_ok"), sem("mix_ok")
        vb_ready, kv_ok, decay_ok, scan_ok, q_ok, prod_ok, sum_ready = (sem(n) for n in ("vb", "kv_ok", "decay_ok", "scan_ok", "q_ok", "prod_ok", "sum"))
        og_read, gn_step, vsum_ok, gstd_ok, z_ok = sem("og_read"), sem("gn_step"), sem("vsum_ok"), sem("gstd_ok"), sem("z_ok")
        st_ok, mv2_ok, std2_ok, c_step, xn2_ok, c_first = sem("st_ok"), sem("mv2_ok"), sem("std2_ok"), sem("c_step"), sem("xn2_ok"), sem("c_first")
        xk_step, xk_ok, relu_ok, result_ok, stored = (sem(n) for n in ("xk_step", "xk_ok", "relu_ok", "result_ok", "stored"))
        g_tanh_ok, gn_ok, z_step = sem("g_tanh_ok"), sem("gn_ok"), sem("z_step")
        block = ctx.enter_context(nc.Block())
        ctx_rows = core.cT[:, :, :].rearrange("p k (b t) -> p k b t", b=NB)

        def static(p):
            return isinstance(p, int)

        def exists(p):
            return not static(p) or 0 <= p < NP

        def over_slots(eng, slot):
            over_steps(eng, slot)
            slot(NP, NP % 2)

        flat = lambda t: t.rearrange("p k b t -> p k (b t)")
        halves = lambda t, n=2: t[:, :].rearrange("p (k t) -> p k t", k=n)

        @block.sync
        def _(sp):
            core.load(sp, stage)
            for i, n in enumerate(("gn_w", "gn_b")):
                sp.dma_start(gn_rows[:, i, :], core.dram["row_" + n]).then_inc(gn_in, DMA)

            def slot(p, par):
                if exists(p - 1):
                    sp.wait_ge(result_ok, p)
                    sp.dma_start(core.out[bass.ds((p - 1) * PAIR, PAIR), :, :].rearrange("b t d -> t b d"), result[:, :, :]).then_inc(stored, DMA)
            over_slots(sp, slot)
            sp.wait_ge(stored, NP * DMA)

        @block.gpsimd
        def _(gp):
            gp.memset(pick[:, :, :], 0.0).then_inc(made, 1)
            gp.memset(head_sum[:, :], 1.0).then_inc(made, 1)
            gp.memset(decay[:, :, :, :], 0.0).then_inc(made, 1)
            gp.wait_ge(made, 3)
            gp.affine_select(out=pick[:, :, :].rearrange("p j (h i) -> p j h i", i=J), in_=pick[:, :, :].rearrange("p j (h i) -> p j h i", i=J),
                             compare_op=ALU.not_equal, fill=1.0, base=0, pattern=[[-1, J], [-J, HT], [0, J]], channel_multiplier=1).then_inc(made, 1)
            gp.affine_select(out=head_sum[:, :], in_=head_sum[:, :], compare_op=ALU.is_ge, fill=0.0,
                             base=0, pattern=[[-J, HT]], channel_multiplier=1).then_inc(made, 1)
            gp.wait_ge(made, 5)
            gp.affine_select(out=head_sum[:, :], in_=head_sum[:, :], compare_op=ALU.is_ge, fill=0.0,
                             base=J - 1, pattern=[[J, HT]], channel_multiplier=-1).then_inc(made, 1)

            def times_r(p, par, s):
                k, b = s // PAIR, s % PAIR
                gp.wait_ge(read["r"], p + 1)
                gp.wait_ge(q_ok, p * UNITS + (s + 1))
                gp.tensor_tensor(prod[:, s % 2, :, :], prod[:, s % 2, :, :],
                                 rT[:, par, k, b * P:(b + 1) * P][:, None, :].to_broadcast([P, J, P]), ALU.mult).then_inc(prod_ok, 1)

            def add_xa(a):
                for f in range(F):
                    gp.wait_ge(f_read, a * F + (f + 1))
                    gp.tensor_tensor(mixed[:, f, :, :].rearrange("p k (b t) -> p k b t", b=PAIR), mixed[:, f, :, :].rearrange("p k (b t) -> p k b t", b=PAIR),
                                     xa[:, :, :, 1:P + 1], ALU.add).then_inc(mix_ok, 1)

            def scale_and_gate(c, par):
                per_token = og[:, :, :, :].rearrange("p (b k) h j -> p b (k h j)", b=PAIR)
                row = lambda i: gn_rows[:, i:i + 1, :].to_broadcast([P, PAIR, D])
                gp.wait_ge(gn_ok, c + 1)
                gp.tensor_tensor(per_token, per_token, row(0), ALU.mult).then_inc(z_step, 1)
                gp.wait_ge(z_step, c * 2 + 1)
                gp.tensor_tensor(per_token, per_token, row(1), ALU.add).then_inc(z_step, 1)
                gp.wait_ge(z_step, c * 2 + 2)
                gp.wait_ge(read["g"], c + 1)
                gp.tensor_tensor(per_token, per_token, gate[:, par, :, :], ALU.mult).then_inc(z_ok, 1)

            def slot(p, par):
                if exists(p):
                    for s in range(UNITS):
                        if s == UNITS - 1 and exists(p + 1):
                            add_xa(p + 1)
                        times_r(p, par, s)
                    scale_and_gate(p, par)
            add_xa(0)
            gp.wait_ge(gn_in, 2 * DMA)
            over_steps(gp, slot)

        @block.tensor
        def _(pe):
            def spread_v(p, par, s):
                k, b = s // PAIR, s % PAIR
                pe.wait_ge(read["v"], p + 1)
                if not (static(p) and p == 0 and s == 0):
                    pe.wait_ge(kv_ok, p * (2 * UNITS) + (2 * s - 1))
                for j in range(J):
                    mm = pe.matmul(VB[:, j, :], pick[:, j, :], vT[:, par, k, b * P:(b + 1) * P], start=True, stop=True)
                mm.then_inc(vb_ready, 1)

            def sum_heads(p, s):
                pe.wait_ge(prod_ok, p * UNITS + (s + 1))
                if s == 0:
                    wait(pe, og_read, p)
                b, k = s % PAIR, s // PAIR
                for j in range(J):
                    at = (b * KC + k) * P + j * HT
                    mm = pe.matmul(OG[:, at:at + HT], prod[:, s % 2, j, :], head_sum[:, :], start=True, stop=True)
                mm.then_inc(sum_ready, 1)

            def transposes(to, src):
                for k in range(KC):
                    for b in range(PAIR):
                        mm = pe.transpose(to[:, k * PT + b * P:k * PT + (b + 1) * P], src[:, b, k * P:(k + 1) * P], core.ident[:, :])
                return mm

            def feature_major(to, weight, moving):
                for t in range(KC):
                    for k in range(KC):
                        mm = pe.matmul(to[:, t * PT:(t + 1) * PT], weight[:, k, t * P:(t + 1) * P], moving[:, k, :], start=(k == 0), stop=(k == KC - 1))
                return mm

            def token_major(to, source, weight):
                for b in range(PAIR):
                    for k in range(KC):
                        mm = pe.matmul(to[:, b * D:(b + 1) * D], source[:, k, b * P:(b + 1) * P], weight[:, k, :], start=(k == 0), stop=(k == KC - 1))
                return mm

            def a_transpose(a):
                pe.wait_ge(xn_ok, a * PAIR + PAIR)
                wait(pe, read["v"], a)
                transposes(bank[3], xn).then_inc(ready["xa"], 1)

            def a_low(a):
                pe.wait_ge(xmaa_ok, a * KC + KC)
                pe.wait_ge(read["xa"], a + 1)
                for m0, m1 in ((0, P), (P, F * R)):
                    at = 0 if m0 == 0 else PT
                    for k in range(KC):
                        mm = pe.matmul(bank[3][0:m1 - m0, at:at + PT], maa_w1[:, k, m0:m1], flat(xmaa[:, :, :, :])[:, k, :], start=(k == 0), stop=(k == KC - 1))
                mm.then_inc(ready["low"], 1)

            def a_mix(a):
                pe.wait_ge(read["low"], a + 1)
                for f in range(F):
                    if f == 0:
                        wait(pe, read["g"], a)
                    elif f == 1:
                        wait(pe, read["rate"], a)
                    elif f > 2:
                        pe.wait_ge(f_read, a * F + (f - 2))
                    r0 = R * f if f < FG else 0
                    src, rhs = (maa_w2, low) if f < FG else (maa_w2g, low_g)
                    for k in range(KC):
                        mm = pe.matmul(MIX[f][:, k * PT:(k + 1) * PT], src[r0:r0 + R, k * P:(k + 1) * P], rhs[r0:r0 + R, :], start=True, stop=True)
                    mm.then_inc(f_ready, 1)

            def project_k(a):
                pe.wait_ge(mix_ok, a * F + FW + 1)
                pe.wait_ge(f_read, a * F + 3)
                for k in range(KC):
                    mm = pe.matmul(bank[3][0:RD, 0:PT], td_w1[:, k, :], mixed[:, FW, k, :], start=(k == 0), stop=(k == KC - 1))
                mm.then_inc(ready["td"], 1)
                pe.wait_ge(f_read, a * F + F)
                feature_major(bank[5], w["Wk"], mixed[:, FK, :, :]).then_inc(ready["k"], 1)

            def project_v(a):
                pe.wait_ge(mix_ok, a * F + FV + 1)
                pe.wait_ge(read["td"], a + 1)
                feature_major(bank[3], w["Wv"], mixed[:, FV, :, :]).then_inc(ready["v"], 1)
                pe.wait_ge(read["k"], a + 1)
                for t in range(KC):
                    mm = pe.matmul(bank[5][:, t * PT:(t + 1) * PT], td_w2[:, t * P:(t + 1) * P], td_low[:, :], start=True, stop=True)
                mm.then_inc(ready["rate"], 1)

            def project_r(a):
                pe.wait_ge(mix_ok, a * F + FR + 1)
                feature_major(bank[4], w["Wr"], mixed[:, FR, :, :]).then_inc(ready["r"], 1)

            def project_g(a):
                pe.wait_ge(read["r"], a + 1)
                pe.wait_ge(mix_ok, a * F + FG + 1)
                token_major(bank[4], mixed[:, FG, :, :], w["Wg"]).then_inc(ready["g"], 1)

            def slot(p, par):
                u, a, c = exists(p), exists(p + 1), exists(p - 1)
                if c:
                    pe.wait_ge(z_ok, p)
                    if not static(p) or p > 1:
                        pe.wait_ge(read["rr"], p - 1)
                    transposes(bank[6], og[:, :, :, :].rearrange("p (b k) h j -> p b (k h j)", b=PAIR)).then_inc(ready["z"], 1)
                if u:
                    spread_v(p, par, 1)
                if c:
                    pe.wait_ge(read["z"], p)
                    if not static(p) or p > 1:
                        pe.wait_ge(read["ff"], p - 1)
                    token_major(bank[7], zT, w["Wo"]).then_inc(ready["out"], 1)
                if a:
                    a_transpose(p + 1)
                if u:
                    project_g(p)
                    sum_heads(p, 0)
                    spread_v(p, par, 2)
                if a:
                    a_low(p + 1)
                if u:
                    sum_heads(p, 1)
                if c:
                    pe.wait_ge(xn2_ok, p * PAIR)
                    transposes(bank[6], xn2).then_inc(ready["xc"], 1)
                if u:
                    spread_v(p, par, 3)
                if a:
                    a_mix(p + 1)
                if u:
                    sum_heads(p, 2)
                if a:
                    project_k(p + 1)
                if u:
                    sum_heads(p, 3)
                if a:
                    project_v(p + 1)
                if c:
                    pe.wait_ge(xk_ok, p * (2 * KC))
                    pe.wait_ge(read["out"], p)
                    feature_major(bank[7], w["Wfk"], xk2).then_inc(ready["kk"], 1)
                if a:
                    spread_v(p + 1, 1 - par, 0)
                    project_r(p + 1)
                if c:
                    pe.wait_ge(read["xc"], p)
                    token_major(bank[6], xr2, w["Wfr"]).then_inc(ready["rr"], 1)
                    pe.wait_ge(read["kk"], p)
                    token_major(bank[7], kkT, w["Wfv"]).then_inc(ready["ff"], 1)

            core.wait_loaded(pe, stage, "maa_w1", "maa_w2", "maa_w2g")
            a_transpose(0)
            a_low(0)
            a_mix(0)
            core.wait_loaded(pe, stage, "td_w1", "td_w2", "Wk", "Wv", "Wr", "Wg")
            project_k(0)
            project_v(0)
            pe.wait_ge(made, 6)
            spread_v(0, 0, 0)
            project_r(0)
            core.wait_loaded(pe, stage, "Wo", "Wfk", "Wfr", "Wfv")
            over_slots(pe, slot)

        @block.scalar
        def _(act):
            def copy_xa(a):
                act.wait_ge(ready["xa"], a + 1)
                wait(act, mix_ok, a * F)
                for k in range(KC):
                    done = act.activation(xa[:, k, :, 1:P + 1], halves(bank[3])[:, k, :].rearrange("p (b t) -> p b t", b=PAIR), ACT.Identity,
                                          scale=core.col(pre + "ln1_w", k), bias=core.col(pre + "ln1_b", k))
                done.then_inc(read["xa"], 1)

            def tanh_low(a):
                act.wait_ge(ready["low"], a + 1)
                act.activation(low[:, :], bank[3][:, 0:PT], ACT.Tanh)
                act.activation(low_g[:, :], bank[3][0:R, PT:2 * PT], ACT.Tanh).then_inc(read["low"], 1)

            def copy_g(a):
                act.wait_ge(ready["g"], a + 1)
                wait(act, read["g"], a)
                act.activation(g_tanh[:, :, :], halves(bank[4]), ACT.Tanh, scale=0.5).then_inc(g_tanh_ok, 1)

            def tanh_td(a):
                act.wait_ge(ready["td"], a + 1)
                act.activation(td_low[:, :], bank[3][0:RD, 0:PT], ACT.Tanh).then_inc(read["td"], 1)

            def make_rate(a, par):
                act.wait_ge(ready["rate"], a + 1)
                for t in range(KC):
                    done = act.activation(rate[:, par, t, :], bank[5][:, t * PT:(t + 1) * PT], ACT.Exp, bias=core.col(pre + "time_decay", t))
                done.then_inc(read["rate"], 1)
                make_decay(a, par, 0)

            def copy_r(a, par):
                act.wait_ge(ready["r"], a + 1)
                act.activation(rT[:, par, :, :], halves(bank[4]), ACT.Copy).then_inc(read["r"], 1)
                make_decay(a, par, 1)

            def make_decay(p, par, s):
                k, b = s // PAIR, s % PAIR
                if not (static(p) and p == 0 and s < 2):
                    act.wait_ge(scan_ok, p * UNITS + (s - 1))
                if s == 0:
                    act.wait_ge(read["rate"], p + 1)
                act.activation(decay[:, s % 2, :, 1:P + 1], rate[:, par, k, b * P:(b + 1) * P][:, None, :].to_broadcast([P, J, P]),
                               ACT.Exp, scale=-1.0).then_inc(decay_ok, 1)

            def slot(p, par):
                u, a, c = exists(p), exists(p + 1), exists(p - 1)
                if c:
                    act.wait_ge(ready["z"], p)
                    act.activation(zT[:, :, :], halves(bank[6]), ACT.Copy, scale=0.5).then_inc(read["z"], 1)
                if a:
                    copy_xa(p + 1)
                if u:
                    make_decay(p, par, 2)
                    copy_g(p)
                if c:
                    act.wait_ge(mv2_ok, p * PAIR)
                    act.activation(std2[:, :], core.mv_new[:, :, 1], ACT.Sqrt, bias=core.eps[:, 0:1]).then_inc(std2_ok, 1)
                if a:
                    tanh_low(p + 1)
                if u:
                    make_decay(p, par, 3)
                if c:
                    act.wait_ge(ready["xc"], p)
                    for k in range(KC):
                        done = act.activation(xc[:, k, :, 1:P + 1], halves(bank[6])[:, k, :].rearrange("p (b t) -> p b t", b=PAIR), ACT.Identity,
                                              scale=core.col(pre + "ln2_w", k), bias=core.col(pre + "ln2_b", k))
                    done.then_inc(read["xc"], 1)
                if a:
                    tanh_td(p + 1)
                if u:
                    act.wait_ge(vsum_ok, p + 1)
                    act.activation(gstd[:, :], vsum[:, :], ACT.Sqrt, scale=1.0 / J, bias=core.eps[:, 0:1]).then_inc(gstd_ok, 1)
                if a:
                    make_rate(p + 1, 1 - par)
                if c:
                    act.wait_ge(ready["kk"], p)
                    act.activation(relu[:, :, :], halves(bank[7]), ACT.Relu).then_inc(relu_ok, 1)
                    act.wait_ge(relu_ok, p)
                    act.activation(kkT[:, :, :], relu[:, :, :], ACT.Square).then_inc(read["kk"], 1)
                if a:
                    copy_r(p + 1, 1 - par)
                if c:
                    act.wait_ge(ready["rr"], p)
                    act.activation(r_tanh[:, :, :], halves(bank[6]), ACT.Tanh, scale=0.5).then_inc(read["rr"], 1)

            rstd_scalar(core, act, root)
            copy_xa(0)
            tanh_low(0)
            tanh_td(0)
            act.wait_ge(made, 6)
            make_rate(0, 0)
            copy_r(0, 0)
            over_slots(act, slot)

        @block.vector
        def _(dve):
            def normalise(a):
                wait(dve, ready["xa"], a)
                for b in range(PAIR):
                    i = a * PAIR + b
                    dve.tensor_scalar(xn[:, b, :], core.x[:, i, :], core.mv[:, i, 0:1], core.rstd[:, bass.ds(i, 1)],
                                      ALU.subtract, ALU.mult).then_inc(xn_ok, 1)
                wait(dve, mix_ok, a * F)
                dve.tensor_scalar(xa[:, :, :, 0:1], ctx_rows[:, :, bass.ds(a * PAIR, PAIR), 1:2], 1.0, None, ALU.mult).then_inc(first_ok, 1)

            def shift_a(a):
                dve.wait_ge(first_ok, a * 2 + 1)
                dve.wait_ge(read["xa"], a + 1)
                dve.tensor_tensor(sx[:, :, :, :].rearrange("p k b t -> p (k b) t"), xa[:, :, :, 0:P].rearrange("p k b t -> p (k b) t"),
                                  xa[:, :, :, 1:P + 1].rearrange("p k b t -> p (k b) t"), ALU.subtract).then_inc(first_ok, 1)
                dve.wait_ge(first_ok, a * 2 + 2)
                for k in range(KC):
                    dve.scalar_tensor_tensor(xmaa[:, k, :, :], sx[:, k, :, :], core.col(pre + "maa_x", k), xa[:, k, :, 1:P + 1],
                                             ALU.mult, ALU.add).then_inc(xmaa_ok, 1)

            def mix(a):
                for f in range(F):
                    dve.wait_ge(f_ready, a * F + (f + 1))
                    for k in range(KC):
                        done = dve.scalar_tensor_tensor(mixed[:, f, k, :], MIX[f][:, k * PT:(k + 1) * PT],
                                                        core.col(pre + "maa_stack", f * KC + k), flat(sx[:, :, :, :])[:, k, :], ALU.add, ALU.mult)
                    done.then_inc(f_read, 1)

            def copy_k(a, par):
                dve.wait_ge(ready["k"], a + 1)
                dve.tensor_copy(kT[:, par, :, :], halves(bank[5])).then_inc(read["k"], 1)

            def copy_v(a, par):
                dve.wait_ge(ready["v"], a + 1)
                dve.tensor_copy(vT[:, par, :, :], halves(bank[3])).then_inc(read["v"], 1)

            def make_gate(a, par):
                dve.wait_ge(g_tanh_ok, a + 1)
                dve.scalar_tensor_tensor(gate[:, par, :, :], g_tanh[:, :, :], 1.0, halves(bank[4]), ALU.add, ALU.mult).then_inc(read["g"], 1)

            def scan(p, par, s):
                k, b = s // PAIR, s % PAIR
                n = p * UNITS + s
                wait(dve, q_ok, n)
                dve.wait_ge(vb_ready, n + 1)
                dve.tensor_tensor(kv[:, :, 1:P + 1], VB, kT[:, par, k, b * P:(b + 1) * P][:, None, :].to_broadcast([P, J, P]), ALU.mult).then_inc(kv_ok, 1)
                dve.tensor_scalar(kv[:, :, 0:1], state0[:, k, bass.ds(p * PAIR + b, 1), :].rearrange("p b j -> p j b"), 1.0, None, ALU.mult).then_inc(kv_ok, 1)
                dve.wait_ge(kv_ok, n * 2 + 2)
                dve.wait_ge(decay_ok, n + 1)
                dve.tensor_tensor_scan(states[:, :, :].rearrange("p j t -> p (j t)"), decay[:, s % 2, :, :].rearrange("p j t -> p (j t)"),
                                       kv[:, :, :].rearrange("p j t -> p (j t)"), 0.0, ALU.mult, ALU.add).then_inc(scan_ok, 1)
                dve.wait_ge(scan_ok, n + 1)
                if not (static(p) and p == 0 and s < 2):
                    dve.wait_ge(sum_ready, p * UNITS + (s - 1))
                dve.scalar_tensor_tensor(prod[:, s % 2, :, :], kv[:, :, 1:P + 1], core.col(pre + "u", k), states[:, :, 0:P],
                                         ALU.mult, ALU.add).then_inc(q_ok, 1)

            def group_moments(c):
                dve.wait_ge(sum_ready, c * UNITS + UNITS)
                wait(dve, ready["z"], c)
                dve.tensor_copy(og[:, :, :, :], OG[:, :].rearrange("p (n j h) -> p n h j", j=J, h=HT)).then_inc(og_read, 1)
                heads = og[:, :, :, :].rearrange("p n h j -> p (n h) j")
                squares = sq[:, :, :, :].rearrange("p n h j -> p (n h) j")
                over_j = lambda t: t[:, :, None].to_broadcast([P, UNITS * HT, J])
                s0 = c * 5
                dve.wait_ge(og_read, c + 1)
                dve.tensor_reduce(msum[:, :], heads, AX_X, ALU.add).then_inc(gn_step, 1)
                dve.wait_ge(gn_step, s0 + 1)
                dve.tensor_scalar(mean[:, :], msum[:, :], 1.0 / J, None, ALU.mult).then_inc(gn_step, 1)
                dve.wait_ge(gn_step, s0 + 2)
                dve.tensor_tensor(heads, heads, over_j(mean), ALU.subtract).then_inc(gn_step, 1)
                dve.wait_ge(gn_step, s0 + 3)
                dve.tensor_tensor(squares, heads, heads, ALU.mult).then_inc(gn_step, 1)
                dve.wait_ge(gn_step, s0 + 4)
                dve.tensor_reduce(vsum[:, :], squares, AX_X, ALU.add).then_inc(vsum_ok, 1)

            def group_norm(c):
                heads = og[:, :, :, :].rearrange("p n h j -> p (n h) j")
                over_j = lambda t: t[:, :, None].to_broadcast([P, UNITS * HT, J])
                s0 = c * 5
                dve.wait_ge(gstd_ok, c + 1)
                dve.reciprocal(grstd[:, :], gstd[:, :]).then_inc(gn_step, 1)
                dve.wait_ge(gn_step, s0 + 5)
                dve.tensor_tensor(heads, heads, over_j(grstd), ALU.mult).then_inc(gn_ok, 1)

            def residual(c):
                dve.wait_ge(ready["out"], c + 1)
                wait(dve, result_ok, c)
                dve.tensor_tensor(core.x_new[:, :, :], core.x[:, bass.ds(c * PAIR, PAIR), :], halves(bank[7]), ALU.add).then_inc(read["out"], 1)
                dve.wait_ge(read["out"], c + 1)
                for b in range(PAIR):
                    dve.bn_stats(core.stats[:, b, :], core.x_new[:, b, :]).then_inc(st_ok, 1)
                wait(dve, std2_ok, c)
                dve.wait_ge(st_ok, c * PAIR + PAIR)
                dve.tensor_scalar(xc[:, :, :, 0:1], ctx_rows[:, :, bass.ds(c * PAIR, PAIR), 0:1], 1.0, None, ALU.mult).then_inc(c_first, 1)
                for b in range(PAIR):
                    dve.bn_aggr(core.mv_new[:, b, :], core.stats[:, b, :]).then_inc(mv2_ok, 1)

            def normalise2(c):
                dve.wait_ge(std2_ok, c + 1)
                dve.wait_ge(mv2_ok, c * PAIR + PAIR)
                dve.reciprocal(rstd2[:, :], std2[:, :]).then_inc(c_step, 1)
                dve.wait_ge(c_step, c + 1)
                for b in range(PAIR):
                    dve.tensor_scalar(xn2[:, b, :], core.x_new[:, b, :], core.mv_new[:, b, 0:1], rstd2[:, b:b + 1],
                                      ALU.subtract, ALU.mult).then_inc(xn2_ok, 1)

            def shift_c(c):
                dve.wait_ge(read["xc"], c + 1)
                dve.wait_ge(c_first, c + 1)
                dve.tensor_tensor(sx2[:, :, :, :].rearrange("p k b t -> p (k b) t"), xc[:, :, :, 0:P].rearrange("p k b t -> p (k b) t"),
                                  xc[:, :, :, 1:P + 1].rearrange("p k b t -> p (k b) t"), ALU.subtract).then_inc(xk_step, 1)
                dve.wait_ge(xk_step, c + 1)
                for to, n in ((xk2, "ffn_maa_k"), (xr2, "ffn_maa_r")):
                    for k in range(KC):
                        dve.scalar_tensor_tensor(to[:, k, :].rearrange("p (b t) -> p b t", b=PAIR), sx2[:, k, :, :], core.col(pre + n, k),
                                                 xc[:, k, :, 1:P + 1], ALU.mult, ALU.add).then_inc(xk_ok, 1)

            def finish(c):
                dve.wait_ge(read["rr"], c + 1)
                dve.wait_ge(ready["ff"], c + 1)
                dve.scalar_tensor_tensor(gated[:, :, :], r_tanh[:, :, :], 1.0, halves(bank[7]), ALU.add, ALU.mult).then_inc(read["ff"], 1)
                wait(dve, stored, c * DMA)
                dve.wait_ge(read["ff"], c + 1)
                dve.scalar_tensor_tensor(result[:, :, :], gated[:, :, :], 0.5, core.x_new[:, :, :], ALU.mult, ALU.add).then_inc(result_ok, 1)

            def slot(p, par):
                u, a, c = exists(p), exists(p + 1), exists(p - 1)
                if a:
                    normalise(p + 1)
                if u:
                    scan(p, par, 1)
                if c:
                    residual(p - 1)
                if u:
                    make_gate(p, par)
                if a:
                    shift_a(p + 1)
                if c:
                    normalise2(p - 1)
                if u:
                    scan(p, par, 2)
                if a:
                    mix(p + 1)
                if u:
                    scan(p, par, 3)
                if c:
                    shift_c(p - 1)
                if a:
                    copy_k(p + 1, 1 - par)
                if u:
                    group_moments(p)
                if a:
                    copy_v(p + 1, 1 - par)
                if u:
                    group_norm(p)
                if a:
                    scan(p + 1, 1 - par, 0)
                if c:
                    finish(p - 1)

            rstd_vector(core, dve, root, rstep)
            normalise(0)
            shift_a(0)
            mix(0)
            copy_k(0, 0)
            copy_v(0, 0)
            core.wait_loaded(dve, stage, "state0")
            scan(0, 0, 0)
            over_slots(dve, slot)


def store_stage(core):
    nc = core.nc
    with ExitStack() as ctx:
        stored = ctx.enter_context(nc.semaphore("stored"))
        block = ctx.enter_context(nc.Block())

        @block.sync
        def _(sp):
            sp.dma_start(core.out.rearrange("b t d -> t b d"), core.x[:, :, :]).then_inc(stored, DMA)
            sp.wait_ge(stored, DMA)


def build_program(nc, dram, out):
    with ExitStack() as ctx:
        core = Core(nc, ctx, dram, out)
        load_stage(core)
        for stage in STAGES:
            if stage == "l0_self":
                narrow_attention(core, stage, "self")
            elif stage == "l0_cross":
                narrow_attention(core, stage, "cross")
            elif stage == "l0_mlp":
                mlp(core, stage, "L0_xattn_ln3_s", "L0_xattn_ln3_b", "L0_xattn_b1", ACT.Gelu_apprx_tanh)
            elif stage == "l1_first":
                wide_attention(core, stage, 1)
            elif stage == "l1_second":
                wide_attention(core, stage, 2)
            elif stage == "l1_mlp":
                mlp(core, stage, "L1_xattn_ln_mlp_scale", "L1_xattn_ln_mlp_offset", "L1_xattn_b_fc1", ACT.Gelu)
            elif stage == "l2":
                single_attention(core, stage)
            elif stage == "l3":
                recurrence(core, stage)
        if STAGES[-1] != "l3":
            store_stage(core)


PLAIN = ["L0_xattn_w_qkv", "L0_xattn_w_ao", "L0_xattn_w_q", "L0_xattn_w_kv", "L0_xattn_w_co", "L0_xattn_w1", "L0_xattn_w2",
         "L1_xattn_wq1", "L1_xattn_wk1", "L1_xattn_wv1", "L1_xattn_wo1", "L1_xattn_wq2", "L1_xattn_wk2", "L1_xattn_wv2",
         "L1_xattn_wo2", "L1_xattn_w_fc1", "L1_xattn_w_fc2", "L3_xattn_maa_w1", "L3_xattn_td_w1", "L3_xattn_td_w2"]
TRANSPOSED = ["L2_xattn_w_q", "L2_xattn_w_k", "L2_xattn_w_v", "L2_xattn_w_o", "L3_xattn_Wr", "L3_xattn_Wk", "L3_xattn_Wv",
              "L3_xattn_Wg", "L3_xattn_Wo", "L3_xattn_Wfk", "L3_xattn_Wfr", "L3_xattn_Wfv"]


def kernel(**inputs):
    import concourse.bacc as bacc
    from concourse.bass_utils import run_bass_kernel_spmd

    a = {k: np.asarray(v) for k, v in inputs.items()}
    arrays = {
        "x": a["x"],
        "ctx_t": np.ascontiguousarray(a["ctx_2048"].reshape(TOK, D).T),
        "state0": np.ascontiguousarray(a["ctx_2048"][:, 2:10, :].reshape(NB, KC, P, 8).transpose(2, 1, 0, 3)).reshape(P, D),
        "mask_self": a["mask_1x1xSxS2_fc1"].reshape(P, P),
        "mask_cross": np.ascontiguousarray(a["mask_Bx1xSxS2_ff1"].reshape(NB, P, P)),
        "columns": np.ascontiguousarray(np.concatenate([a[n].reshape(-1, P) for n, _ in COLUMNS]).T),
        "maa_w2": np.ascontiguousarray(a["L3_xattn_maa_w2"].reshape(5 * 32, D)[:P]),
        "maa_w2g": np.ascontiguousarray(a["L3_xattn_maa_w2"].reshape(5 * 32, D)[P:]),
        "alpha": np.ascontiguousarray(np.broadcast_to(a["L2_xattn_alpha"].reshape(1, 1), (P, 1))),
    }
    for n, of in ROWS.items():
        arrays["row_" + n] = np.ascontiguousarray(np.broadcast_to(a[of], (P, D)))
    for n in PLAIN:
        arrays[n] = a[n]
    for n in TRANSPOSED:
        arrays[n] = np.ascontiguousarray(a[n].T)
    nc = bacc.Bacc("TRN2", target_bir_lowering=False, num_devices=1)
    dram = {n: nc.dram_tensor("in_" + n, v.shape, mybir.dt.from_np(v.dtype), kind="ExternalInput").ap()
            for n, v in arrays.items()}
    out = nc.dram_tensor("out", (NB, P, D), F32, kind="ExternalOutput").ap()
    build_program(nc, dram, out)
    r = run_bass_kernel_spmd(nc, [{"in_" + n: v for n, v in arrays.items()}], core_ids=[0])
    return r.results[0]["out"]
```
